# Optimizing a Trainium2 kernel written in Bass

```python
import numpy as np
import jax
import jax.numpy as jnp

def _softmax(x, axis=-1):
    return jax.nn.softmax(x, axis=axis)

def _gelu(x):
    return jax.nn.gelu(x, approximate=True)

def _silu(x):
    return jax.nn.silu(x)

def _sigmoid(x):
    return jax.nn.sigmoid(x)

def _layernorm(x, axis=-1, eps=1e-05):
    m = jnp.mean(x, axis=axis, keepdims=True)
    v = jnp.var(x, axis=axis, keepdims=True)
    return (x - m) / jnp.sqrt(v + eps)

def _scatter_add(tgt, idx, src, axis=0):
    return tgt.at[idx].add(src)

def _segment_sum(src, seg, n):
    return jax.ops.segment_sum(src, seg, n)
kernel_name = 'mk_decoder_postln_d2_seqx_r8_73c823'

def setup_inputs(seed: int=0):
    np.random.seed(seed)
    _w = jnp.asarray

    def _rec_inputs():
        import jax
        import jax.numpy as jnp
        _rk = jax.random.key(seed)
        x = -0.0002928 + 1 * jax.random.normal(jax.random.fold_in(_rk, 1), (32, 128, 128), jnp.float32)
        _lenS = 128 - jax.random.randint(jax.random.fold_in(_rk, 7), (32,), 0, max(1, 128 // 4) + 1, jnp.int32)
        _lenS2 = 77 - jax.random.randint(jax.random.fold_in(_rk, 8), (32,), 0, max(1, 77 // 4) + 1, jnp.int32)
        _ctx_1024P = jax.random.normal(jax.random.fold_in(_rk, 11), (32, 16, 128), jnp.float32)
        _ctx_1024c = jax.random.dirichlet(jax.random.fold_in(_rk, 511), 0.3 * jnp.ones((16,), jnp.float32), (32, 77))
        _ctx_1024t = jnp.einsum('bsk,bkd->bsd', _ctx_1024c, _ctx_1024P)
        _ctx_1024t = _ctx_1024t * jax.lax.rsqrt(jnp.mean(jnp.square(_ctx_1024t)) + 1e-12) * 0.953939
        ctx_1024 = -1.39393e-06 + 0.999914 * (_ctx_1024t + 0.3 * jax.random.normal(jax.random.fold_in(_rk, 611), (32, 77, 128), jnp.float32))
        _validS = jnp.arange(128)[None, :] < _lenS[:, None]
        _validS2 = jnp.arange(77)[None, :] < _lenS2[:, None]
        _causal = jnp.tril(jnp.ones((128, 128), dtype=bool))
        mask_BxS2_if0 = jnp.where(jnp.ones((32, 77), dtype=bool), 0, 1).astype(jnp.int32)
        return (x, ctx_1024, mask_BxS2_if0)
    x, ctx_1024, mask_BxS2_if0 = _rec_inputs()

    def _L0_attn_setup():
        import jax, jax.numpy as jnp
        import numpy as np
        import math
        B, T, C = (2, 256, 128)
        H = 16
        D = C // H

        def alibi_slopes(n_heads):
            start = 2.0 ** (-2.0 ** (-(math.log2(n_heads) - 3)))
            return jnp.asarray([start * start ** i for i in range(n_heads)], dtype=jnp.float32)
        key = jax.random.key(seed)
        ks = jax.random.split(key, 6)
        x = jax.random.normal(ks[0], (B, T, C), dtype=jnp.float32)
        W_attn = jax.random.normal(ks[1], (C, 3 * C), dtype=jnp.float32) * 0.02
        b_attn = jnp.zeros((3 * C,), dtype=jnp.float32)
        W_proj = jax.random.normal(ks[2], (C, C), dtype=jnp.float32) * 0.02
        b_proj = jnp.zeros((C,), dtype=jnp.float32)
        temperature = jnp.ones((1,), dtype=jnp.float32) * 2.0
        return {'x': x, 'W_attn': W_attn, 'b_attn': b_attn, 'W_proj': W_proj, 'b_proj': b_proj, 'temperature': temperature}
    _L0_attn_all = _L0_attn_setup()
    _L0_attn_in = {k: v for k, v in _L0_attn_all.items() if k in ('W_attn', 'b_attn', 'W_proj', 'b_proj', 'temperature')}
    del _L0_attn_all

    def _L0_xattn_setup():
        import jax, jax.numpy as jnp
        import numpy as np
        B, NQ, NK = (2, 256, 256)
        DIM_Q = DIM_KV = DIM_E = DIM_O = 128
        H = 16
        HD = DIM_E // H
        SCALE = HD ** (-0.5)
        key = jax.random.key(seed)
        ks = jax.random.split(key, 8)
        inp = {'query': jax.random.normal(ks[0], (B, NQ, DIM_Q), dtype=jnp.float32), 'key': jax.random.normal(ks[1], (B, NK, DIM_KV), dtype=jnp.float32), 'value': jax.random.normal(ks[2], (B, NK, DIM_KV), dtype=jnp.float32), 'Wq': jax.random.normal(ks[3], (DIM_Q, DIM_E), dtype=jnp.float32) * DIM_Q ** (-0.5), 'Wk': jax.random.normal(ks[4], (DIM_KV, DIM_E), dtype=jnp.float32) * DIM_KV ** (-0.5), 'Wv': jax.random.normal(ks[5], (DIM_KV, DIM_E), dtype=jnp.float32) * DIM_KV ** (-0.5), 'Wo': jax.random.normal(ks[6], (DIM_E, DIM_O), dtype=jnp.float32) * DIM_E ** (-0.5), 'bo': jax.random.normal(ks[7], (DIM_O,), dtype=jnp.float32) * 0.01}
        return inp
    _L0_xattn_all = _L0_xattn_setup()
    _L0_xattn_in = {k: v for k, v in _L0_xattn_all.items() if k in ('Wq', 'Wk', 'Wv', 'Wo', 'bo')}
    del _L0_xattn_all

    def _L0_ffn_setup():
        import jax, jax.numpy as jnp
        import numpy as np
        E = 8
        K = 2
        D = 128
        key = jax.random.key(seed)
        k0, k1, k2, k3 = jax.random.split(key, 4)
        x = jax.random.normal(k0, (2, 256, D), dtype=jnp.float32)
        gate_w = jax.random.normal(k1, (D, E), dtype=jnp.float32) * 0.02
        fc_w = jax.random.normal(k2, (E, D, 4 * D), dtype=jnp.float32) * 0.02
        proj_w = jax.random.normal(k3, (E, 4 * D, D), dtype=jnp.float32) * 0.02
        return {'x': x, 'gate_w': gate_w, 'fc_w': fc_w, 'proj_w': proj_w}
    _L0_ffn_all = _L0_ffn_setup()
    _L0_ffn_in = {k: v for k, v in _L0_ffn_all.items() if k in ('gate_w', 'fc_w', 'proj_w')}
    del _L0_ffn_all

    def _L1_attn_setup():
        import jax, jax.numpy as jnp
        import numpy as np
        DIM = 128
        HEADS = 16
        HEAD_DIM = DIM // HEADS
        key = jax.random.key(seed)
        k1, k2, k3, k4 = jax.random.split(key, 4)
        x = jax.random.normal(k1, (4, 512, DIM), dtype=jnp.float32)
        w_qkv = jax.random.normal(k2, (3 * DIM, DIM), dtype=jnp.float32) * DIM ** (-0.5)
        w_proj = jax.random.normal(k3, (DIM, DIM), dtype=jnp.float32) * DIM ** (-0.5)
        b_proj = jax.random.normal(k4, (DIM,), dtype=jnp.float32) * 0.01
        return {'x': x, 'w_qkv': w_qkv, 'w_proj': w_proj, 'b_proj': b_proj}
    _L1_attn_all = _L1_attn_setup()
    _L1_attn_in = {k: v for k, v in _L1_attn_all.items() if k in ('w_qkv', 'w_proj', 'b_proj')}
    del _L1_attn_all

    def _L1_xattn_setup():
        import jax, jax.numpy as jnp
        import numpy as np
        import math
        B, M, D, H, NK = (4, 256, 128, 16, 5)
        HD = D // H

        def _gather_pad0(x, idx):
            Bx, Hx, W, hd = x.shape
            valid = (idx >= 0) & (idx < W)
            idxc = jnp.clip(idx, 0, W - 1).reshape(Bx, Hx, -1)
            g = jnp.take_along_axis(x, idxc[..., None], axis=2)
            g = g.reshape(idx.shape + (hd,))
            return g * valid[..., None].astype(x.dtype)
        key = jax.random.key(seed)
        ks = jax.random.split(key, 9)
        w = lambda k, shape: jax.random.normal(k, shape, jnp.float32) * 0.02
        return {'k': jax.random.normal(ks[0], (B, M, D), jnp.float32), 'v': jax.random.normal(ks[1], (B, M, D), jnp.float32), 'q': jax.random.normal(ks[2], (B, M, D), jnp.float32), 'mask': jnp.zeros((B, M), jnp.int32), 'Wk': w(ks[3], (D, D)), 'bk': jnp.zeros((D,), jnp.float32), 'Wv': w(ks[4], (D, D)), 'bv': jnp.zeros((D,), jnp.float32), 'Wq': w(ks[5], (D, D)), 'bq': jnp.zeros((D,), jnp.float32), 'Woff': w(ks[6], (H * NK, D)), 'boff': jnp.zeros((H * NK,), jnp.float32), 'Wo': w(ks[7], (D, D)), 'bo': jnp.zeros((D,), jnp.float32)}
    _L1_xattn_all = _L1_xattn_setup()
    _L1_xattn_in = {k: v for k, v in _L1_xattn_all.items() if k in ('Wk', 'bk', 'Wv', 'bv', 'Wq', 'bq', 'Woff', 'boff', 'Wo', 'bo')}
    del _L1_xattn_all

    def _L1_ffn_setup():
        import jax, jax.numpy as jnp
        import numpy as np
        import math
        BETA = 0.9
        THRESHOLD = 1.0
        NUM_STEPS = 5
        ALPHA = 2.0

        @jax.custom_vjp
        def spike_fn(u):
            return (u > 0).astype(u.dtype)

        def _spike_fwd(u):
            return (spike_fn(u), u)

        def _spike_bwd(u, g):
            s = jnp.pi / 2.0 * ALPHA * u
            return (g * (ALPHA / 2.0) / (1.0 + s * s),)
        spike_fn.defvjp(_spike_fwd, _spike_bwd)
        key = jax.random.key(seed)
        k1, k2, k3 = jax.random.split(key, 3)
        n_embd = 128
        x = jax.random.normal(k1, (4, 256, n_embd), dtype=jnp.float32)
        W_fc = jax.random.normal(k2, (4 * n_embd, n_embd), dtype=jnp.float32) / math.sqrt(n_embd)
        W_proj = jax.random.normal(k3, (n_embd, 4 * n_embd), dtype=jnp.float32) / math.sqrt(4 * n_embd)
        return {'x': x, 'W_fc': W_fc, 'W_proj': W_proj}
    _L1_ffn_all = _L1_ffn_setup()
    _L1_ffn_in = {k: v for k, v in _L1_ffn_all.items() if k in ('W_fc', 'W_proj')}
    del _L1_ffn_all
    return {'x': x, 'ctx_1024': ctx_1024, 'mask_BxS2_if0': mask_BxS2_if0, 'L0_attn_W_attn': _L0_attn_in['W_attn'], 'L0_attn_b_attn': _L0_attn_in['b_attn'], 'L0_attn_W_proj': _L0_attn_in['W_proj'], 'L0_attn_b_proj': _L0_attn_in['b_proj'], 'L0_attn_temperature': _L0_attn_in['temperature'], 'L0_xattn_Wq': _L0_xattn_in['Wq'], 'L0_xattn_Wk': _L0_xattn_in['Wk'], 'L0_xattn_Wv': _L0_xattn_in['Wv'], 'L0_xattn_Wo': _L0_xattn_in['Wo'], 'L0_xattn_bo': _L0_xattn_in['bo'], 'L0_ffn_gate_w': _L0_ffn_in['gate_w'], 'L0_ffn_fc_w': _L0_ffn_in['fc_w'], 'L0_ffn_proj_w': _L0_ffn_in['proj_w'], 'L1_attn_w_qkv': _L1_attn_in['w_qkv'], 'L1_attn_w_proj': _L1_attn_in['w_proj'], 'L1_attn_b_proj': _L1_attn_in['b_proj'], 'L1_xattn_Wk': _L1_xattn_in['Wk'], 'L1_xattn_bk': _L1_xattn_in['bk'], 'L1_xattn_Wv': _L1_xattn_in['Wv'], 'L1_xattn_bv': _L1_xattn_in['bv'], 'L1_xattn_Wq': _L1_xattn_in['Wq'], 'L1_xattn_bq': _L1_xattn_in['bq'], 'L1_xattn_Woff': _L1_xattn_in['Woff'], 'L1_xattn_boff': _L1_xattn_in['boff'], 'L1_xattn_Wo': _L1_xattn_in['Wo'], 'L1_xattn_bo': _L1_xattn_in['bo'], 'L1_ffn_W_fc': _L1_ffn_in['W_fc'], 'L1_ffn_W_proj': _L1_ffn_in['W_proj']}

def reference(x, ctx_1024, mask_BxS2_if0, L0_attn_W_attn, L0_attn_b_attn, L0_attn_W_proj, L0_attn_b_proj, L0_attn_temperature, L0_xattn_Wq, L0_xattn_Wk, L0_xattn_Wv, L0_xattn_Wo, L0_xattn_bo, L0_ffn_gate_w, L0_ffn_fc_w, L0_ffn_proj_w, L1_attn_w_qkv, L1_attn_w_proj, L1_attn_b_proj, L1_xattn_Wk, L1_xattn_bk, L1_xattn_Wv, L1_xattn_bv, L1_xattn_Wq, L1_xattn_bq, L1_xattn_Woff, L1_xattn_boff, L1_xattn_Wo, L1_xattn_bo, L1_ffn_W_fc, L1_ffn_W_proj):
    import jax
    import jax.numpy as jnp

    def _L0_attn_ref(x, W_attn, b_attn, W_proj, b_proj, temperature):
        import jax, jax.numpy as jnp
        import numpy as np
        import math
        B, T, C = (2, 256, 128)
        H = 16
        D = C // H

        def alibi_slopes(n_heads):
            start = 2.0 ** (-2.0 ** (-(math.log2(n_heads) - 3)))
            return jnp.asarray([start * start ** i for i in range(n_heads)], dtype=jnp.float32)
        Bc, Tc, Cc = x.shape
        qkv = x @ W_attn + b_attn
        q, k, v = jnp.split(qkv, 3, axis=-1)
        q = q.reshape(Bc, Tc, H, D)
        k = k.reshape(Bc, Tc, H, D)
        v = v.reshape(Bc, Tc, H, D)
        scale = 1.0 / math.sqrt(D)
        att = jnp.einsum('bqhd,bkhd->bhqk', q, k) * scale
        att = att / temperature
        pos = jnp.arange(Tc, dtype=jnp.float32)
        rel = pos[None, :] - pos[:, None]
        slopes = alibi_slopes(H)
        bias = slopes[:, None, None] * rel[None, :, :]
        causal = pos[None, :] <= pos[:, None]
        bias = jnp.where(causal[None, :, :], bias, -jnp.inf)
        att = att + bias[None, :, :, :]
        w = jax.nn.softmax(att, axis=-1)
        y = jnp.einsum('bhqk,bkhd->bqhd', w, v).reshape(Bc, Tc, Cc)
        return y @ W_proj + b_proj

    def _L0_xattn_ref(query, key, value, Wq, Wk, Wv, Wo, bo):
        import jax, jax.numpy as jnp
        import numpy as np
        B, NQ, NK = (2, 256, 256)
        DIM_Q = DIM_KV = DIM_E = DIM_O = 128
        H = 16
        HD = DIM_E // H
        SCALE = HD ** (-0.5)
        b, nq, _ = query.shape
        nk = key.shape[1]
        q = (query @ Wq).reshape(b, nq, H, HD).transpose(0, 2, 1, 3)
        k = (key @ Wk).reshape(b, nk, H, HD).transpose(0, 2, 1, 3)
        v = (value @ Wv).reshape(b, nk, H, HD).transpose(0, 2, 1, 3)
        attn = jnp.einsum('bhqd,bhkd->bhqk', q, k) * SCALE
        attn = jax.nn.softmax(attn, axis=-1)
        x = jnp.einsum('bhqk,bhkd->bhqd', attn, v)
        x = x.transpose(0, 2, 1, 3).reshape(b, nq, H * HD)
        return x @ Wo + bo

    def _L0_ffn_ref(x, gate_w, fc_w, proj_w):
        import jax, jax.numpy as jnp
        import numpy as np
        E = 8
        K = 2
        D = 128
        orig_shape = x.shape
        d = orig_shape[-1]
        xt = x.reshape(-1, d)
        gates = jax.nn.softmax(xt @ gate_w, axis=-1)
        top_v, top_i = jax.lax.top_k(gates, K)
        top_v = top_v / jnp.sum(top_v, axis=-1, keepdims=True)
        h = jnp.einsum('nd,edf->enf', xt, fc_w)
        h = jax.nn.gelu(h, approximate=False)
        eo = jnp.einsum('enf,efd->end', h, proj_w)
        eo_nt = jnp.swapaxes(eo, 0, 1)
        sel = jnp.take_along_axis(eo_nt, top_i[:, :, None], axis=1)
        out = jnp.sum(sel * top_v[:, :, None], axis=1)
        return out.reshape(orig_shape)

    def _L1_attn_ref(x, w_qkv, w_proj, b_proj):
        import jax, jax.numpy as jnp
        import numpy as np
        DIM = 128
        HEADS = 16
        HEAD_DIM = DIM // HEADS
        B, N, C = x.shape
        H, D = (HEADS, HEAD_DIM)
        qkv = x @ w_qkv.T
        qkv = qkv.reshape(B, N, 3, H, D).transpose(2, 0, 3, 1, 4)
        q, k, v = (qkv[0], qkv[1], qkv[2])
        q = jax.nn.elu(q) + 1.0
        k = jax.nn.elu(k) + 1.0
        kv = jnp.einsum('bhnd,bhne->bhde', k, v)
        num = jnp.einsum('bhnd,bhde->bhne', q, kv)
        k_sum = k.sum(axis=-2)
        qk = jnp.einsum('bhnd,bhd->bhn', q, k_sum)[..., None]
        out = num / (qk + 1e-08)
        out = out.transpose(0, 2, 1, 3).reshape(B, N, C)
        return out @ w_proj.T + b_proj

    def _L1_xattn_ref(k, v, q, mask, Wk, bk, Wv, bv, Wq, bq, Woff, boff, Wo, bo):
        import jax, jax.numpy as jnp
        import numpy as np
        import math
        B, M, D, H, NK = (4, 256, 128, 16, 5)
        HD = D // H

        def _gather_pad0(x, idx):
            Bx, Hx, W, hd = x.shape
            valid = (idx >= 0) & (idx < W)
            idxc = jnp.clip(idx, 0, W - 1).reshape(Bx, Hx, -1)
            g = jnp.take_along_axis(x, idxc[..., None], axis=2)
            g = g.reshape(idx.shape + (hd,))
            return g * valid[..., None].astype(x.dtype)
        Bq, Q, _ = q.shape
        key_len = k.shape[1]
        K = jnp.einsum('bmd,ed->bme', k, Wk) + bk
        V = jnp.einsum('bmd,ed->bme', v, Wv) + bv
        Qp = jnp.einsum('bqd,ed->bqe', q, Wq) + bq
        off = jnp.einsum('bqd,ed->bqe', Qp, Woff) + boff
        off = off.reshape(Bq, Q, H, NK).transpose(0, 2, 1, 3)
        Kh = K.reshape(Bq, key_len, H, HD).transpose(0, 2, 1, 3)
        Vh = V.reshape(Bq, key_len, H, HD).transpose(0, 2, 1, 3)
        Qh = Qp.reshape(Bq, Q, H, HD).transpose(0, 2, 1, 3)
        loc = jnp.arange(Q, dtype=jnp.float32)[:, None]
        left = -NK // 2
        ref = jnp.arange(left, NK + left, dtype=jnp.float32)
        sign_lens = (1 - mask).sum(-1).astype(jnp.float32) - 1.0
        loc_x = jnp.mod(ref + off + loc, sign_lens[:, None, None, None])
        xg = loc_x / (key_len - 1) * 2.0 - 1.0
        ix = ((xg + 1.0) * key_len - 1.0) / 2.0
        x0 = jnp.floor(ix)
        dx = ix - x0
        i0 = x0.astype(jnp.int32)
        i1 = i0 + 1
        w0 = (1.0 - dx)[..., None]
        w1 = dx[..., None]
        sk = 0.5 * (w0 * _gather_pad0(Kh, i0) + w1 * _gather_pad0(Kh, i1))
        sv = 0.5 * (w0 * _gather_pad0(Vh, i0) + w1 * _gather_pad0(Vh, i1))
        scores = jnp.einsum('bhqd,bhqkd->bhqk', Qh / math.sqrt(HD), sk)
        attn = jax.nn.softmax(scores, axis=-1)
        ctx = jnp.einsum('bhqk,bhqkd->bhqd', attn, sv)
        ctx = ctx.transpose(0, 2, 1, 3).reshape(Bq, Q, H * HD)
        return jnp.einsum('bqd,ed->bqe', ctx, Wo) + bo

    def _L1_ffn_ref(x, W_fc, W_proj):
        import jax, jax.numpy as jnp
        import numpy as np
        import math
        BETA = 0.9
        THRESHOLD = 1.0
        NUM_STEPS = 5
        ALPHA = 2.0

        @jax.custom_vjp
        def spike_fn(u):
            return (u > 0).astype(u.dtype)

        def _spike_fwd(u):
            return (spike_fn(u), u)

        def _spike_bwd(u, g):
            s = jnp.pi / 2.0 * ALPHA * u
            return (g * (ALPHA / 2.0) / (1.0 + s * s),)
        spike_fn.defvjp(_spike_fwd, _spike_bwd)
        h = jnp.square(jax.nn.relu(jnp.einsum('bsd,fd->bsf', x, W_fc)))
        y = jnp.einsum('bsf,df->bsd', h, W_proj)

        def step(mem, _):
            reset = jax.lax.stop_gradient(spike_fn(mem - THRESHOLD))
            mem_new = BETA * mem + y - reset * THRESHOLD
            spk = spike_fn(mem_new - THRESHOLD)
            return (mem_new, spk)
        mem0 = jnp.zeros_like(y)
        _, spks = jax.lax.scan(step, mem0, None, length=NUM_STEPS)
        return jnp.sum(spks, axis=0) / NUM_STEPS
    x = _layernorm(x + _L0_attn_ref(x, L0_attn_W_attn, L0_attn_b_attn, L0_attn_W_proj, L0_attn_b_proj, L0_attn_temperature), axis=-1)
    x = _layernorm(x + _L0_xattn_ref(x, ctx_1024, ctx_1024, L0_xattn_Wq, L0_xattn_Wk, L0_xattn_Wv, L0_xattn_Wo, L0_xattn_bo), axis=-1)
    x = _layernorm(x + _L0_ffn_ref(x, L0_ffn_gate_w, L0_ffn_fc_w, L0_ffn_proj_w), axis=-1)
    x = _layernorm(x + _L1_attn_ref(x, L1_attn_w_qkv, L1_attn_w_proj, L1_attn_b_proj), axis=-1)
    x = _layernorm(x + _L1_xattn_ref(ctx_1024, ctx_1024, x, mask_BxS2_if0, L1_xattn_Wk, L1_xattn_bk, L1_xattn_Wv, L1_xattn_bv, L1_xattn_Wq, L1_xattn_bq, L1_xattn_Woff, L1_xattn_boff, L1_xattn_Wo, L1_xattn_bo), axis=-1)
    x = _layernorm(x + _L1_ffn_ref(x, L1_ffn_W_fc, L1_ffn_W_proj), axis=-1)
    return x

_drawn_inputs = setup_inputs


def setup_inputs(seed=0):
    import zlib

    import numpy as np

    out = dict(_drawn_inputs(seed))
    spreads = {'L0_attn_b_attn': (0.0, 0.1),
     'L0_attn_b_proj': (0.0, 0.1),
     'L1_xattn_bk': (0.0, 2.0),
     'L1_xattn_bv': (0.0, 0.32),
     'L1_xattn_bq': (0.0, 2.0),
     'L1_xattn_boff': (0.0, 2.0),
     'L1_xattn_bo': (0.0, 0.1)}
    factors = {'L1_attn_b_proj': 2.854,
     'L1_xattn_Wk': 25.417,
     'L1_xattn_Wq': 8.0,
     'L1_xattn_Woff': 22.334}
    for name, (base, spread) in spreads.items():
        noise = np.random.default_rng([zlib.crc32(name.encode()), seed]).standard_normal(out[name].shape)
        drawn = base * np.exp(spread * noise) if base else spread * noise
        out[name] = jnp.asarray(drawn.astype(out[name].dtype))
    for name, factor in factors.items():
        out[name] = (out[name] * factor).astype(out[name].dtype)
    return out
```

```python
from contextlib import ExitStack

import numpy as np
import concourse.bass as bass
from concourse import mybir

F32 = mybir.dt.float32
F16 = mybir.dt.float16
BF16 = mybir.dt.bfloat16
I32 = mybir.dt.int32
ALU = mybir.AluOpType
ACT = mybir.ActivationFunctionType
AX = mybir.AxisListType.X

P = 128
D = 128
H = 16
E = D // H
NKEY = 77
NKP = 96
B = 4
T = B * P
HC = 4
NCH = H // HC
NE = 8
NF = 4
NS = 5
HS = H * NS
HH = H // 2
HHS = HH * NS
NCTR = 38
EPS = 1e-5
SEED = 1597463007.0


class Signal:

    def __init__(self, sem, per):
        self.sem, self.per = sem, per

    def at(self, g, n):
        return g * self.per + n


class Banks:

    def __init__(self, written, emptied):
        self.written, self.emptied = written, emptied
        self.turns = [0] * 8
        self.place = {}

    def product(self, name, bank):
        self.place[name] = (bank, self.turns[bank])
        self.turns[bank] += 1

    def bank(self, name):
        return self.place[name][0]


def plan_products(banks):
    for name, bank in (("xT", 0), 6), ("q1T", 7), ("k1T", 5), ("v1", 4), ("cT", 0), ("k2T", 1), ("v2", 2):
        banks.product(name, bank)
    for s in (1, 2):
        if s == 2:
            banks.product(("xT", 1), 6)
            banks.product("q2T", 7)
        for i in range(B * NCH):
            banks.product(("S", s, i), i % 2)
            banks.product(("PT", s, i), 2 + i % 2)
        for b in range(B):
            banks.product(("PV", s, b), 4 + b % 2)
            banks.product(("y", s, b), 6 + b % 2)
    banks.product(("xT", 2), 6)
    banks.product("gate", 7)
    for b in range(B):
        banks.product(("tab", b), 6 + b % 2)
    for i in range(NE * NF):
        banks.product(("h", i), i % 4)
    for e in range(NE):
        banks.product(("expert", e), 4 + e % 2)
    banks.product(("xT", 3), 6)
    banks.product("q4T", 7)
    for p in range(2):
        banks.product(("kv4", p), p)
    for b in range(B):
        banks.product(("kvsum", b), 2 + b % 2)
    for p in range(2):
        banks.product(("nd", p), 4 + p)
    banks.product("y4", 7)
    banks.product(("xT", 4), 6)
    banks.product("q5T", 7)
    banks.product("q5", 5)
    banks.product("off", 4)
    for half in range(2):
        banks.product(("uT", half), 6 + half)
    for j in range(HS):
        banks.product(("hit", j), (0, 1, 2, 7)[j % 4])
    for h in range(H):
        for p in range(2):
            banks.product(("G", h, p), 3 + 2 * (h % 2) + p)
    banks.product("c5T", 0)
    banks.product("y5", 1)
    banks.product(("xT", 5), 6)
    for c in range(NF):
        banks.product(("h6", c), c)
    banks.product("y6", 4)


def decoder(nc, a, out):
    NB = a["x"].shape[0]
    G = NB // B
    with ExitStack() as ctx:
        def sb(name, shape, dt=F32):
            return ctx.enter_context(nc.sbuf_tensor(name, shape, dt))

        def sem(name):
            return ctx.enter_context(nc.semaphore(name))

        def signal(name, per):
            return Signal(sem(name), per)

        ps = ctx.enter_context(nc.psum_tensor("ps", [P, 8, 512], F32))
        banks = Banks([sem(f"bank{k}_written") for k in range(8)], [sem(f"bank{k}_emptied") for k in range(8)])
        plan_products(banks)

        def may_write(eng, g, name):
            k, n = banks.place[name]
            eng.wait_ge(banks.emptied[k], g * banks.turns[k] + n + 1)

        def written(eng, g, name):
            k, n = banks.place[name]
            eng.wait_ge(banks.written[k], g * banks.turns[k] + n + 1)

        def emptied(eng, g, name):
            k, n = banks.place[name]
            eng.wait_ge(banks.emptied[k], g * banks.turns[k] + n + 2)

        def wr(name):
            return banks.written[banks.bank(name)]

        def em(name):
            return banks.emptied[banks.bank(name)]

        def ap(name):
            return ps[:, banks.bank(name), :]

        ident = sb("ident", [P, P])
        w1_qkv = sb("w1_qkv", [D, 3 * D])
        w1_o = sb("w1_o", [D, D])
        w2_q = sb("w2_q", [D, D])
        w2_k = sb("w2_k", [D, D])
        w2_v = sb("w2_v", [D, D])
        w2_o = sb("w2_o", [D, D])
        w3_gate = sb("w3_gate", [D, P])
        w3_fc = sb("w3_fc", [D, NE, NF * P])
        w3_proj = sb("w3_proj", [P, NE, NF, D])
        w4_q = sb("w4_q", [D, D])
        w4_kv = sb("w4_kv", [D, 2 * D])
        w4_o = sb("w4_o", [D, D])
        w5_kv = sb("w5_kv", [D, 2 * D])
        w5_q = sb("w5_q", [D, D])
        w5_off = sb("w5_off", [D, P])
        w5_o = sb("w5_o", [D, D])
        w6_fc = sb("w6_fc", [D, NF * P])
        w6_proj = sb("w6_proj", [P, NF, D])
        bias1 = sb("bias1", [P, H, P])
        b1_qk = sb("b1_qk", [D, 2])
        b1_v = sb("b1_v", [P, D])
        b1_o = sb("b1_o", [P, D])
        b2_o = sb("b2_o", [P, D])
        b4_o = sb("b4_o", [P, D])
        b5_qcol = sb("b5_qcol", [D, 1])
        b5_q = sb("b5_q", [P, D])
        b5_off = sb("b5_off", [P, HS])
        b5_o = sb("b5_o", [P, D])
        b5_tab = sb("b5_tab", [NKP, 4, D])
        temp = sb("temp", [P, 1])
        qscale1 = sb("qscale1", [P, 1])
        qbias1 = sb("qbias1", [P, 1])
        ramp = sb("ramp", [P, HS])
        token = sb("token", [P, 1])
        zero64 = sb("zero64", [P, HH * E])
        b5_qs = sb("b5_qs", [P, D])
        glen = sb("glen", [P, 3, B])
        pick = sb("pick", [NKP, HHS, NKP], F16)
        hitbias = sb("hitbias", [NKP, 1])
        rank8 = sb("rank8", [P, NE])
        block4 = sb("block4", [P, 2, D])
        masked = sb("masked", [P, NB])
        length = sb("length", [P, NB])
        length2 = sb("length2", [P, NB])

        xin = sb("xin", [P, B, D])
        ctxin = sb("ctxin", [NKEY, B, D])
        xs = sb("xs", [P, B, D])
        xb = sb("xb", [P, B, D])
        ys = sb("ys", [P, B, D])
        xout = sb("xout", [P, B, D])
        xT = sb("xT", [D, T])
        cT = sb("cT", [D, B, P])
        qT = sb("qT", [D, T])
        kT = sb("kT", [D, T])
        k2T = sb("k2T", [D, B, NKEY])
        v1 = sb("v1", [P, B, D])
        v2 = sb("v2", [NKP, B, D])
        KM = sb("KM", [D, 2, H, P])
        VM = sb("VM", [P, 2, 2, HH * P])
        Pq = sb("Pq", [P, 4, HC, P])
        mx = sb("mx", [P, 4, HC])
        PT = [sb("pt1", [P, 2, HC * P]), sb("pt2", [NKP, 2, HC * P])]
        rden = sb("rden", [P // 2, 2, 2, P])
        oT = sb("oT", [D, 2, P])
        stats = sb("stats", [P, B, 6])
        mv = sb("mv", [P, B, 2])
        pause = sb("pause", [P, 1])
        vare = sb("vare", [P, B])
        hvar = sb("hvar", [P, B])
        rs = sb("rs", [P, 2, B])
        nt = sb("nt", [P, 2, B])
        gl = sb("gl", [P, 10, B, NE])
        gm = sb("gm", [P, 6, B])
        gw = sb("gw", [P, B, NE])
        hT = sb("hT", [P, 2, NF, T])
        hflat = hT[:, :, :, :].rearrange("p a c t -> p (a c t)")
        pflat = Pq[:, :, :, :].rearrange("p a h k -> p (a h k)")
        mask_i = hflat[:, 0:NB * NKEY].bitcast(I32).rearrange("p (b k) -> p b k", b=NB)
        tabf = Pq[0:NKP, 0:2, :, :]
        tabr = Pq[0:NKP, 2:4, :, :]
        tab = sb("tab", [NKP, B, 3, H, 4 * E], BF16)
        e4 = hT[:, 0, 0:2, :]
        t4 = hT[:, 0, 2:4, :]
        k4 = hT[:, 1, 2, :].rearrange("p (b d) -> p b d", b=B)
        v4 = sb("v4", [P, B, 2 * D])
        kv4 = sb("kv4", [D, B, 2 * D])
        dn4 = hT[:, 1, 0:2, :].rearrange("p a (b t) -> p a b t", b=2)
        q5 = sb("q5", [P, H, B, E])
        NI = B * HS
        ix = [pflat[:, n * NI:(n + 1) * NI].rearrange("p (b j) -> p b j", b=B) for n in range(4)]
        w01 = sb("w01", [P, B, HS, 2])
        uu = sb("uu", [P, B, 2, NKP])
        uT = sb("uT", [NKP, 2, T], F16)
        NHIT = 6
        hit = sb("hit", [NKP, NHIT, T], BF16)
        NKV, NPR = HH * B * NS * 2 * E, HH * B * NS * E
        kvs = hflat[:, 0:NKV].rearrange("p (h b n e) -> p h b n e", h=HH, b=B, n=NS)
        gwt = hflat[:, NKV:NKV + 4 * 4 * NS * 2 * E].rearrange("p (k b n s e) -> p k b n s e", k=4, b=2, n=NS, s=2)
        prod5 = pflat[:, 0:NPR].rearrange("p (a n e) -> p a n e", n=NS, e=E)
        sc5 = pflat[:, NPR:NPR + 3 * HH * B * NS].rearrange("p (k a n) -> p k a n", k=3, n=NS)
        sm5 = sb("sm5", [P, 4, HH * B])
        o5 = sb("o5", [P, B, D])
        lif = hT[:, 1, :, :]

        w_loaded = sem("weights_loaded")
        zeroed = sem("constants_zeroed")
        prepared = sem("constants_prepared")
        x_loaded = signal("x_loaded", 16)
        c_loaded = signal("context_loaded", 16)
        km_loaded = [[signal(f"masked_keys{s}_slot{k}_loaded", 16 * H * B // 2) for k in range(2)] for s in (1, 2)]
        vm_ready = [signal("masked_values1_ready", B), signal("masked_values2_ready", B)]
        max_ready = signal("row_maxima_ready", B * NCH)
        shifted = signal("scores_shifted", B * NCH)
        probs = signal("probabilities_ready", 2 * B * NCH)
        inputs_used = signal("inputs_used", 1)
        xb_ready = signal("residual_ready", 3)
        ln_ready = signal("layer_norm_ready", 6)
        gate_shifted = signal("gates_shifted", 1)
        gate_exp = signal("gates_exponentiated", 1)
        tab_ready = signal("tables_ready", B)
        e4_ready = signal("elu_exponentials_ready", 3)
        q4_ready = signal("linear_q_ready", 1)
        k4_ready = signal("linear_k_ready", 2)
        uu_ready = signal("samples_ready", 1)
        kvs_ready = signal("sampled_keys_values_ready", 2 * H)
        s5_shifted = signal("sample_scores_shifted", 2)
        s5_exp = signal("sample_scores_exponentiated", 2)
        o5_ready = signal("sampled_output_ready", 2)
        h6_ready = signal("spiking_hidden_ready", NF)
        chain = sem("vector_chain")
        stored = sem("output_stored")

        NLOAD = [0]
        NZ = 12
        NPREP = 7
        CHAIN_PER = 209

        block = ctx.enter_context(nc.Block())

        @block.sync
        def _(sp):
            def load(dst, src):
                sp.dma_start(dst, src).then_inc(w_loaded, 16)
                NLOAD[0] += 1

            load(ident[:, :], a["c_ident"])
            load(w1_qkv[:, :], a["L0_attn_W_attn"])
            load(w1_o[:, :], a["L0_attn_W_proj"])
            load(w2_q[:, :], a["L0_xattn_Wq"])
            load(w2_k[:, :], a["L0_xattn_Wk"])
            load(w2_v[:, :], a["L0_xattn_Wv"])
            load(w2_o[:, :], a["L0_xattn_Wo"])
            for t in range(2):
                load(b1_qk[:, t:t + 1], a["L0_attn_b_attn"][t * D:(t + 1) * D].rearrange("(p a) -> p a", a=1))
            load(b1_v[:, :], a["L0_attn_b_attn"][2 * D:3 * D].rearrange("(a d) -> a d", a=1).broadcast_to([P, D]))
            for dst, name in (b1_o, "L0_attn_b_proj"), (b2_o, "L0_xattn_bo"), (b4_o, "L1_attn_b_proj"), \
                    (b5_q, "L1_xattn_bq"), (b5_off, "L1_xattn_boff"), (b5_o, "L1_xattn_bo"):
                n = dst.shape[1]
                load(dst[:, :], a[name].rearrange("(a d) -> a d", a=1).broadcast_to([P, n]))
            load(temp[:, :], a["L0_attn_temperature"].rearrange("(a d) -> a d", a=1).broadcast_to([P, 1]))
            load(bias1[:, :, :], a["c_bias1"])
            load(w4_q[:, :], a["w4T"][:, 0:D])
            load(w4_kv[:, :], a["w4T"][:, D:3 * D])
            load(w4_o[:, :], a["w4_oT"])
            load(w5_kv[:, 0:D], a["w5_kT"])
            load(w5_kv[:, D:2 * D], a["w5_vT"])
            load(w5_q[:, :], a["w5_qT"])
            load(w5_o[:, :], a["w5_oT"])
            load(b5_qcol[:, :], a["L1_xattn_bq"].rearrange("(p a) -> p a", a=1))
            load(w6_fc[:, :], a["w6_fcT"])
            load(w6_proj[:, :, :], a["w6_projT"].rearrange("(c p) d -> p c d", p=P))
            load(ramp[:, :], a["c_ramp"])
            load(token[:, :], a["c_token"])
            load(pick[:, :, :], a["c_pick"])
            load(hitbias[:, :], a["c_hitbias"])
            load(rank8[:, :], a["c_rank8"])
            load(block4[:, :, :], a["c_block4"])
            load(mask_i, a["mask_BxS2_if0"].rearrange("(a b) k -> a b k", a=1).broadcast_to([P, NB, NKEY]))
            load(w3_fc[:, :, :], a["L0_ffn_fc_w"].rearrange("e d f -> d e f"))
            load(w3_proj[:, :, :, :], a["L0_ffn_proj_w"].rearrange("e (c p) d -> p e c d", p=P))
            sp.wait_ge(zeroed, NZ)
            load(w3_gate[:, 0:NE], a["L0_ffn_gate_w"])
            load(w5_off[:, 0:HS], a["w5_offT"])
            for s in range(2):
                lo = 1 - s
                load(b5_tab[lo:lo + NKEY, 2 * s, :],
                     a["L1_xattn_bk"].rearrange("(a d) -> a d", a=1).broadcast_to([NKEY, D]))
                load(b5_tab[lo:lo + NKEY, 2 * s + 1, :],
                     a["L1_xattn_bv"].rearrange("(a d) -> a d", a=1).broadcast_to([NKEY, D]))
            with sp.Fori(0, G, 1) as g:
                x_at, c_at = sp.snap(g * (B * P * D)), sp.snap(g * (B * NKEY * D))
                sp.wait_ge(inputs_used.sem, inputs_used.at(g, 1))
                group = lambda t, at, rows: bass.AP(t.tensor, at, [[D, rows], [rows * D, B], [1, D]])
                sp.dma_start(xin[:, :, :], group(a["x"], x_at, P)).then_inc(x_loaded.sem, 16)
                sp.dma_start(ctxin[:, :, :], group(a["ctx_1024"], c_at, NKEY)).then_inc(c_loaded.sem, 16)
                for s in range(2):
                    for b in range(B):
                        if s == 0 and b == 0:
                            emptied(sp, g, "k1T")
                        if s == 0 and b >= 2:
                            written(sp, g, ("S", 1, (b - 1) * NCH - 1))
                        if s == 1:
                            written(sp, g, ("S", 1, (b + 3) * NCH - 1) if b < 2 else ("S", 2, (b - 1) * NCH - 1))
                        for h in range(H):
                            src = kT[E * h:E * h + E, b * P:(b + 1) * P] if s == 0 else k2T[E * h:E * h + E, b, :]
                            sp.dma_start(KM[E * h:E * h + E, b % 2, h, 0:src.shape[1]], src).then_inc(km_loaded[s][b % 2].sem, 16)
                sp.wait_ge(ln_ready.sem, ln_ready.at(g, 6))
                sp.dma_start(group(out, x_at, P), xout[:, :, :]).then_inc(stored, 16)
            sp.wait_ge(stored, 16 * (G + 1))

        @block.tensor
        def _(pe):
            def mm(o, lhsT, rhs, start=True, stop=True):
                return pe.matmul(o, lhsT, rhs, start=start, stop=stop)

            pe.wait_ge(w_loaded, 16 * NLOAD[0])
            pe.wait_ge(zeroed, NZ)
            pe.wait_ge(prepared, NPREP)
            with pe.Fori(0, G, 1) as g:
                def transpose_x(s, src):
                    may_write(pe, g, ("xT", s))
                    for b in range(B):
                        m = pe.transpose(ap(("xT", s))[:, b * P:(b + 1) * P], src[:, b, :], ident[:, :])
                    m.then_inc(wr(("xT", s)), 1)

                def project(name, w, x):
                    may_write(pe, g, name)
                    mm(ap(name), w, x).then_inc(wr(name), 1)

                def project_rows(name, w, x, n, m=P):
                    may_write(pe, g, name)
                    for b in range(B):
                        last = mm(ap(name)[0:m, b * P:b * P + n], x(b), w)
                    last.then_inc(wr(name), 1)

                pe.wait_ge(x_loaded.sem, x_loaded.at(g, 16))
                transpose_x(0, xin)
                emptied(pe, g, ("xT", 0))
                project("k1T", w1_qkv[:, D:2 * D], xT[:, :])
                project("q1T", w1_qkv[:, 0:D], xT[:, :])
                project_rows("v1", w1_qkv[:, 2 * D:3 * D], lambda b: xT[:, b * P:(b + 1) * P], D)
                pe.wait_ge(c_loaded.sem, c_loaded.at(g, 16))
                may_write(pe, g, "cT")
                for b in range(B):
                    m = pe.transpose(ap("cT")[:, b * P:b * P + NKEY], ctxin[:, b, :], ident[0:NKEY, 0:NKEY])
                m.then_inc(wr("cT"), 1)
                emptied(pe, g, "cT")
                may_write(pe, g, "k2T")
                mm(ap("k2T")[:, 0:B * NKEY], w2_k[:, :], cT[:, :, 1:1 + NKEY]).then_inc(wr("k2T"), 1)
                project_rows("v2", w2_v[:, :], lambda b: cT[:, b, 1:1 + NKP], D, NKP)

                def attention(s):
                    nk = (P, NKEY)[s - 1]
                    rows = (P, NKP)[s - 1]

                    def scores(i):
                        b, c = divmod(i, NCH)
                        if c == 0:
                            loaded = km_loaded[s - 1][b % 2]
                            pe.wait_ge(loaded.sem, loaded.at(g, 16 * H * (b // 2 + 1)))
                        may_write(pe, g, ("S", s, i))
                        mm(ap(("S", s, i))[:, 0:HC * nk], qT[:, b * P:(b + 1) * P],
                           KM[:, b % 2, c * HC:(c + 1) * HC, 0:nk]).then_inc(wr(("S", s, i)), 1)

                    def transposes(i):
                        pe.wait_ge(probs.sem, probs.at(g, (s - 1) * B * NCH + i + 1))
                        may_write(pe, g, ("PT", s, i))
                        for n in range(HC):
                            m = pe.transpose(ap(("PT", s, i))[0:nk, n * P:(n + 1) * P], Pq[:, i % 4, n, 0:nk],
                                             ident[:, :])
                        m.then_inc(wr(("PT", s, i)), 1)

                    def mix(i):
                        b, c = divmod(i, NCH)
                        name = ("PV", s, b)
                        if c == 0:
                            pe.wait_ge(vm_ready[s - 1].sem, vm_ready[s - 1].at(g, b + 1))
                            may_write(pe, g, name)
                        emptied(pe, g, ("PT", s, i))
                        for n in range(HC):
                            h = c * HC + n
                            half, r = divmod(h, HH)
                            m = mm(ap(name)[:, half * P:(half + 1) * P],
                                   VM[0:rows, b % 2, half, r * P:(r + 1) * P],
                                   PT[s - 1][0:rows, i % 2, n * P:(n + 1) * P], start=(r == 0), stop=(r == HH - 1))
                        if c == NCH - 1:
                            m.then_inc(wr(name), 1)

                    def output(b):
                        emptied(pe, g, ("PV", s, b))
                        may_write(pe, g, ("y", s, b))
                        mm(ap(("y", s, b))[:, 0:D], oT[:, b % 2, :], (w1_o, w2_o)[s - 1][:, :])\
                            .then_inc(wr(("y", s, b)), 1)

                    N = B * NCH
                    for i in range(N + 4):
                        if i < N:
                            scores(i)
                        if 3 <= i < N + 3:
                            transposes(i - 3)
                        if 4 <= i:
                            mix(i - 4)
                        if i >= 9 and (i - 9) % NCH == 0:
                            output((i - 9) // NCH)
                    output(B - 1)

                attention(1)
                pe.wait_ge(ln_ready.sem, ln_ready.at(g, 1))
                transpose_x(1, xs)
                emptied(pe, g, ("xT", 1))
                project("q2T", w2_q[:, :], xT[:, :])
                emptied(pe, g, "q2T")
                attention(2)

                pe.wait_ge(ln_ready.sem, ln_ready.at(g, 2))
                transpose_x(2, xs)
                emptied(pe, g, ("xT", 2))
                project_rows("gate", w3_gate[:, :], lambda b: xT[:, b * P:(b + 1) * P], P)

                def table(b):
                    may_write(pe, g, ("tab", b))
                    for s in range(2):
                        m = mm(ap(("tab", b))[0:NKP, s * 2 * D:(s + 1) * 2 * D], cT[:, b, s:s + NKP], w5_kv[:, :])
                    m.then_inc(wr(("tab", b)), 1)

                def hidden(e):
                    for c in range(NF):
                        name = ("h", e * NF + c)
                        may_write(pe, g, name)
                        mm(ap(name), w3_fc[:, e, c * P:(c + 1) * P], xT[:, :]).then_inc(wr(name), 1)

                def expert(e):
                    may_write(pe, g, ("expert", e))
                    for c in range(NF):
                        emptied(pe, g, ("h", e * NF + c))
                    for b in range(B):
                        for c in range(NF):
                            m = mm(ap(("expert", e))[:, b * P:(b + 1) * P], hT[:, e % 2, c, b * P:(b + 1) * P],
                                   w3_proj[:, e, c, :], start=(c == 0), stop=(c == NF - 1))
                    m.then_inc(wr(("expert", e)), 1)

                for e in range(NE + 1):
                    if e < NE:
                        hidden(e)
                    if 1 <= e <= 4:
                        table(e - 1)
                    if e >= 1:
                        expert(e - 1)

                pe.wait_ge(ln_ready.sem, ln_ready.at(g, 3))
                transpose_x(3, xs)
                emptied(pe, g, ("xT", 3))
                for p in range(2):
                    may_write(pe, g, ("kv4", p))
                    for j in range(2):
                        b = 2 * p + j
                        m = mm(ap(("kv4", p))[:, j * 2 * D:(j + 1) * 2 * D], xT[:, b * P:(b + 1) * P], w4_kv[:, :])
                    m.then_inc(wr(("kv4", p)), 1)
                project("q4T", w4_q[:, :], xT[:, :])
                for b in range(B):
                    pe.wait_ge(k4_ready.sem, k4_ready.at(g, b // 2 + 1))
                    may_write(pe, g, ("kvsum", b))
                    mm(ap(("kvsum", b))[:, 0:2 * D], k4[:, b, :], v4[:, b, :]).then_inc(wr(("kvsum", b)), 1)
                pe.wait_ge(q4_ready.sem, q4_ready.at(g, 1))
                for p in range(2):
                    may_write(pe, g, ("nd", p))
                    for j in range(2):
                        b = 2 * p + j
                        emptied(pe, g, ("kvsum", b))
                        for t in range(2):
                            m = mm(ap(("nd", p))[:, (2 * t + j) * P:(2 * t + j + 1) * P],
                                   kv4[:, b, t * D:(t + 1) * D], qT[:, b * P:(b + 1) * P])
                    m.then_inc(wr(("nd", p)), 1)
                may_write(pe, g, "y4")
                for b in range(B):
                    emptied(pe, g, ("nd", b // 2))
                    m = mm(ap("y4")[:, b * P:(b + 1) * P], t4[:, 0, b * P:(b + 1) * P], w4_o[:, :])
                m.then_inc(wr("y4"), 1)

                pe.wait_ge(ln_ready.sem, ln_ready.at(g, 4))
                transpose_x(4, xs)
                emptied(pe, g, ("xT", 4))
                project("q5T", w5_q[:, :], xT[:, :])
                project_rows("q5", w5_q[:, :], lambda b: xT[:, b * P:(b + 1) * P], D)
                emptied(pe, g, "q5T")
                project_rows("off", w5_off[:, :], lambda b: qT[:, b * P:(b + 1) * P], P)
                pe.wait_ge(uu_ready.sem, uu_ready.at(g, 1))
                for half in range(2):
                    may_write(pe, g, ("uT", half))
                    for b in range(B):
                        m = pe.transpose(ap(("uT", half))[0:NKP, b * P:(b + 1) * P], uu[:, b, half, :], ident[:, :])
                    m.then_inc(wr(("uT", half)), 1)
                pe.wait_ge(tab_ready.sem, tab_ready.at(g, B))
                emptied(pe, g, ("uT", 0))
                emptied(pe, g, ("uT", 1))

                def spread(j):
                    may_write(pe, g, ("hit", j))
                    mm(ap(("hit", j))[0:NKP, :], pick[:, j % HHS, :], uT[:, j // HHS, :]).then_inc(wr(("hit", j)), 1)

                def gather(j):
                    h, n = divmod(j, NS)
                    emptied(pe, g, ("hit", j))
                    for p in range(2):
                        name = ("G", h, p)
                        if n == 0:
                            may_write(pe, g, name)
                        for t in range(2):
                            b = 2 * p + t
                            o = t * 256 + n * 4 * E
                            for part in range(3):
                                m = mm(ap(name)[:, o:o + 4 * E], hit[:, j % NHIT, b * P:(b + 1) * P],
                                       tab[:, b, part, h, :], start=(part == 0), stop=(part == 2))
                        if n == NS - 1:
                            m.then_inc(wr(name), 1)

                for j in range(HS + 3):
                    if j < HS:
                        spread(j)
                    if j >= 3:
                        gather(j - 3)
                pe.wait_ge(o5_ready.sem, o5_ready.at(g, 2))
                may_write(pe, g, "c5T")
                for b in range(B):
                    m = pe.transpose(ap("c5T")[:, b * P:(b + 1) * P], o5[:, b, :], ident[:, :])
                m.then_inc(wr("c5T"), 1)
                emptied(pe, g, "c5T")
                project_rows("y5", w5_o[:, :], lambda b: kT[:, b * P:(b + 1) * P], D)

                pe.wait_ge(ln_ready.sem, ln_ready.at(g, 5))
                transpose_x(5, xs)
                emptied(pe, g, ("xT", 5))
                for c in range(NF):
                    may_write(pe, g, ("h6", c))
                    mm(ap(("h6", c)), w6_fc[:, c * P:(c + 1) * P], xT[:, :]).then_inc(wr(("h6", c)), 1)
                pe.wait_ge(h6_ready.sem, h6_ready.at(g, NF))
                may_write(pe, g, "y6")
                for b in range(B):
                    for c in range(NF):
                        m = mm(ap("y6")[:, b * P:(b + 1) * P], hT[:, 0, c, b * P:(b + 1) * P], w6_proj[:, c, :],
                               start=(c == 0), stop=(c == NF - 1))
                m.then_inc(wr("y6"), 1)

        @block.scalar
        def _(act):
            def copy(o, i):
                return act.copy(o, i)

            act.wait_ge(prepared, NPREP)
            act.wait_ge(w_loaded, 16 * NLOAD[0])
            act.wait_ge(zeroed, NZ)
            with act.Fori(0, G, 1) as g:
                def take_xT(s):
                    written(act, g, ("xT", s))
                    copy(xT[:, :], ap(("xT", s))).then_inc(em(("xT", s)), 1)

                take_xT(0)
                written(act, g, "k1T")
                act.activation(kT[:, :], ap("k1T"), ACT.Identity, bias=b1_qk[:, 1:2]).then_inc(em("k1T"), 1)
                written(act, g, "q1T")
                act.activation(qT[:, :], ap("q1T"), ACT.Identity, bias=qbias1[:, :], scale=qscale1[:, :])\
                    .then_inc(em("q1T"), 1)
                written(act, g, "v1")
                copy(v1[:, :, :], ap("v1")).then_inc(em("v1"), 1)
                written(act, g, "cT")
                copy(cT[:, :, 1:1 + NKEY], ap("cT").rearrange("p (b k) -> p b k", b=B)[:, :, 0:NKEY])\
                    .then_inc(em("cT"), 1)
                written(act, g, "k2T")
                copy(k2T[:, :, :], ap("k2T")[:, 0:B * NKEY]).then_inc(em("k2T"), 1)
                written(act, g, "v2")
                copy(v2[:, :, :], ap("v2")[0:NKP, :]).then_inc(em("v2"), 1)

                def attention(s):
                    nk = (P, NKEY)[s - 1]
                    N = B * NCH
                    for i in range(N + 1):
                        if i < N:
                            if s == 1:
                                act.wait_ge(shifted.sem, shifted.at(g, i + 1))
                            else:
                                emptied(act, g, ("S", s, i))
                            act.activation(Pq[:, i % 4, :, 0:nk], Pq[:, i % 4, :, 0:nk], ACT.Exp).then_inc(probs.sem, 1)
                        if i >= 1:
                            written(act, g, ("PT", s, i - 1))
                            copy(PT[s - 1][0:nk, (i - 1) % 2, :], ap(("PT", s, i - 1))[0:nk, :])\
                                .then_inc(em(("PT", s, i - 1)), 1)

                attention(1)
                take_xT(1)
                written(act, g, "q2T")
                act.activation(qT[:, :], ap("q2T"), ACT.Copy, scale=float(E) ** -0.5).then_inc(em("q2T"), 1)
                attention(2)

                take_xT(2)
                act.wait_ge(gate_shifted.sem, gate_shifted.at(g, 1))
                act.activation(gl[:, 8, :, :], gl[:, 7, :, :], ACT.Exp).then_inc(gate_exp.sem, 1)
                for i in range(NE * NF):
                    e, c = divmod(i, NF)
                    written(act, g, ("h", i))
                    act.activation(hT[:, e % 2, c, :], ap(("h", i)), ACT.Gelu).then_inc(em(("h", i)), 1)

                take_xT(3)
                for p in range(2):
                    written(act, g, ("kv4", p))
                    act.activation(e4[:, 0, p * 2 * P:(p + 1) * 2 * P].rearrange("p (b k) -> p b k", b=2),
                                   ap(("kv4", p)).rearrange("p (b k) -> p b k", b=2)[:, :, 0:D], ACT.Exp)\
                        .then_inc(e4_ready.sem, 1)
                written(act, g, "q4T")
                act.activation(e4[:, 1, :], ap("q4T"), ACT.Exp).then_inc(e4_ready.sem, 1)

                take_xT(4)
                written(act, g, "q5T")
                act.activation(qT[:, :], ap("q5T"), ACT.Identity, bias=b5_qcol[:, :]).then_inc(em("q5T"), 1)
                for half in range(2):
                    written(act, g, ("uT", half))
                    copy(uT[:, half, :], ap(("uT", half))[0:NKP, :]).then_inc(em(("uT", half)), 1)

                def soften(half):
                    act.wait_ge(s5_shifted.sem, s5_shifted.at(g, half + 1))
                    act.activation(sc5[:, 2, :, :], sc5[:, 1, :, :], ACT.Exp).then_inc(s5_exp.sem, 1)

                for j in range(HS):
                    if j % NS == NS - 1:
                        continue
                    written(act, g, ("hit", j))
                    act.activation(hit[:, j % NHIT, :], ap(("hit", j))[0:NKP, :], ACT.Relu, bias=hitbias[:, :])\
                        .then_inc(em(("hit", j)), 1)
                    if j == (HH + 2) * NS:
                        soften(0)
                soften(1)
                written(act, g, "c5T")
                copy(kT[:, :], ap("c5T")).then_inc(em("c5T"), 1)
                take_xT(5)
                for c in range(NF):
                    written(act, g, ("h6", c))
                    act.activation(hT[:, 1, c, :], ap(("h6", c)), ACT.Relu).then_inc(em(("h6", c)), 1)

        @block.gpsimd
        def _(pool):
            for k in range(8):
                pool.sem_inc(banks.emptied[k], 1)
            pool.sem_inc(inputs_used.sem, 1)
            pool.sem_inc(stored, 16)
            pool.memset(w3_gate[:, :], 0.0).then_inc(zeroed, 1)
            pool.memset(w5_off[:, :], 0.0).then_inc(zeroed, 1)
            pool.memset(b5_tab[:, :, :], 0.0).then_inc(zeroed, 1)
            pool.memset(cT[:, :, :], 0.0).then_inc(zeroed, 1)
            pool.memset(KM[:, :, :, :], 0.0).then_inc(zeroed, 1)
            pool.memset(VM[:, :, :, :], 0.0).then_inc(zeroed, 1)
            pool.memset(PT[1][:, :, :], 0.0).then_inc(zeroed, 1)
            pool.memset(uu[:, :, :, :], 0.0).then_inc(zeroed, 1)
            pool.memset(zero64[:, :], 0.0).then_inc(zeroed, 1)
            pool.wait_ge(zeroed, 9)
            for slot in range(2):
                for half in range(2):
                    v = VM[:, slot, half, :]
                    ones = bass.AP(v.tensor, v.offset + HH * E, [list(v.ap[0]), [P + E, HH], [1, E]])
                    last = pool.memset(ones, 1.0)
            last.then_inc(zeroed, 1)
            pool.memset(v4[:, :, D:2 * D], 1.0).then_inc(zeroed, 1)
            pool.memset(mx[:, :, :], 0.0).then_inc(zeroed, 1)
            pool.wait_ge(w_loaded, 16 * NLOAD[0])
            with pool.Fori(0, G, 1) as g:
                def residual(src, bias, ready=xb_ready):
                    pool.tensor_tensor(xb[:, :, :], src[:, :, :], bias[:, :].unsqueeze(1).broadcast_to([P, B, D]),
                                       ALU.add).then_inc(ready.sem, 1)

                def values(s, b):
                    emptied(pool, g, ("v1", "v2")[s - 1])
                    if b >= 2:
                        written(pool, g, ("PV", s, b - 2))
                    rows = (P, NKP)[s - 1]
                    for half in range(2):
                        v = VM[0:rows, b % 2, half, :]
                        o = bass.AP(v.tensor, v.offset, [list(v.ap[0]), [P + E, HH], [1, E]])
                        src = (v1, v2)[s - 1][0:rows, b, half * HH * E:(half + 1) * HH * E].rearrange("p (h e) -> p h e", e=E)
                        if s == 1:
                            bias = b1_v[:, half * HH * E:(half + 1) * HH * E].rearrange("p (h e) -> p h e", e=E)
                        else:
                            bias = zero64[0:rows, :].rearrange("p (h e) -> p h e", e=E)
                        m = pool.tensor_tensor(o, src, bias, ALU.add)
                    m.then_inc(vm_ready[s - 1].sem, 1)

                def shift(i):
                    pool.wait_ge(max_ready.sem, max_ready.at(g, i + 1))
                    pool.tensor_tensor(Pq[:, i % 4, :, :], Pq[:, i % 4, :, :],
                                       mx[:, i % 4, :].unsqueeze(2).broadcast_to([P, HC, P]), ALU.subtract)\
                        .then_inc(shifted.sem, 1)

                pool.wait_ge(x_loaded.sem, x_loaded.at(g, 16))
                values(1, 0)
                values(1, 1)
                emptied(pool, g, "cT")
                residual(xin, b1_o, inputs_used)
                for i in range(B * NCH):
                    shift(i)
                    if i in (5, 9):
                        values(1, (i + 3) // 4)
                pool.wait_ge(ln_ready.sem, ln_ready.at(g, 1))
                residual(xs, b2_o)
                for b in range(B):
                    values(2, b)
                pool.wait_ge(ln_ready.sem, ln_ready.at(g, 3))
                residual(xs, b4_o)
                pool.wait_ge(ln_ready.sem, ln_ready.at(g, 4))
                residual(xs, b5_o)
                for k in range(2 * H):
                    h, p = divmod(k, 2)
                    emptied(pool, g, ("G", h, p))
                    if k == H:
                        pool.wait_ge(o5_ready.sem, o5_ready.at(g, 1))
                    pool.tensor_tensor(kvs[:, h % HH, 2 * p:2 * p + 2, :, :].rearrange("q b n e -> q (b n) e"),
                                       gwt[:, k % 4, :, :, 0, :].rearrange("q b n e -> q (b n) e"),
                                       gwt[:, k % 4, :, :, 1, :].rearrange("q b n e -> q (b n) e"),
                                       ALU.add).then_inc(kvs_ready.sem, 1)


        @block.vector
        def _(dve):
            V = nc.vector
            pre = [0]

            def prep(ins, last=False):
                ins.then_inc(prepared, 1)
                pre[0] += 1
                dve.wait_ge(prepared, pre[0])

            dve.wait_ge(w_loaded, 16 * NLOAD[0])
            prep(dve.reciprocal(temp[:, :], temp[:, :]))
            prep(dve.tensor_scalar(qscale1[:, :], temp[:, :], float(E) ** -0.5, None, ALU.mult))
            prep(dve.tensor_tensor(qbias1[:, :], b1_qk[:, 0:1], qscale1[:, :], ALU.mult))
            prep(dve.tensor_scalar(b5_qs[:, :], b5_q[:, :], 0.5 * float(E) ** -0.5, None, ALU.mult))
            prep(dve.tensor_reduce(masked[:, :], mask_i, AX, ALU.add))
            prep(dve.tensor_scalar(length[:, :], masked[:, :], -1.0, float(NKEY - 1), ALU.mult, ALU.add))
            prep(dve.tensor_tensor(length2[:, :], length[:, :], length[:, :], ALU.mult))
            assert pre[0] == NPREP, pre
            with dve.Fori(0, G, 1) as g:
                links = [0]

                def link(ins):
                    ins.then_inc(chain, 1)
                    links[0] += 1
                    dve.wait_ge(chain, g * CHAIN_PER + links[0])

                def bc(t, n):
                    return t.unsqueeze(len(t.shape)).broadcast_to([*t.shape, n])

                def per_batch(t, n=B):
                    return t.unsqueeze(1).broadcast_to([t.shape[0], n, *t.shape[1:]])

                def layer_norm(dst):
                    for b in range(B):
                        m = dve.bn_stats(stats[:, b, :], ys[:, b, :])
                    link(m)
                    dve.memset(pause[:, :], 0.0)
                    for b in range(B):
                        m = dve.bn_aggr(mv[:, b, :], stats[:, b, :])
                    link(m)
                    link(dve.tensor_scalar(vare[:, :], mv[:, :, 1], EPS, None, ALU.add))
                    dve.tensor_scalar(hvar[:, :], vare[:, :], -0.5, None, ALU.mult)
                    link(dve.tensor_scalar(rs[:, 0, :].bitcast(I32), vare[:, :].bitcast(I32), -0.5, SEED,
                                           ALU.mult, ALU.add))
                    for n in range(4):
                        link(dve.tensor_tensor(nt[:, 0, :], rs[:, n % 2, :], rs[:, n % 2, :], ALU.mult))
                        link(dve.tensor_tensor(nt[:, 1, :], nt[:, 0, :], hvar[:, :], ALU.mult))
                        link(dve.scalar_tensor_tensor(out=rs[:, (n + 1) % 2, :], in0=nt[:, 1, :], scalar=1.5,
                                                      in1=rs[:, n % 2, :], op0=ALU.add, op1=ALU.mult))
                    for b in range(B):
                        m = dve.tensor_scalar(dst[:, b, :], ys[:, b, :], mv[:, b, 0:1], rs[:, 0, b:b + 1],
                                              ALU.subtract, ALU.mult)
                    m.then_inc(ln_ready.sem, 1)

                def attention(s):
                    nk = (P, NKEY)[s - 1]

                    def chunk(i):
                        c = i % NCH
                        name = ("S", s, i)
                        written(dve, g, name)
                        if i >= 4:
                            written(dve, g, ("PT", s, i - 4))
                        src = ap(name)[:, 0:HC * nk].rearrange("p (h k) -> p h k", h=HC)
                        if s == 1:
                            dve.tensor_tensor(Pq[:, i % 4, :, :], src, bias1[:, c * HC:(c + 1) * HC, :], ALU.add)\
                               .then_inc(em(name), 1)
                            emptied(dve, g, name)
                            dve.tensor_reduce(mx[:, i % 4, :], Pq[:, i % 4, :, :], AX, ALU.max)\
                               .then_inc(max_ready.sem, 1)
                        else:
                            link(dve.tensor_reduce(mx[:, i % 4, :], src, AX, ALU.max))
                            dve.tensor_tensor(Pq[:, i % 4, :, 0:nk], src, bc(mx[:, i % 4, :], nk), ALU.subtract)\
                               .then_inc(em(name), 1)

                    def normalise(b):
                        name = ("PV", s, b)
                        written(dve, g, name)
                        if b >= 2:
                            written(dve, g, ("y", s, b - 2))
                        src = ap(name)
                        link(dve.reciprocal(rden[:, b % 2, :, :].rearrange("p a t -> p (a t)"), src[P // 2:P, 0:2 * P]))
                        dve.tensor_tensor(oT[0:P // 2, b % 2, :], src[0:P // 2, 0:P], rden[:, b % 2, 0, :], ALU.mult)
                        dve.tensor_tensor(oT[P // 2:P, b % 2, :], src[0:P // 2, P:2 * P], rden[:, b % 2, 1, :],
                                          ALU.mult).then_inc(em(name), 1)

                    def add_residual(b):
                        name = ("y", s, b)
                        written(dve, g, name)
                        if b == 0:
                            if s == 1:
                                dve.wait_ge(inputs_used.sem, inputs_used.at(g, 2))
                            else:
                                dve.wait_ge(xb_ready.sem, xb_ready.at(g, 1))
                        dve.tensor_tensor(ys[:, b, :], ap(name)[:, 0:D], xb[:, b, :], ALU.add).then_inc(em(name), 1)

                    N = B * NCH
                    for i in range(N):
                        chunk(i)
                        if i >= 8 and i % NCH == 0:
                            normalise((i - 8) // NCH)
                        if i >= 10 and (i - 10) % NCH == 0:
                            add_residual((i - 10) // NCH)
                    for b in range(2, B):
                        normalise(b)
                        add_residual(b)
                    emptied(dve, g, ("y", s, B - 1))

                attention(1)
                layer_norm(xs)
                attention(2)
                layer_norm(xs)

                written(dve, g, "gate")
                dve.tensor_copy(gl[:, 0, :, :], ap("gate").rearrange("p (b k) -> p b k", b=B)[:, :, 0:NE])\
                   .then_inc(em("gate"), 1)
                emptied(dve, g, "gate")
                rank = per_batch(rank8[:, :])

                def best(src, m, km, dst):
                    link(dve.tensor_reduce(gm[:, m, :], gl[:, src, :, :], AX, ALU.max))
                    link(dve.tensor_tensor(gl[:, 1, :, :], gl[:, src, :, :], bc(gm[:, m, :], NE), ALU.is_equal))
                    link(dve.tensor_tensor(gl[:, 2, :, :], gl[:, 1, :, :], rank, ALU.mult))
                    link(dve.tensor_reduce(gm[:, km, :], gl[:, 2, :, :], AX, ALU.max))
                    link(dve.tensor_tensor(gl[:, dst, :, :], gl[:, 2, :, :], bc(gm[:, km, :], NE), ALU.is_equal))

                best(0, 0, 1, 3)
                dve.tensor_tensor(gl[:, 7, :, :], gl[:, 0, :, :], bc(gm[:, 0, :], NE), ALU.subtract)\
                   .then_inc(gate_shifted.sem, 1)
                link(dve.scalar_tensor_tensor(out=gl[:, 4, :, :], in0=gl[:, 3, :, :], scalar=-1e30,
                                              in1=gl[:, 0, :, :], op0=ALU.mult, op1=ALU.add))
                best(4, 2, 3, 5)
                link(dve.tensor_tensor(gl[:, 6, :, :], gl[:, 3, :, :], gl[:, 5, :, :], ALU.add))
                dve.wait_ge(gate_exp.sem, gate_exp.at(g, 1))
                link(dve.tensor_tensor(gl[:, 9, :, :], gl[:, 8, :, :], gl[:, 6, :, :], ALU.mult))
                link(dve.tensor_reduce(gm[:, 4, :], gl[:, 9, :, :], AX, ALU.add))
                link(dve.reciprocal(gm[:, 5, :], gm[:, 4, :]))
                link(dve.tensor_tensor(gw[:, :, :], gl[:, 9, :, :], bc(gm[:, 5, :], NE), ALU.mult))

                def table(b):
                    written(dve, g, ("tab", b))
                    f, r = tabf[:, b % 2, :, :], tabr[:, b % 2, :, :]
                    by_head = lambda t: t.rearrange("p s (h e) -> p s h e", e=E)
                    part = lambda n: tab[:, b, n, :, :].rearrange("p h (s e) -> p s h e", e=E)
                    dve.tensor_tensor(f, ap(("tab", b))[0:NKP, :].rearrange("p (s d) -> p s d", s=4),
                                      b5_tab[:, :, :], ALU.add).then_inc(em(("tab", b)), 1)
                    emptied(dve, g, ("tab", b))
                    link(dve.tensor_copy(part(0), by_head(f)))
                    link(dve.tensor_tensor(by_head(r), by_head(f), part(0), ALU.subtract))
                    link(dve.tensor_copy(part(1), by_head(r)))
                    dve.tensor_tensor(part(2), by_head(r), part(1), ALU.subtract).then_inc(tab_ready.sem, 1)

                for e in range(NE):
                    name = ("expert", e)
                    if 1 <= e <= 4:
                        table(e - 1)
                    written(dve, g, name)
                    if e:
                        emptied(dve, g, ("expert", e - 1))
                    for b in range(B):
                        m = dve.scalar_tensor_tensor(out=ys[:, b, :], in0=ap(name)[:, b * P:(b + 1) * P],
                                                     scalar=gw[:, b, e:e + 1], in1=(ys if e else xs)[:, b, :],
                                                     op0=ALU.mult, op1=ALU.add)
                    m.then_inc(em(name), 1)
                emptied(dve, g, ("expert", NE - 1))
                layer_norm(xs)

                for p in range(2):
                    src = ap(("kv4", p)).rearrange("p (b k) -> p b k", b=2)
                    cols = slice(2 * p * P, (2 * p + 2) * P)
                    two = lambda t: t.rearrange("p (b k) -> p b k", b=2)
                    dve.wait_ge(e4_ready.sem, e4_ready.at(g, p + 1))
                    dve.tensor_scalar(two(t4[:, 1, cols]), src[:, :, 0:D], 0.0, None, ALU.max)
                    dve.tensor_copy(v4[:, 2 * p:2 * p + 2, 0:D], src[:, :, D:2 * D]).then_inc(em(("kv4", p)), 1)
                    emptied(dve, g, ("kv4", p))
                    dve.scalar_tensor_tensor(out=k4[:, 2 * p:2 * p + 2, :], in0=two(e4[:, 0, cols]), scalar=1.0,
                                             in1=two(t4[:, 1, cols]), op0=ALU.min, op1=ALU.add)\
                       .then_inc(k4_ready.sem, 1)
                dve.wait_ge(e4_ready.sem, e4_ready.at(g, 3))
                dve.tensor_scalar(t4[:, 0, :], ap("q4T"), 0.0, None, ALU.max).then_inc(em("q4T"), 1)
                emptied(dve, g, "q4T")
                dve.scalar_tensor_tensor(out=qT[:, :], in0=e4[:, 1, :], scalar=1.0, in1=t4[:, 0, :],
                                         op0=ALU.min, op1=ALU.add).then_inc(q4_ready.sem, 1)
                for b in range(B):
                    written(dve, g, ("kvsum", b))
                    dve.tensor_tensor(kv4[:, b, :], ap(("kvsum", b))[:, 0:2 * D],
                                      block4[:, :, :].rearrange("p a d -> p (a d)"), ALU.mult)\
                       .then_inc(em(("kvsum", b)), 1)
                dve.wait_ge(q4_ready.sem, q4_ready.at(g, 1))
                for p in range(2):
                    src = ap(("nd", p))
                    written(dve, g, ("nd", p))
                    link(dve.tensor_scalar(dn4[:, p, 0, :], src[:, 2 * P:4 * P], 1e-8, None, ALU.add))
                    link(dve.reciprocal(dn4[:, p, 1, :], dn4[:, p, 0, :]))
                    dve.tensor_tensor(t4[:, 0, 2 * p * P:(2 * p + 2) * P], src[:, 0:2 * P], dn4[:, p, 1, :],
                                      ALU.mult).then_inc(em(("nd", p)), 1)

                def whole_residual(name, n):
                    written(dve, g, name)
                    dve.wait_ge(xb_ready.sem, xb_ready.at(g, n))
                    dve.tensor_tensor(ys[:, :, :], ap(name).rearrange("p (b d) -> p b d", b=B), xb[:, :, :],
                                      ALU.add).then_inc(em(name), 1)
                    emptied(dve, g, name)

                whole_residual("y4", 2)
                layer_norm(xs)

                dve.tensor_copy(glen[:, 0, :], length[:, bass.ds(g * B, B)])
                link(dve.tensor_copy(glen[:, 1, :], length2[:, bass.ds(g * B, B)]))
                link(dve.reciprocal(glen[:, 2, :], glen[:, 0, :]))
                written(dve, g, "q5")
                heads = lambda t: t.rearrange("p (h e) -> p h e", e=E)
                for b in range(B):
                    m = dve.scalar_tensor_tensor(out=q5[:, :, b, :], in0=heads(ap("q5")[:, b * D:(b + 1) * D]),
                                                 scalar=0.5 * float(E) ** -0.5, in1=heads(b5_qs[:, :]),
                                                 op0=ALU.mult, op1=ALU.add)
                m.then_inc(em("q5"), 1)
                ia, ib, ic, idd = [t[:, :, :] for t in ix]
                L, L2, LR = [bc(glen[:, k, :], HS) for k in range(3)]

                def tt(o, x, y, op):
                    link(dve.tensor_tensor(o, x, y, op))

                def ts(o, x, s1, op1, s2=None, op2=ALU.bypass):
                    link(dve.tensor_scalar(o, x, s1, s2, op1, op2))

                MAGIC = 1.5 * 2.0 ** 23
                written(dve, g, "off")
                dve.tensor_tensor(ia, ap("off").rearrange("p (b k) -> p b k", b=B)[:, :, 0:HS],
                                  per_batch(b5_off[:, :]), ALU.add).then_inc(em("off"), 1)
                emptied(dve, g, "off")
                tt(ib, ia, per_batch(ramp[:, :]), ALU.add)
                ts(ic, ib, token[:, 0:1], ALU.add)
                tt(ia, ic, LR, ALU.mult)
                ts(ib, ia, MAGIC, ALU.add, MAGIC, ALU.subtract)
                tt(idd, ib, ia, ALU.is_gt)
                tt(ib, ib, idd, ALU.subtract)
                tt(idd, ib, L, ALU.mult)
                tt(ia, ic, idd, ALU.subtract)
                tt(ib, ia, L, ALU.mult)
                ts(ib, ib, 0.0, ALU.is_lt)
                tt(ib, ib, L, ALU.mult)
                tt(ia, ia, ib, ALU.add)
                tt(ib, ia, L, ALU.mult)
                tt(ib, ib, L2, ALU.is_ge)
                tt(ib, ib, L, ALU.mult)
                tt(ia, ia, ib, ALU.subtract)
                ts(ia, ia, 1.0 / (NKEY - 1), ALU.mult, 2.0, ALU.mult)
                ts(ia, ia, 1.0, ALU.subtract, 1.0, ALU.add)
                ts(ia, ia, float(NKEY), ALU.mult, 1.0, ALU.subtract)
                ts(ic, ia, 0.5, ALU.mult)
                ts(ia, ic, MAGIC, ALU.add, MAGIC, ALU.subtract)
                tt(ib, ia, ic, ALU.is_gt)
                tt(idd, ia, ib, ALU.subtract)
                tt(w01[:, :, :, 1], ic, idd, ALU.subtract)
                ts(w01[:, :, :, 0], w01[:, :, :, 1], -1.0, ALU.mult, 1.0, ALU.add)
                ts(ia, idd, -2.0, ALU.max, float(NKEY + 1), ALU.min)
                halves = ia.rearrange("p b (s j) -> p b s j", s=2)
                ts(uu[:, :, :, 0:HHS], halves, float(NCTR), ALU.subtract)
                dve.tensor_tensor(uu[:, :, :, HHS:2 * HHS], uu[:, :, :, 0:HHS], uu[:, :, :, 0:HHS], ALU.mult)\
                   .then_inc(uu_ready.sem, 1)

                def find(j):
                    written(dve, g, ("hit", j))
                    dve.tensor_scalar(hit[:, j % NHIT, :], ap(("hit", j))[0:NKP, :], hitbias[:, 0:1], 0.0,
                                      ALU.add, ALU.max).then_inc(em(("hit", j)), 1)

                def weight(h):
                    for p in range(2):
                        k = 2 * h + p
                        name = ("G", h, p)
                        written(dve, g, name)
                        if k >= 4:
                            dve.wait_ge(kvs_ready.sem, kvs_ready.at(g, k - 3))
                        src = ap(name).rearrange("q (t r) -> q t r", t=2)[:, :, 0:NS * 4 * E]\
                            .rearrange("q t (m e) -> q t m e", e=2 * E)
                        w = w01[:, 2 * p:2 * p + 2, h * NS:(h + 1) * NS, :].rearrange("q t n s -> q t (n s)")
                        dve.tensor_tensor(gwt[:, k % 4, :, :, :, :].rearrange("q t n s e -> q t (n s) e"), src,
                                          bc(w, 2 * E), ALU.mult).then_inc(em(name), 1)

                def score(half):
                    dve.wait_ge(kvs_ready.sem, kvs_ready.at(g, (half + 1) * H))
                    kv = kvs[:, :, :, :, :].rearrange("p h b n e -> p (h b) n e")
                    q = q5[:, half * HH:(half + 1) * HH, :, :].rearrange("p h b e -> p (h b) e")
                    link(dve.tensor_tensor(prod5[:, :, :, :], kv[:, :, :, 0:E],
                                           q.unsqueeze(2).broadcast_to([P, HH * B, NS, E]), ALU.mult))
                    link(dve.tensor_reduce(sc5[:, 0, :, :], prod5[:, :, :, :], AX, ALU.add))
                    link(dve.tensor_reduce(sm5[:, 0, :], sc5[:, 0, :, :], AX, ALU.max))
                    dve.tensor_tensor(sc5[:, 1, :, :], sc5[:, 0, :, :], bc(sm5[:, 0, :], NS), ALU.subtract)\
                       .then_inc(s5_shifted.sem, 1)

                def mix(half):
                    dve.wait_ge(s5_exp.sem, s5_exp.at(g, half + 1))
                    link(dve.tensor_reduce(sm5[:, 1, :], sc5[:, 2, :, :], AX, ALU.add))
                    link(dve.reciprocal(sm5[:, 2, :], sm5[:, 1, :]))
                    link(dve.scalar_tensor_tensor(out=sc5[:, 0, :, :], in0=sc5[:, 2, :, :], scalar=0.5,
                                                  in1=bc(sm5[:, 2, :], NS), op0=ALU.mult, op1=ALU.mult))
                    kv = kvs[:, :, :, :, :].rearrange("p h b n e -> p (h b) n e")
                    link(dve.tensor_tensor(prod5[:, :, :, :], kv[:, :, :, E:2 * E], bc(sc5[:, 0, :, :], E), ALU.mult))
                    by_seq = prod5.rearrange("p (h b) n e -> p b h e n", b=B)
                    for b in range(B):
                        m = dve.tensor_reduce(o5[:, b, half * HH * E:(half + 1) * HH * E]
                                              .rearrange("p (h e) -> p h e", e=E), by_seq[:, b], AX, ALU.add)
                    m.then_inc(o5_ready.sem, 1)

                for h in range(H + 1):
                    if h < H:
                        find(h * NS + NS - 1)
                    if h >= 1:
                        weight(h - 1)
                    if h == HH + 1:
                        score(0)
                    if h == HH + 2:
                        mix(0)
                score(1)
                mix(1)
                whole_residual("y5", 3)
                layer_norm(xs)

                for c in range(NF):
                    emptied(dve, g, ("h6", c))
                    dve.tensor_tensor(hT[:, 0, c, :], hT[:, 1, c, :], hT[:, 1, c, :], ALU.mult)\
                       .then_inc(h6_ready.sem, 1)
                y, n, t, s = [lif[:, k, :] for k in range(4)]
                written(dve, g, "y6")
                dve.tensor_copy(y, ap("y6")).then_inc(em("y6"), 1)
                emptied(dve, g, "y6")
                dve.tensor_scalar(n, y, -1.0, None, ALU.mult)
                link(dve.tensor_scalar(s, y, 1.0, None, ALU.is_gt))
                for _ in range(4):
                    link(dve.scalar_tensor_tensor(out=t, in0=n, scalar=-0.9, in1=y, op0=ALU.mult, op1=ALU.add))
                    link(dve.scalar_tensor_tensor(out=n, in0=n, scalar=-1.0, in1=t, op0=ALU.is_lt,
                                                  op1=ALU.subtract))
                    link(dve.scalar_tensor_tensor(out=s, in0=n, scalar=-1.0, in1=s, op0=ALU.is_lt, op1=ALU.add))
                link(dve.scalar_tensor_tensor(out=ys[:, :, :], in0=s.rearrange("p (b d) -> p b d", b=B), scalar=0.2,
                                              in1=xs[:, :, :], op0=ALU.mult, op1=ALU.add))
                dve.wait_ge(stored, g * 16 + 16)
                layer_norm(xout)
                assert links[0] == CHAIN_PER, links


def constants():
    q = np.arange(P, dtype=np.float32)
    start = 2.0 ** (-2.0 ** (-(np.log2(H) - 3)))
    slopes = np.asarray([start * start ** i for i in range(H)], np.float32)
    rel = q[None, :] - q[:, None]
    bias = np.where(rel[:, None, :] <= 0, slopes[None, :, None] * rel[:, None, :], np.float32(-1e30))
    key = np.arange(NKP) - 1 - NCTR
    pick = np.zeros((NKP, HHS, NKP), np.float16)
    for j in range(HHS):
        pick[j, j, :] = 2 * key
        pick[HHS + j, j, :] = -1
    head = np.arange(D) // E
    block = (head[:, None] == head[None, :]).astype(np.float32)
    return {
        "c_ident": np.eye(P, dtype=np.float32),
        "c_bias1": bias.astype(np.float32),
        "c_ramp": np.tile(np.arange(-NS // 2, NS - NS // 2 - 1, dtype=np.float32), (P, H)),
        "c_token": q[:, None].copy(),
        "c_pick": pick,
        "c_hitbias": (1.0 - key.astype(np.float32) ** 2)[:, None].copy(),
        "c_rank8": np.tile(np.arange(NE, 0, -1, dtype=np.float32), (P, 1)),
        "c_block4": np.stack([block, block], 1).copy(),
    }


AS_GIVEN = ["x", "ctx_1024", "mask_BxS2_if0", "L0_attn_W_attn", "L0_attn_b_attn", "L0_attn_W_proj", "L0_attn_b_proj",
            "L0_attn_temperature", "L0_xattn_Wq", "L0_xattn_Wk", "L0_xattn_Wv", "L0_xattn_Wo", "L0_xattn_bo",
            "L0_ffn_gate_w", "L0_ffn_fc_w", "L0_ffn_proj_w", "L1_attn_b_proj", "L1_xattn_bk", "L1_xattn_bv",
            "L1_xattn_bq", "L1_xattn_boff", "L1_xattn_bo"]
TRANSPOSED = {"w4T": "L1_attn_w_qkv", "w4_oT": "L1_attn_w_proj", "w5_kT": "L1_xattn_Wk", "w5_vT": "L1_xattn_Wv",
              "w5_qT": "L1_xattn_Wq", "w5_offT": "L1_xattn_Woff", "w5_oT": "L1_xattn_Wo", "w6_fcT": "L1_ffn_W_fc",
              "w6_projT": "L1_ffn_W_proj"}


def layout(inputs):
    arrays = {name: np.ascontiguousarray(inputs[name]) for name in AS_GIVEN}
    for name, source in TRANSPOSED.items():
        arrays[name] = np.ascontiguousarray(np.transpose(np.asarray(inputs[source])))
    arrays.update(constants())
    return arrays


def kernel(**inputs):
    import concourse.bacc as bacc
    from concourse.bass_utils import run_bass_kernel_spmd

    nc = bacc.Bacc("TRN2", target_bir_lowering=False, num_devices=1)
    arrays, a = {}, {}
    for name, value in layout(inputs).items():
        arrays[f"in_{name}_dram"] = value
        a[name] = nc.dram_tensor(f"in_{name}_dram", value.shape, mybir.dt.from_np(value.dtype),
                                 kind="ExternalInput").ap()
    shape = inputs["x"].shape
    out = nc.dram_tensor("out_dram", shape, F32, kind="ExternalOutput").ap()
    decoder(nc, a, out)
    r = run_bass_kernel_spmd(nc, [arrays], core_ids=[0])
    return r.results[0]["out_dram"]
```

```python
from contextlib import ExitStack

import numpy as np
import concourse.bass as bass
from concourse import mybir

F32 = mybir.dt.float32
F16 = mybir.dt.float16
BF16 = mybir.dt.bfloat16
I32 = mybir.dt.int32
ALU = mybir.AluOpType
ACT = mybir.ActivationFunctionType
AX = mybir.AxisListType.X

P = 128
D = 128
H = 16
E = D // H
NKEY = 77
NKP = 96
B = 4
T = B * P
HC = 4
NCH = H // HC
NE = 8
NF = 4
NS = 5
HS = H * NS
HH = H // 2
HHS = HH * NS
HQ = H // 4
NCTR = 38
EPS = 1e-5
SEED = 1597463007.0
NEWTON = 3
VN = 3
VECTOR_ROW = range(2, H - 1)
CHAIN = (91, 113)


class Signal:

    def __init__(self, sem, per, start=0):
        self.sem, self.per, self.start = sem, per, start

    def at(self, g, n):
        return g[0] * self.per + (g[1] * self.per + n + self.start)


class Banks:

    def __init__(self, written, emptied):
        self.written, self.emptied = written, emptied
        self.turns = [0] * 8
        self.place = {}

    def product(self, name, bank):
        self.place[name] = (bank, self.turns[bank])
        self.turns[bank] += 1

    def bank(self, name):
        return self.place[name][0]


NCHUNK = B * NCH
NATT = NCHUNK + 6
LAST = NATT - 1


def output_of(i):
    return B - 1 if i == LAST else (i - 10) // NCH if i >= 10 and (i - 10) % NCH == 0 and i < LAST - 1 else None


def plan_products(banks):
    for name, bank in (("xT", 0), 0), ("k1T", 1), ("q1T", 2), ("v1", 3), ("cT", 0):
        banks.product(name, bank)
    for s in (1, 2):
        if s == 2:
            for name, bank in ("k2T", 1), ("v2", 3), (("xT", 1), 0), ("q2T", 1):
                banks.product(name, bank)
        for i in range(NATT):
            if i < NCHUNK:
                banks.product(("S", s, i), i % 2)
            if 4 <= i < NCHUNK + 4:
                banks.product(("PT", s, i - 4), 2)
            if output_of(i) is not None:
                banks.product(("y", s, output_of(i)), 2)
        for b in range(B):
            banks.product(("PV", s, b), 3)
    banks.product(("xT", 2), 0)
    banks.product("gate", 3)
    for i in range(NE * NF):
        banks.product(("h", i), 1 + i % 2)
    for b in range(B):
        banks.product(("tab", b), 0)
    for e in range(NE):
        banks.product(("expert", e), 3)
    for name, bank in (("xT", 3), 4), (("kv4", 0), 6), (("kv4", 1), 7), ("q4T", 5), (("kvsum", 0), 4), \
            (("kvsum", 1), 5), (("nd", 0), 6), (("nd", 1), 7), ("y4", 4), (("xT", 4), 5), ("q5T", 6), ("q5", 7), \
            ("off", 4), (("uT", 0), 5), (("uT", 1), 6):
        banks.product(name, bank)
    for j in range(HS):
        banks.product(("hit", j), 4 + j % 2)
    for h in range(H):
        for p in range(2):
            banks.product(("G", h, p), 6 + p)
    for name, bank in ("c5T", 4), ("y5", 5), (("xT", 5), 6), (("h6", 0), 7), (("h6", 1), 4), (("h6", 2), 5), \
            (("h6", 3), 6), ("y6", 7):
        banks.product(name, bank)


def schedule():
    after = {
        ("a1", 1): ["xT3"], ("a1", 2): ["kv4"], ("a1", 3): ["elu"], ("a1", 4): ["kvsum"], ("a1", 5): ["kvmask"],
        ("a1", 6): ["nd", ("ratio", 0)], ("a1", 7): [("ratio", 1)], ("a1", 8): ["y4"], ("a1", 9): ["norm4"],
        ("a1", 11): ["xT4"], ("a1", 12): ["q5", "off"], ("a1", 13): ["scale5", ("place", 0)], ("a1", 14): [("place", 1)],
        ("a1", 15): [("place", 2)], ("a1", 17): [("place", 3)], ("a1", 19): ["uT"],
        ("a1", LAST): [("head", 0), ("head", 1)],
        ("a2", 17): [("head", 13), ("score", 2)], ("a2", 18): [("mix", 2)],
        ("a2", 19): [("head", 14)], ("a2", 20): [("head", 15)], ("a2", LAST): [("head", 16)], "gates": [("score", 3)],
        ("m", 1): [("mix", 3)], ("m", 3): ["c5T"], ("m", 4): ["y5", "norm5"],
        ("m", 6): ["xT5"], ("m", 7): ["h6"], ("m", 8): ["square", "y6"],
        ("m", 9): [("spikes", 0)], ("m", 10): [("spikes", 1), ("spikes", 2)],
        ("m", 11): [("spikes", 3)], ("m", 12): [("spikes", 4)], ("m", 13): ["out"],
    }
    for h in range(2, 13):
        after.setdefault(("a2", (h - 2) * 3 // 2 + 1), []).append(("head", h))
    for q in range(2):
        at = (4 * q + 3) * 3 // 2 + 2
        after.setdefault(("a2", at), []).append(("score", q))
        after.setdefault(("a2", at + 1), []).append(("mix", q))
    tables = {("m", m): ("tab", b) for b, m in enumerate((2, 6, 8, 11))}
    steps = ["load", "prep1"] + [("a1", i) for i in range(NATT)] + ["prep2"] + [("a2", i) for i in range(NATT)]
    steps += ["gates"]
    shares = {("m", 0): "gate_exp", ("m", 1): "gate_shares"}
    for i in range(2 * NE + 2):
        steps += [("m", i)] + [t["m", i] for t in (tables, shares) if ("m", i) in t]
    steps += ["end"]
    order = []
    for x in steps:
        order.append(("x", x))
        order += [("y", y) for y in after.get(x, [])]
    return order


ORDER = schedule()


def decoder(nc, a, out):
    NB = a["x"].shape[0]
    G = NB // B
    with ExitStack() as ctx:
        def sb(name, shape, dt=F32):
            return ctx.enter_context(nc.sbuf_tensor(name, shape, dt))

        def sem(name):
            return ctx.enter_context(nc.semaphore(name))

        def signal(name, per, start=0):
            return Signal(sem(name), per, start)

        ps = ctx.enter_context(nc.psum_tensor("ps", [P, 8, 512], F32))
        banks = Banks([sem(f"bank{k}_written") for k in range(8)], [sem(f"bank{k}_emptied") for k in range(8)])
        plan_products(banks)

        def turn(g, name, n):
            k, before = banks.place[name]
            return g[0] * banks.turns[k] + (g[1] * banks.turns[k] + before + n)

        def bank_free(g, name):
            return turn(g, name, 1)

        def product_done(g, name):
            return turn(g, name, 1)

        def product_read(g, name):
            return turn(g, name, 2)

        def wr(name):
            return banks.written[banks.bank(name)]

        def em(name):
            return banks.emptied[banks.bank(name)]

        def ap(name):
            return ps[:, banks.bank(name), :]

        def run(eng, first, second):
            def both(gx, gy):
                for half, step in ORDER:
                    if half == "x" and gx is not None:
                        first(gx, step)
                    if half == "y" and gy is not None:
                        second(gy, step)

            both((0, 0), None)
            if G > 1:
                with eng.Fori(0, G - 1, 1) as i:
                    both((i, 1), (i, 0))
            both(None, (0, G - 1))

        ident = sb("ident", [P, P])
        w1_qkv = sb("w1_qkv", [D, 3 * D])
        w1_o = sb("w1_o", [D, D])
        w2_q = sb("w2_q", [D, D])
        w2_k = sb("w2_k", [D, D])
        w2_v = sb("w2_v", [D, D])
        w2_o = sb("w2_o", [D, D])
        w3_gate = sb("w3_gate", [D, P])
        w3_fc = sb("w3_fc", [D, NE, NF * P])
        w3_proj = sb("w3_proj", [P, NE, NF, D])
        w4_q = sb("w4_q", [D, D])
        w4_kv = sb("w4_kv", [D, 2 * D])
        w4_o = sb("w4_o", [D, D])
        w5_kv = sb("w5_kv", [D, 2 * D])
        w5_q = sb("w5_q", [D, D])
        w5_off = sb("w5_off", [D, P])
        w5_o = sb("w5_o", [D, D])
        w6_fc = sb("w6_fc", [D, NF * P])
        w6_proj = sb("w6_proj", [P, NF, D])
        bias1 = sb("bias1", [P, H, P])
        b1_qk = sb("b1_qk", [D, 2])
        b1_v = sb("b1_v", [P, D])
        b1_o = sb("b1_o", [P, D])
        b2_o = sb("b2_o", [P, D])
        b4_o = sb("b4_o", [P, D])
        b5_qcol = sb("b5_qcol", [D, 1])
        b5_q = sb("b5_q", [P, D])
        b5_off = sb("b5_off", [P, HS])
        b5_o = sb("b5_o", [P, D])
        b5_tab = sb("b5_tab", [NKP, 2 * D])
        iskey = sb("iskey", [NKP, 2])
        temp = sb("temp", [P, 1])
        qscale1 = sb("qscale1", [P, 1])
        qbias1 = sb("qbias1", [P, 1])
        ramp = sb("ramp", [P, HS])
        token = sb("token", [P, 1])
        zero64 = sb("zero64", [P, HH * E])
        glen = sb("glen", [P, 3, B])
        pick = sb("pick", [NKP, HHS, NKP], F16)
        hitbias = sb("hitbias", [NKP, 1])
        rank8 = sb("rank8", [P, NE])
        headmask = sb("headmask", [P, H])
        block4 = sb("block4", [P, 2, D])
        masked = sb("masked", [P, NB])
        length = sb("length", [P, NB])
        length2 = sb("length2", [P, NB])

        xin = sb("xin", [P, B, D])
        ctxin = sb("ctxin", [NKEY, B, D])
        xs = sb("xs", [P, B, D])
        xb = sb("xb", [P, B, D])
        ys = xb
        xT = sb("xT", [D, T])
        cT = sb("cT", [D, B, P])
        qT = sb("qT", [D, T])
        kT = sb("kT", [D, T])
        v = sb("v", [P, B, D])
        KM = sb("KM", [D, 4, HC, P])
        VM = sb("VM", [P, 2, 2, HH * P])
        Pq = sb("Pq", [P, 4, HC, P])
        mx = sb("mx", [P, 4, HC])
        PT = [sb("pt1", [P, 2, HC * P]), sb("pt2", [NKP, 2, HC * P])]
        rden = sb("rden", [P // 2, 2, P])
        oT = sb("oT", [D, 2, P])
        gl = Pq[:, 0, :, :].rearrange("p h k -> p (h k)")[:, 0:10 * B * NE]\
            .rearrange("p (s b e) -> p s b e", s=10, b=B)
        gm = sb("gm", [P, 6, B])
        gw = sb("gw", [P, B, NE])
        hT = sb("hT", [P, 2, NF, T])
        mask_i = hT[:, :, :, :].rearrange("p a c t -> p (a c t)")[:, 0:NB * NKEY].bitcast(I32)\
            .rearrange("p (b k) -> p b k", b=NB)

        stats = sb("stats", [P, B, 6])
        mv = sb("mv", [P, B, 2])
        pause = sb("pause", [P, 1])
        vare = sb("vare", [P, B])
        hvar = sb("hvar", [P, B])
        rs = sb("rs", [P, 2, B])
        nt = sb("nt", [P, 2, B])

        xs2 = sb("xs2", [P, B, D])
        xb2 = sb("xb2", [P, B, D])
        ys2 = xb2
        xT2 = sb("xT2", [D, T])
        qT2 = sb("qT2", [D, T])
        v4 = sb("v4", [P, B, 2 * D])
        tab = sb("tab", [NKP, B, 3, H, 4 * E], BF16)
        q5 = sb("q5", [P, H, B, E])
        w01 = sb("w01", [P, B, HS, 2])
        uT = sb("uT", [NKP, 2, T], F16)
        NHIT = 2 * NS
        hit = sb("hit", [NKP, NHIT, T], BF16)
        o5 = sb("o5", [P, B, D])
        RING = HH * B * NS * 2 * E
        scratch = sb("scratch", [P, RING + 2208])

        def area(at, shape):
            n = int(np.prod(shape))
            names = "abcdef"[:len(shape)]
            t = scratch[:, at:at + n]
            if len(shape) == 1:
                return t
            return t.rearrange(f"p ({' '.join(names)}) -> p {' '.join(names)}", **dict(zip(names, shape)))

        e4, t4, k4 = area(0, [2, T]), area(2 * T, [2, T]), area(4 * T, [B, D])
        kv4, dn4 = area(5 * T, [B, 2 * D]), area(7 * T, [2, 2, 2 * P])
        ix = [area(n * B * HS, [B, HS]) for n in range(4)]
        tabf, tabr = [Pq[0:NKP, k, :, :] for k in (1, 2)]
        uu = area(4 * B * HS, [B, 2, 2 * HHS])
        kvs = area(0, [HH, B, NS, 2 * E])
        gwt = area(RING, [4, 2, NS, 2, 2 * E])
        prod5 = area(RING + 1280, [HQ * B, NS, E])
        sc5 = area(RING + 1920, [3, HQ * B, NS])
        sm5 = area(RING + 2160, [3, HQ * B])
        h6 = area(0, [NF, T])
        lif = area(NF * T, [4, T])
        c5T = qT2

        w_loaded = sem("weights_loaded")
        zeroed = sem("constants_zeroed")
        prepared = sem("constants_prepared")
        x_loaded = signal("x_loaded", 16)
        c_loaded = signal("context_loaded", 16)
        km_ready = signal("masked_keys_ready", 2 * NCHUNK)
        vm_ready = signal("masked_values_ready", 2 * B)
        max_ready = signal("row_maxima_ready", NCHUNK)
        shifted = signal("scores_shifted", NCHUNK)
        probs = signal("probabilities_ready", 2 * NCHUNK)
        inputs_used = signal("inputs_used", 1, 1)
        xb_ready = signal("residual_ready", 1)
        xb2_ready = signal("residual2_ready", 2)
        ln_ready = signal("layer_norm_ready", 3, 1)
        ln2_ready = signal("layer_norm2_ready", 3)
        gate_shifted = signal("gates_shifted", 1)
        gate_exp = signal("gates_exponentiated", 1)
        tab_ready = signal("tables_ready", B)
        q4_ready = signal("linear_q_ready", 1)
        k4_ready = signal("linear_k_ready", 2)
        uu_ready = signal("samples_ready", 1)
        kvs_ready = signal("sampled_keys_values_ready", 2 * H)
        s5_shifted = signal("sample_scores_shifted", 4)
        s5_exp = signal("sample_scores_exponentiated", 4)
        o5_ready = signal("sampled_output_ready", 4)
        h6_ready = signal("spiking_hidden_ready", NF)
        stored = signal("output_stored", 32, 32)

        NLOAD = [0]
        NZ = 10
        NPREP = 7
        chain = {"x": signal("vector_chain", CHAIN[0]), "y": signal("vector_chain2", CHAIN[1])}

        block = ctx.enter_context(nc.Block())

        @block.sync
        def _(sp):
            def load(dst, src):
                sp.dma_start(dst, src).then_inc(w_loaded, 16)
                NLOAD[0] += 1

            load(ident[:, :], a["c_ident"])
            load(w1_qkv[:, :], a["L0_attn_W_attn"])
            load(w1_o[:, :], a["L0_attn_W_proj"])
            load(w2_q[:, :], a["L0_xattn_Wq"])
            load(w2_k[:, :], a["L0_xattn_Wk"])
            load(w2_v[:, :], a["L0_xattn_Wv"])
            load(w2_o[:, :], a["L0_xattn_Wo"])
            for t in range(2):
                load(b1_qk[:, t:t + 1], a["L0_attn_b_attn"][t * D:(t + 1) * D].rearrange("(p a) -> p a", a=1))
            load(b1_v[:, :], a["L0_attn_b_attn"][2 * D:3 * D].rearrange("(a d) -> a d", a=1).broadcast_to([P, D]))
            for dst, name in (b1_o, "L0_attn_b_proj"), (b2_o, "L0_xattn_bo"), (b4_o, "L1_attn_b_proj"), \
                    (b5_q, "L1_xattn_bq"), (b5_off, "L1_xattn_boff"), (b5_o, "L1_xattn_bo"):
                n = dst.shape[1]
                load(dst[:, :], a[name].rearrange("(a d) -> a d", a=1).broadcast_to([P, n]))
            load(temp[:, :], a["L0_attn_temperature"].rearrange("(a d) -> a d", a=1).broadcast_to([P, 1]))
            load(bias1[:, :, :], a["c_bias1"])
            load(w4_q[:, :], a["w4T"][:, 0:D])
            load(w4_kv[:, :], a["w4T"][:, D:3 * D])
            load(w4_o[:, :], a["w4_oT"])
            load(w5_kv[:, 0:D], a["w5_kT"])
            load(w5_kv[:, D:2 * D], a["w5_vT"])
            load(w5_q[:, :], a["w5_qT"])
            load(w5_o[:, :], a["w5_oT"])
            load(b5_qcol[:, :], a["L1_xattn_bq"].rearrange("(p a) -> p a", a=1))
            load(w6_fc[:, :], a["w6_fcT"])
            load(w6_proj[:, :, :], a["w6_projT"].rearrange("(c p) d -> p c d", p=P))
            load(ramp[:, :], a["c_ramp"])
            load(token[:, :], a["c_token"])
            load(pick[:, :, :], a["c_pick"])
            load(hitbias[:, :], a["c_hitbias"])
            load(rank8[:, :], a["c_rank8"])
            load(block4[:, :, :], a["c_block4"])
            load(headmask[:, :], a["c_headmask"])
            load(mask_i, a["mask_BxS2_if0"].rearrange("(a b) k -> a b k", a=1).broadcast_to([P, NB, NKEY]))
            load(w3_fc[:, :, :], a["L0_ffn_fc_w"].rearrange("e d f -> d e f"))
            load(w3_proj[:, :, :, :], a["L0_ffn_proj_w"].rearrange("e (c p) d -> p e c d", p=P))
            sp.wait_ge(zeroed, NZ)
            load(w3_gate[:, 0:NE], a["L0_ffn_gate_w"])
            load(w5_off[:, 0:HS], a["w5_offT"])
            for t, name in enumerate(("L1_xattn_bk", "L1_xattn_bv")):
                load(b5_tab[:, t * D:(t + 1) * D], a[name].rearrange("(a d) -> a d", a=1).broadcast_to([NKP, D]))
            load(iskey[:, :], a["c_iskey"])

            def group(t, g, rows, b=0, n=B):
                at = g[0] * (B * rows * D) + (g[1] * B + b) * (rows * D)
                return bass.AP(t.tensor, at, [[D, rows], [rows * D, n], [1, D]])

            def first(g, step):
                if step == "load":
                    src_x, src_c = group(a["x"], g, P), group(a["ctx_1024"], g, NKEY)
                    sp.wait_ge(inputs_used.sem, inputs_used.at(g, 0))
                    sp.dma_start(xin[:, :, :], src_x).then_inc(x_loaded.sem, 16)
                    sp.dma_start(ctxin[:, :, :], src_c).then_inc(c_loaded.sem, 16)

            def second(g, step):
                if step == "out":
                    sp.wait_ge(ln2_ready.sem, ln2_ready.at(g, 3))
                    for b in (B // 2, 0):
                        sp.dma_start(group(out, g, P, b, B // 2), xs2[:, b:b + B // 2, :]).then_inc(stored.sem, 16)

            run(sp, first, second)
            sp.wait_ge(stored.sem, stored.at((0, G - 1), 32))

        @block.tensor
        def _(pe):
            def mm(o, lhsT, rhs, start=True, stop=True):
                return pe.matmul(o, lhsT, rhs, start=start, stop=stop)

            def transpose_x(g, s, src):
                pe.wait_ge(em(("xT", s)), bank_free(g, ("xT", s)))
                for b in range(B):
                    m = pe.transpose(ap(("xT", s))[:, b * P:(b + 1) * P], src[:, b, :], ident[:, :])
                m.then_inc(wr(("xT", s)), 1)

            def project(g, name, w, x):
                pe.wait_ge(em(name), bank_free(g, name))
                mm(ap(name)[:, 0:x.shape[-1] if len(x.shape) == 2 else x.shape[1] * x.shape[2]], w, x)\
                    .then_inc(wr(name), 1)

            def project_rows(g, name, w, x, n, m=P):
                pe.wait_ge(em(name), bank_free(g, name))
                for b in range(B):
                    last = mm(ap(name)[0:m, b * P:b * P + n], x(b), w)
                last.then_inc(wr(name), 1)

            def cols(t):
                return lambda b: t[:, b * P:(b + 1) * P]

            def attention(g, s, i):
                nk = (P, NKEY)[s - 1]
                rows = (P, NKP)[s - 1]
                if i < NCHUNK:
                    b = i // NCH
                    pe.wait_ge(km_ready.sem, km_ready.at(g, (s - 1) * NCHUNK + i + 1))
                    pe.wait_ge(em(("S", s, i)), bank_free(g, ("S", s, i)))
                    mm(ap(("S", s, i))[:, 0:HC * nk], qT[:, b * P:(b + 1) * P], KM[:, i % 4, :, 0:nk])\
                        .then_inc(wr(("S", s, i)), 1)
                if 4 <= i < NCHUNK + 4:
                    k = i - 4
                    pe.wait_ge(probs.sem, probs.at(g, (s - 1) * NCHUNK + k + 1))
                    pe.wait_ge(em(("PT", s, k)), bank_free(g, ("PT", s, k)))
                    for n in range(HC):
                        m = pe.transpose(ap(("PT", s, k))[0:nk, n * P:(n + 1) * P], Pq[:, k % 4, n, 0:nk],
                                         ident[:, :])
                    m.then_inc(wr(("PT", s, k)), 1)
                if 5 <= i < NCHUNK + 5:
                    b, c = divmod(i - 5, NCH)
                    name = ("PV", s, b)
                    if c == 0:
                        pe.wait_ge(vm_ready.sem, vm_ready.at(g, (s - 1) * B + b + 1))
                        pe.wait_ge(em(name), bank_free(g, name))
                    pe.wait_ge(em(("PT", s, i - 5)), product_read(g, ("PT", s, i - 5)))
                    for n in range(HC):
                        half, r = divmod(c * HC + n, HH)
                        m = mm(ap(name)[:, half * P:(half + 1) * P], VM[0:rows, b % 2, half, r * P:(r + 1) * P],
                               PT[s - 1][0:rows, (i - 5) % 2, n * P:(n + 1) * P], start=(r == 0), stop=(r == HH - 1))
                    if c == NCH - 1:
                        m.then_inc(wr(name), 1)
                b = output_of(i)
                if b is not None:
                    pe.wait_ge(em(("PV", s, b)), product_read(g, ("PV", s, b)))
                    pe.wait_ge(em(("y", s, b)), bank_free(g, ("y", s, b)))
                    mm(ap(("y", s, b))[:, 0:D], oT[:, b % 2, :], (w1_o, w2_o)[s - 1][:, :])\
                        .then_inc(wr(("y", s, b)), 1)

            def first(g, step):
                if step == "prep1":
                    pe.wait_ge(x_loaded.sem, x_loaded.at(g, 16))
                    transpose_x(g, 0, xin)
                    pe.wait_ge(em(("xT", 0)), product_read(g, ("xT", 0)))
                    project(g, "k1T", w1_qkv[:, D:2 * D], xT[:, :])
                    project(g, "q1T", w1_qkv[:, 0:D], xT[:, :])
                    project_rows(g, "v1", w1_qkv[:, 2 * D:3 * D], cols(xT), D)
                    pe.wait_ge(c_loaded.sem, c_loaded.at(g, 16))
                    pe.wait_ge(em("cT"), bank_free(g, "cT"))
                    for b in range(B):
                        m = pe.transpose(ap("cT")[:, b * P:b * P + NKEY], ctxin[:, b, :], ident[0:NKEY, 0:NKEY])
                    m.then_inc(wr("cT"), 1)
                elif step == "prep2":
                    project(g, "k2T", w2_k[:, :], cT[:, :, 1:1 + NKEY])
                    project_rows(g, "v2", w2_v[:, :], lambda b: cT[:, b, 1:1 + NKP], D, NKP)
                    pe.wait_ge(ln_ready.sem, ln_ready.at(g, 1))
                    transpose_x(g, 1, xs)
                    pe.wait_ge(em(("xT", 1)), product_read(g, ("xT", 1)))
                    project(g, "q2T", w2_q[:, :], xT[:, :])
                    pe.wait_ge(em("q2T"), product_read(g, "q2T"))
                elif step == "gates":
                    pe.wait_ge(ln_ready.sem, ln_ready.at(g, 2))
                    transpose_x(g, 2, xs)
                    pe.wait_ge(em(("xT", 2)), product_read(g, ("xT", 2)))
                    project_rows(g, "gate", w3_gate[:, :], cols(xT), P)
                elif step[0] in ("a1", "a2"):
                    if step == ("a1", 0):
                        pe.wait_ge(em("q1T"), product_read(g, "q1T"))
                    attention(g, 1 if step[0] == "a1" else 2, step[1])
                elif step[0] == "tab":
                    b = step[1]
                    pe.wait_ge(em(("tab", b)), bank_free(g, ("tab", b)))
                    for s in range(2):
                        m = mm(ap(("tab", b))[0:NKP, s * 2 * D:(s + 1) * 2 * D], cT[:, b, s:s + NKP], w5_kv[:, :])
                    m.then_inc(wr(("tab", b)), 1)
                elif step[0] == "m" and step[1] % 2 == 0 and step[1] < 2 * NE:
                    e = step[1] // 2
                    for c in range(NF):
                        name = ("h", e * NF + c)
                        pe.wait_ge(em(name), bank_free(g, name))
                        mm(ap(name), w3_fc[:, e, c * P:(c + 1) * P], xT[:, :]).then_inc(wr(name), 1)
                elif step[0] == "m" and step[1] % 2 == 1 and step[1] >= 3:
                    e = step[1] // 2 - 1
                    pe.wait_ge(em(("expert", e)), bank_free(g, ("expert", e)))
                    hidden = ("h", e * NF + NF - 1)
                    pe.wait_ge(em(hidden), product_read(g, hidden))
                    for b in range(B):
                        for c in range(NF):
                            m = mm(ap(("expert", e))[:, b * P:(b + 1) * P], hT[:, e % 2, c, b * P:(b + 1) * P],
                                   w3_proj[:, e, c, :], start=(c == 0), stop=(c == NF - 1))
                    m.then_inc(wr(("expert", e)), 1)

            def spread(g, j):
                pe.wait_ge(em(("hit", j)), bank_free(g, ("hit", j)))
                mm(ap(("hit", j))[0:NKP, :], pick[:, j % HHS, :], uT[:, j // HHS, :]).then_inc(wr(("hit", j)), 1)

            def gather(g, h, p, n):
                j = h * NS + n
                name = ("G", h, p)
                pe.wait_ge(em(("hit", j)), product_read(g, ("hit", j)))
                if n == 0:
                    pe.wait_ge(em(name), bank_free(g, name))
                for t in range(2):
                    b = 2 * p + t
                    o = t * 256 + n * 4 * E
                    for part in range(3):
                        m = mm(ap(name)[:, o:o + 4 * E], hit[:, j % NHIT, b * P:(b + 1) * P],
                               tab[:, b, part, h, :], start=(part == 0), stop=(part == 2))
                if n == NS - 1:
                    m.then_inc(wr(name), 1)

            def second(g, step):
                if step == "xT3":
                    pe.wait_ge(ln_ready.sem, ln_ready.at(g, 3))
                    transpose_x(g, 3, xs2)
                elif step == "kv4":
                    pe.wait_ge(em(("xT", 3)), product_read(g, ("xT", 3)))
                    for p in range(2):
                        pe.wait_ge(em(("kv4", p)), bank_free(g, ("kv4", p)))
                        for j in range(2):
                            m = mm(ap(("kv4", p))[:, j * 2 * D:(j + 1) * 2 * D], cols(xT2)(2 * p + j), w4_kv[:, :])
                        m.then_inc(wr(("kv4", p)), 1)
                    project(g, "q4T", w4_q[:, :], xT2[:, :])
                elif step == "kvsum":
                    for p in range(2):
                        pe.wait_ge(k4_ready.sem, k4_ready.at(g, p + 1))
                        pe.wait_ge(em(("kvsum", p)), bank_free(g, ("kvsum", p)))
                        for j in range(2):
                            b = 2 * p + j
                            m = mm(ap(("kvsum", p))[:, j * 2 * D:(j + 1) * 2 * D], k4[:, b, :], v4[:, b, :])
                        m.then_inc(wr(("kvsum", p)), 1)
                elif step == "nd":
                    pe.wait_ge(q4_ready.sem, q4_ready.at(g, 1))
                    for p in range(2):
                        pe.wait_ge(em(("kvsum", p)), product_read(g, ("kvsum", p)))
                        pe.wait_ge(em(("nd", p)), bank_free(g, ("nd", p)))
                        for j in range(2):
                            b = 2 * p + j
                            for t in range(2):
                                m = mm(ap(("nd", p))[:, (2 * t + j) * P:(2 * t + j + 1) * P],
                                       kv4[:, b, t * D:(t + 1) * D], cols(qT2)(b))
                        m.then_inc(wr(("nd", p)), 1)
                elif step == "y4":
                    pe.wait_ge(em(("nd", 0)), product_read(g, ("nd", 0)))
                    pe.wait_ge(em(("nd", 1)), product_read(g, ("nd", 1)))
                    project_rows(g, "y4", w4_o[:, :], cols(t4[:, 0, :]), D)
                elif step == "xT4":
                    pe.wait_ge(ln2_ready.sem, ln2_ready.at(g, 1))
                    transpose_x(g, 4, xs2)
                elif step == "q5":
                    pe.wait_ge(em(("xT", 4)), product_read(g, ("xT", 4)))
                    project(g, "q5T", w5_q[:, :], xT2[:, :])
                    project_rows(g, "q5", w5_q[:, :], cols(xT2), D)
                elif step == "off":
                    pe.wait_ge(em("q5T"), product_read(g, "q5T"))
                    project_rows(g, "off", w5_off[:, :], cols(qT2), P)
                elif step == "uT":
                    pe.wait_ge(uu_ready.sem, uu_ready.at(g, 1))
                    for half in range(2):
                        pe.wait_ge(em(("uT", half)), bank_free(g, ("uT", half)))
                        for b in range(B):
                            m = pe.transpose(ap(("uT", half))[0:2 * HHS, b * P:(b + 1) * P], uu[:, b, half, :], ident[:, :])
                        m.then_inc(wr(("uT", half)), 1)
                elif step[0] == "head":
                    h = step[1]
                    if h == 0:
                        pe.wait_ge(tab_ready.sem, tab_ready.at(g, B))
                        pe.wait_ge(em(("uT", 0)), product_read(g, ("uT", 0)))
                        pe.wait_ge(em(("uT", 1)), product_read(g, ("uT", 1)))
                    work = [(p, n) for p in range(2) for n in range(NS)]
                    for n in range(NS):
                        if h < H:
                            spread(g, h * NS + n)
                        if 1 <= h <= H:
                            gather(g, h - 1, *work[2 * n])
                            gather(g, h - 1, *work[2 * n + 1])
                elif step == "c5T":
                    pe.wait_ge(o5_ready.sem, o5_ready.at(g, 4))
                    pe.wait_ge(em("c5T"), bank_free(g, "c5T"))
                    for b in range(B):
                        m = pe.transpose(ap("c5T")[:, b * P:(b + 1) * P], o5[:, b, :], ident[:, :])
                    m.then_inc(wr("c5T"), 1)
                elif step == "y5":
                    pe.wait_ge(em("c5T"), product_read(g, "c5T"))
                    project_rows(g, "y5", w5_o[:, :], cols(c5T), D)
                elif step == "xT5":
                    pe.wait_ge(ln2_ready.sem, ln2_ready.at(g, 2))
                    transpose_x(g, 5, xs2)
                elif step == "h6":
                    pe.wait_ge(em(("xT", 5)), product_read(g, ("xT", 5)))
                    for c in range(NF):
                        project(g, ("h6", c), w6_fc[:, c * P:(c + 1) * P], xT2[:, :])
                elif step == "y6":
                    pe.wait_ge(h6_ready.sem, h6_ready.at(g, NF))
                    pe.wait_ge(em("y6"), bank_free(g, "y6"))
                    for b in range(B):
                        for c in range(NF):
                            m = mm(ap("y6")[:, b * P:(b + 1) * P], h6[:, c, b * P:(b + 1) * P], w6_proj[:, c, :],
                                   start=(c == 0), stop=(c == NF - 1))
                    m.then_inc(wr("y6"), 1)

            pe.wait_ge(w_loaded, 16 * NLOAD[0])
            pe.wait_ge(zeroed, NZ)
            pe.wait_ge(prepared, NPREP)
            run(pe, first, second)

        @block.scalar
        def _(act):
            def take(g, name, dst, src=None):
                act.wait_ge(wr(name), product_done(g, name))
                act.copy(dst, ap(name) if src is None else src).then_inc(em(name), 1)

            def attention(g, s, i):
                nk = (P, NKEY)[s - 1]
                if 2 <= i < NCHUNK + 2:
                    k = i - 2
                    if s == 1:
                        act.wait_ge(shifted.sem, shifted.at(g, k + 1))
                    else:
                        act.wait_ge(em(("S", s, k)), product_read(g, ("S", s, k)))
                    act.activation(Pq[:, k % 4, :, 0:nk], Pq[:, k % 4, :, 0:nk], ACT.Exp).then_inc(probs.sem, 1)
                if 4 <= i < NCHUNK + 4:
                    k = i - 4
                    take(g, ("PT", s, k), PT[s - 1][0:nk, k % 2, :], ap(("PT", s, k))[0:nk, :])

            def first(g, step):
                if step == "prep1":
                    take(g, ("xT", 0), xT[:, :])
                    act.wait_ge(wr("k1T"), product_done(g, "k1T"))
                    act.activation(kT[:, :], ap("k1T"), ACT.Identity, bias=b1_qk[:, 1:2]).then_inc(em("k1T"), 1)
                    act.wait_ge(wr("q1T"), product_done(g, "q1T"))
                    act.activation(qT[:, :], ap("q1T"), ACT.Identity, bias=qbias1[:, :], scale=qscale1[:, :])\
                        .then_inc(em("q1T"), 1)
                    take(g, "v1", v[:, :, :])
                    take(g, "cT", cT[:, :, 1:1 + NKEY], ap("cT").rearrange("p (b k) -> p b k", b=B)[:, :, 0:NKEY])
                elif step == "prep2":
                    take(g, "k2T", kT[:, 0:B * NKEY], ap("k2T")[:, 0:B * NKEY])
                    take(g, "v2", v[0:NKP, :, :], ap("v2")[0:NKP, :])
                    take(g, ("xT", 1), xT[:, :])
                    act.wait_ge(wr("q2T"), product_done(g, "q2T"))
                    act.activation(qT[:, :], ap("q2T"), ACT.Copy, scale=float(E) ** -0.5).then_inc(em("q2T"), 1)
                elif step == "gates":
                    take(g, ("xT", 2), xT[:, :])
                elif step == "gate_exp":
                    act.wait_ge(gate_shifted.sem, gate_shifted.at(g, 1))
                    act.activation(gl[:, 8, :, :], gl[:, 7, :, :], ACT.Exp).then_inc(gate_exp.sem, 1)
                elif step[0] in ("a1", "a2"):
                    attention(g, 1 if step[0] == "a1" else 2, step[1])
                elif step[0] == "m" and step[1] % 2 == 0 and step[1] < 2 * NE:
                    e = step[1] // 2
                    for c in range(NF):
                        name = ("h", e * NF + c)
                        act.wait_ge(wr(name), product_done(g, name))
                        act.activation(hT[:, e % 2, c, :], ap(name), ACT.Gelu).then_inc(em(name), 1)

            def second(g, step):
                if step in ("xT3", "xT4", "xT5"):
                    take(g, ("xT", int(step[2])), xT2[:, :])
                elif step == "kv4":
                    for p in range(2):
                        at = slice(p * 2 * P, (p + 1) * 2 * P)
                        src = ap(("kv4", p)).rearrange("p (b k) -> p b k", b=2)
                        act.wait_ge(wr(("kv4", p)), product_done(g, ("kv4", p)))
                        for dst, fn in (e4[:, 0, at], ACT.Exp), (t4[:, 1, at], ACT.Relu):
                            act.activation(dst.rearrange("p (b k) -> p b k", b=2), src[:, :, 0:D], fn)
                        act.copy(v4[:, 2 * p:2 * p + 2, 0:D], src[:, :, D:2 * D]).then_inc(em(("kv4", p)), 1)
                    act.wait_ge(wr("q4T"), product_done(g, "q4T"))
                    act.activation(e4[:, 1, :], ap("q4T"), ACT.Exp)
                    act.activation(t4[:, 0, :], ap("q4T"), ACT.Relu).then_inc(em("q4T"), 1)
                elif step == "q5":
                    act.wait_ge(wr("q5T"), product_done(g, "q5T"))
                    act.activation(qT2[:, :], ap("q5T"), ACT.Identity, bias=b5_qcol[:, :]).then_inc(em("q5T"), 1)
                elif step == "uT":
                    for half in range(2):
                        take(g, ("uT", half), uT[0:2 * HHS, half, :], ap(("uT", half))[0:2 * HHS, :])
                elif step[0] == "head":
                    h = step[1]
                    for n in range(NS):
                        j = h * NS + n
                        if h < H and not (n == VN and h in VECTOR_ROW):
                            act.wait_ge(wr(("hit", j)), product_done(g, ("hit", j)))
                            act.activation(hit[:, j % NHIT, :], ap(("hit", j))[0:NKP, :], ACT.Relu,
                                           bias=hitbias[:, :]).then_inc(em(("hit", j)), 1)
                elif step[0] == "mix":
                    act.wait_ge(s5_shifted.sem, s5_shifted.at(g, step[1] + 1))
                    act.activation(sc5[:, 2, :, :], sc5[:, 1, :, :], ACT.Exp).then_inc(s5_exp.sem, 1)
                elif step == "c5T":
                    take(g, "c5T", c5T[:, :])
                elif step == "h6":
                    for c in range(NF):
                        act.wait_ge(wr(("h6", c)), product_done(g, ("h6", c)))
                        act.activation(h6[:, c, :], ap(("h6", c)), ACT.Relu).then_inc(em(("h6", c)), 1)

            act.wait_ge(prepared, NPREP)
            act.wait_ge(w_loaded, 16 * NLOAD[0])
            act.wait_ge(zeroed, NZ)
            run(act, first, second)

        @block.gpsimd
        def _(pool):
            for k in range(8):
                pool.sem_inc(banks.emptied[k], 1)
            pool.sem_inc(inputs_used.sem, 1)
            pool.sem_inc(ln_ready.sem, 1)
            pool.sem_inc(stored.sem, 32)
            pool.memset(w3_gate[:, :], 0.0).then_inc(zeroed, 1)
            pool.memset(w5_off[:, :], 0.0).then_inc(zeroed, 1)
            pool.memset(cT[:, :, :], 0.0).then_inc(zeroed, 1)
            pool.memset(VM[:, :, :, :], 0.0).then_inc(zeroed, 1)
            pool.memset(PT[1][:, :, :], 0.0).then_inc(zeroed, 1)
            pool.memset(uT[:, :, :], 0.0).then_inc(zeroed, 1)
            pool.memset(zero64[:, :], 0.0).then_inc(zeroed, 1)
            pool.wait_ge(zeroed, 7)
            for slot in range(2):
                for half in range(2):
                    area1 = VM[:, slot, half, :]
                    ones = bass.AP(area1.tensor, area1.offset + HH * E, [list(area1.ap[0]), [P + E, HH], [1, E]])
                    last = pool.memset(ones, 1.0)
            last.then_inc(zeroed, 1)
            pool.memset(v4[:, :, D:2 * D], 1.0).then_inc(zeroed, 1)
            pool.memset(mx[:, :, :], 0.0).then_inc(zeroed, 1)
            pool.wait_ge(w_loaded, 16 * NLOAD[0])

            def spread_rows(t, n):
                return t.unsqueeze(1).broadcast_to([t.shape[0], n, t.shape[1]])

            def residual(dst, src, bias, ready):
                pool.tensor_tensor(dst[:, :, :], src[:, :, :], spread_rows(bias[:, :], B), ALU.add)\
                    .then_inc(ready.sem, 1)

            def values(g, s, b):
                rows = (P, NKP)[s - 1]
                for half in range(2):
                    o = VM[0:rows, b % 2, half, :]
                    o = bass.AP(o.tensor, o.offset, [list(o.ap[0]), [P + E, HH], [1, E]])
                    at = slice(half * HH * E, (half + 1) * HH * E)
                    bias = b1_v[:, at] if s == 1 else zero64[0:rows, :]
                    m = pool.tensor_tensor(o, v[0:rows, b, at].rearrange("p (h e) -> p h e", e=E),
                                           bias.rearrange("p (h e) -> p h e", e=E), ALU.add)
                m.then_inc(vm_ready.sem, 1)

            def mask_keys(g, s, i):
                nk = (P, NKEY)[s - 1]
                b, c = divmod(i, NCH)
                if i >= 4:
                    pool.wait_ge(wr(("S", s, i - 4)), product_done(g, ("S", s, i - 4)))
                pool.tensor_tensor(KM[:, i % 4, :, 0:nk], spread_rows(kT[:, b * nk:(b + 1) * nk], HC),
                                   headmask[:, c * HC:(c + 1) * HC].unsqueeze(2).broadcast_to([P, HC, nk]),
                                   ALU.mult).then_inc(km_ready.sem, 1)

            def first(g, step):
                if step in ("prep1", "prep2"):
                    s = 1 if step == "prep1" else 2
                    pool.wait_ge(em(f"k{s}T"), product_read(g, f"k{s}T"))
                    mask_keys(g, s, 0)
                    mask_keys(g, s, 1)
                    pool.wait_ge(em(f"v{s}"), product_read(g, f"v{s}"))
                    values(g, s, 0)
                    values(g, s, 1)
                    if s == 1:
                        pool.wait_ge(em("cT"), product_read(g, "cT"))
                        pool.wait_ge(ln_ready.sem, ln_ready.at(g, 0))
                        residual(xb, xin, b1_o, inputs_used)
                    else:
                        pool.wait_ge(ln_ready.sem, ln_ready.at(g, 1))
                        residual(xb, xs, b2_o, xb_ready)
                elif step[0] in ("a1", "a2"):
                    s, i = 1 if step[0] == "a1" else 2, step[1]
                    if i + 2 < NCHUNK:
                        mask_keys(g, s, i + 2)
                    if s == 1 and 1 <= i < NCHUNK + 1:
                        k = i - 1
                        pool.wait_ge(max_ready.sem, max_ready.at(g, k + 1))
                        pool.tensor_tensor(Pq[:, k % 4, :, :], Pq[:, k % 4, :, :],
                                           mx[:, k % 4, :].unsqueeze(2).broadcast_to([P, HC, P]), ALU.subtract)\
                            .then_inc(shifted.sem, 1)
                    if i in (9, 13):
                        b = (i - 1) // 4
                        pool.wait_ge(wr(("PV", s, b - 2)), product_done(g, ("PV", s, b - 2)))
                        values(g, s, b)

            def second(g, step):
                if step == "xT3":
                    pool.wait_ge(ln_ready.sem, ln_ready.at(g, 3))
                    residual(xb2, xs2, b4_o, xb2_ready)
                elif step == "xT4":
                    pool.wait_ge(ln2_ready.sem, ln2_ready.at(g, 1))
                    residual(xb2, xs2, b5_o, xb2_ready)
                elif step[0] == "head" and 1 <= step[1] <= H:
                    h = step[1] - 1
                    for p in range(2):
                        k = 2 * h + p
                        pool.wait_ge(em(("G", h, p)), product_read(g, ("G", h, p)))
                        pool.tensor_tensor(kvs[:, h % HH, 2 * p:2 * p + 2, :, :].rearrange("q b n e -> q (b n) e"),
                                           gwt[:, k % 4, :, :, 0, :].rearrange("q b n e -> q (b n) e"),
                                           gwt[:, k % 4, :, :, 1, :].rearrange("q b n e -> q (b n) e"),
                                           ALU.add).then_inc(kvs_ready.sem, 1)

            run(pool, first, second)

        @block.vector
        def _(dve):
            pre = [0]

            def prep(ins, last=False):
                ins.then_inc(prepared, 1)
                pre[0] += 1
                dve.wait_ge(prepared, pre[0])

            dve.wait_ge(w_loaded, 16 * NLOAD[0])
            prep(dve.reciprocal(temp[:, :], temp[:, :]))
            prep(dve.tensor_scalar(qscale1[:, :], temp[:, :], float(E) ** -0.5, None, ALU.mult))
            prep(dve.tensor_tensor(qbias1[:, :], b1_qk[:, 0:1], qscale1[:, :], ALU.mult))
            prep(dve.tensor_scalar(b5_q[:, :], b5_q[:, :], 0.5 * float(E) ** -0.5, None, ALU.mult))
            prep(dve.tensor_reduce(masked[:, :], mask_i, AX, ALU.add))
            prep(dve.tensor_scalar(length[:, :], masked[:, :], -1.0, float(NKEY - 1), ALU.mult, ALU.add))
            prep(dve.tensor_tensor(length2[:, :], length[:, :], length[:, :], ALU.mult))
            assert pre[0] == NPREP, pre

            links = {}
            half_now = ["x"]

            def link(g, ins):
                half = half_now[0]
                ins.then_inc(chain[half].sem, 1)
                links[half] = links.get(half, 0) + 1
                dve.wait_ge(chain[half].sem, chain[half].at(g, links[half]))

            def bc(t, n):
                return t.unsqueeze(len(t.shape)).broadcast_to([*t.shape, n])

            def per_batch(t, n=B):
                return t.unsqueeze(1).broadcast_to([t.shape[0], n, *t.shape[1:]])

            def layer_norm(g, src, dst, ready):
                for b in range(B):
                    m = dve.bn_stats(stats[:, b, :], src[:, b, :])
                link(g, m)
                dve.memset(pause[:, :], 0.0)
                for b in range(B):
                    m = dve.bn_aggr(mv[:, b, :], stats[:, b, :])
                link(g, m)
                link(g, dve.tensor_scalar(vare[:, :], mv[:, :, 1], EPS, None, ALU.add))
                dve.tensor_scalar(hvar[:, :], vare[:, :], -0.5, None, ALU.mult)
                link(g, dve.tensor_scalar(rs[:, 0, :].bitcast(I32), vare[:, :].bitcast(I32), -0.5, SEED,
                                          ALU.mult, ALU.add))
                for n in range(NEWTON):
                    link(g, dve.tensor_tensor(nt[:, 0, :], rs[:, n % 2, :], rs[:, n % 2, :], ALU.mult))
                    link(g, dve.tensor_tensor(nt[:, 1, :], nt[:, 0, :], hvar[:, :], ALU.mult))
                    link(g, dve.scalar_tensor_tensor(out=rs[:, (n + 1) % 2, :], in0=nt[:, 1, :], scalar=1.5,
                                                     in1=rs[:, n % 2, :], op0=ALU.add, op1=ALU.mult))
                for b in range(B):
                    m = dve.tensor_scalar(dst[:, b, :], src[:, b, :], mv[:, b, 0:1], rs[:, NEWTON % 2, b:b + 1],
                                          ALU.subtract, ALU.mult)
                m.then_inc(ready.sem, 1)

            def attention(g, s, i):
                nk = (P, NKEY)[s - 1]
                if 1 <= i < NCHUNK + 1:
                    k = i - 1
                    c = k % NCH
                    name = ("S", s, k)
                    dve.wait_ge(wr(name), product_done(g, name))
                    if k >= 4:
                        dve.wait_ge(wr(("PT", s, k - 4)), product_done(g, ("PT", s, k - 4)))
                    src = ap(name)[:, 0:HC * nk].rearrange("p (h k) -> p h k", h=HC)
                    if s == 1:
                        dve.tensor_tensor(Pq[:, k % 4, :, :], src, bias1[:, c * HC:(c + 1) * HC, :], ALU.add)\
                           .then_inc(em(name), 1)
                        dve.wait_ge(em(name), product_read(g, name))
                        dve.tensor_reduce(mx[:, k % 4, :], Pq[:, k % 4, :, :], AX, ALU.max)\
                           .then_inc(max_ready.sem, 1)
                    else:
                        link(g, dve.tensor_reduce(mx[:, k % 4, :], src, AX, ALU.max))
                        dve.tensor_tensor(Pq[:, k % 4, :, 0:nk], src, bc(mx[:, k % 4, :], nk), ALU.subtract)\
                           .then_inc(em(name), 1)
                if i >= 8 and (i - 8) % NCH == 0:
                    b = (i - 8) // NCH
                    name = ("PV", s, b)
                    dve.wait_ge(wr(name), product_done(g, name))
                    if b >= 2:
                        dve.wait_ge(wr(("y", s, b - 2)), product_done(g, ("y", s, b - 2)))
                    src = ap(name)
                    link(g, dve.reciprocal(rden[:, :, :].rearrange("p a t -> p (a t)"), src[P // 2:P, 0:2 * P]))
                    dve.tensor_tensor(oT[0:P // 2, b % 2, :], src[0:P // 2, 0:P], rden[:, 0, :], ALU.mult)
                    dve.tensor_tensor(oT[P // 2:P, b % 2, :], src[0:P // 2, P:2 * P], rden[:, 1, :],
                                      ALU.mult).then_inc(em(name), 1)
                b = output_of(i)
                if b is not None:
                    name = ("y", s, b)
                    dve.wait_ge(wr(name), product_done(g, name))
                    if b == 0:
                        if s == 1:
                            dve.wait_ge(inputs_used.sem, inputs_used.at(g, 1))
                        else:
                            dve.wait_ge(xb_ready.sem, xb_ready.at(g, 1))
                    dve.tensor_tensor(ys[:, b, :], ap(name)[:, 0:D], xb[:, b, :], ALU.add).then_inc(em(name), 1)
                if i == LAST:
                    dve.wait_ge(em(("y", s, B - 1)), product_read(g, ("y", s, B - 1)))
                    layer_norm(g, ys, xs, ln_ready)

            def gates(g):
                dve.wait_ge(wr("gate"), product_done(g, "gate"))
                dve.tensor_copy(gl[:, 0, :, :], ap("gate").rearrange("p (b k) -> p b k", b=B)[:, :, 0:NE])\
                   .then_inc(em("gate"), 1)
                dve.wait_ge(em("gate"), product_read(g, "gate"))
                rank = per_batch(rank8[:, :])

                def best(src, m, km, dst):
                    link(g, dve.tensor_reduce(gm[:, m, :], gl[:, src, :, :], AX, ALU.max))
                    link(g, dve.tensor_tensor(gl[:, 1, :, :], gl[:, src, :, :], bc(gm[:, m, :], NE), ALU.is_equal))
                    link(g, dve.tensor_tensor(gl[:, 2, :, :], gl[:, 1, :, :], rank, ALU.mult))
                    link(g, dve.tensor_reduce(gm[:, km, :], gl[:, 2, :, :], AX, ALU.max))
                    link(g, dve.tensor_tensor(gl[:, dst, :, :], gl[:, 2, :, :], bc(gm[:, km, :], NE), ALU.is_equal))

                best(0, 0, 1, 3)
                dve.tensor_tensor(gl[:, 7, :, :], gl[:, 0, :, :], bc(gm[:, 0, :], NE), ALU.subtract)\
                   .then_inc(gate_shifted.sem, 1)
                link(g, dve.scalar_tensor_tensor(out=gl[:, 4, :, :], in0=gl[:, 3, :, :], scalar=-1e30,
                                                 in1=gl[:, 0, :, :], op0=ALU.mult, op1=ALU.add))
                best(4, 2, 3, 5)
                link(g, dve.tensor_tensor(gl[:, 6, :, :], gl[:, 3, :, :], gl[:, 5, :, :], ALU.add))

            def gate_shares(g):
                dve.wait_ge(gate_exp.sem, gate_exp.at(g, 1))
                link(g, dve.tensor_tensor(gl[:, 9, :, :], gl[:, 8, :, :], gl[:, 6, :, :], ALU.mult))
                link(g, dve.tensor_reduce(gm[:, 4, :], gl[:, 9, :, :], AX, ALU.add))
                link(g, dve.reciprocal(gm[:, 5, :], gm[:, 4, :]))
                link(g, dve.tensor_tensor(gw[:, :, :], gl[:, 9, :, :], bc(gm[:, 5, :], NE), ALU.mult))

            def table(g, b):
                by_head = lambda t: t.rearrange("p s (h e) -> p s h e", e=E)
                part = lambda n: tab[:, b, n, :, :].rearrange("p h (s e) -> p s h e", e=E)
                dve.wait_ge(wr(("tab", b)), product_done(g, ("tab", b)))
                for t in range(2):
                    m = dve.scalar_tensor_tensor(out=tabf[:, 2 * t:2 * t + 2, :].rearrange("p s d -> p (s d)"),
                                                 in0=b5_tab[:, :], scalar=iskey[:, t:t + 1],
                                                 in1=ap(("tab", b))[0:NKP, t * 2 * D:(t + 1) * 2 * D],
                                                 op0=ALU.mult, op1=ALU.add)
                m.then_inc(em(("tab", b)), 1)
                dve.wait_ge(em(("tab", b)), product_read(g, ("tab", b)))
                link(g, dve.tensor_copy(part(0), by_head(tabf)))
                link(g, dve.tensor_tensor(by_head(tabr), by_head(tabf), part(0), ALU.subtract))
                link(g, dve.tensor_copy(part(1), by_head(tabr)))
                dve.tensor_tensor(part(2), by_head(tabr), part(1), ALU.subtract).then_inc(tab_ready.sem, 1)
                dve.wait_ge(tab_ready.sem, tab_ready.at(g, b + 1))

            def first(g, step):
                half_now[0] = "x"
                if step == "load":
                    links["x"] = 0
                elif step[0] in ("a1", "a2"):
                    attention(g, 1 if step[0] == "a1" else 2, step[1])
                elif step == "gates":
                    gates(g)
                elif step == "gate_shares":
                    gate_shares(g)
                elif step[0] == "tab":
                    table(g, step[1])
                elif step[0] == "m" and step[1] % 2 == 1 and step[1] >= 3:
                    e = step[1] // 2 - 1
                    name = ("expert", e)
                    dve.wait_ge(wr(name), product_done(g, name))
                    if e:
                        dve.wait_ge(em(("expert", e - 1)), product_read(g, ("expert", e - 1)))
                    for b in range(B):
                        m = dve.scalar_tensor_tensor(out=ys[:, b, :], in0=ap(name)[:, b * P:(b + 1) * P],
                                                     scalar=gw[:, b, e:e + 1], in1=(ys if e else xs)[:, b, :],
                                                     op0=ALU.mult, op1=ALU.add)
                    m.then_inc(em(name), 1)
                elif step == "end":
                    dve.wait_ge(em(("expert", NE - 1)), product_read(g, ("expert", NE - 1)))
                    dve.wait_ge(stored.sem, stored.at(g, 0))
                    layer_norm(g, ys, xs2, ln_ready)
                    assert links["x"] == CHAIN[0], links

            def residual(g, name, n):
                dve.wait_ge(wr(name), product_done(g, name))
                dve.wait_ge(xb2_ready.sem, xb2_ready.at(g, n))
                dve.tensor_tensor(ys2[:, :, :], ap(name).rearrange("p (b d) -> p b d", b=B), xb2[:, :, :],
                                  ALU.add).then_inc(em(name), 1)
                dve.wait_ge(em(name), product_read(g, name))

            def linear_kv(g):
                two = lambda t: t.rearrange("p (b k) -> p b k", b=2)
                for p in range(2):
                    at = slice(2 * p * P, (2 * p + 2) * P)
                    dve.wait_ge(em(("kv4", p)), product_read(g, ("kv4", p)))
                    dve.scalar_tensor_tensor(out=k4[:, 2 * p:2 * p + 2, :], in0=two(e4[:, 0, at]), scalar=1.0,
                                             in1=two(t4[:, 1, at]), op0=ALU.min, op1=ALU.add)\
                       .then_inc(k4_ready.sem, 1)
                dve.wait_ge(em("q4T"), product_read(g, "q4T"))
                dve.scalar_tensor_tensor(out=qT2[:, :], in0=e4[:, 1, :], scalar=1.0, in1=t4[:, 0, :],
                                         op0=ALU.min, op1=ALU.add).then_inc(q4_ready.sem, 1)

            def sample_places(g, part):
                ia, ib, ic, idd = ix
                L, L2, LR = [bc(glen[:, k, :], HS) for k in range(3)]

                def tt(o, x, y, op):
                    link(g, dve.tensor_tensor(o, x, y, op))

                def ts(o, x, s1, op1, s2=None, op2=ALU.bypass):
                    link(g, dve.tensor_scalar(o, x, s1, s2, op1, op2))

                MAGIC = 1.5 * 2.0 ** 23
                if part == 0:
                    at = bass.ds((g[0] * B + g[1] * B), B)
                    dve.tensor_copy(glen[:, 0, :], length[:, at])
                    link(g, dve.tensor_copy(glen[:, 1, :], length2[:, at]))
                    link(g, dve.reciprocal(glen[:, 2, :], glen[:, 0, :]))
                    dve.wait_ge(wr("off"), product_done(g, "off"))
                    dve.tensor_tensor(ia, ap("off").rearrange("p (b k) -> p b k", b=B)[:, :, 0:HS],
                                      per_batch(b5_off[:, :]), ALU.add).then_inc(em("off"), 1)
                    dve.wait_ge(em("off"), product_read(g, "off"))
                    tt(ib, ia, per_batch(ramp[:, :]), ALU.add)
                    ts(ic, ib, token[:, 0:1], ALU.add)
                    tt(ia, ic, LR, ALU.mult)
                    ts(ib, ia, MAGIC, ALU.add, MAGIC, ALU.subtract)
                elif part == 1:
                    tt(idd, ib, ia, ALU.is_gt)
                    tt(ib, ib, idd, ALU.subtract)
                    tt(idd, ib, L, ALU.mult)
                    tt(ia, ic, idd, ALU.subtract)
                    tt(ib, ia, L, ALU.mult)
                    link(g, dve.scalar_tensor_tensor(out=ib, in0=ib, scalar=0.0, in1=L, op0=ALU.is_lt, op1=ALU.mult))
                    tt(ia, ia, ib, ALU.add)
                elif part == 2:
                    tt(ib, ia, L, ALU.mult)
                    tt(ib, ib, L2, ALU.is_ge)
                    tt(ib, ib, L, ALU.mult)
                    tt(ia, ia, ib, ALU.subtract)
                    ts(ia, ia, 1.0 / (NKEY - 1), ALU.mult, 2.0, ALU.mult)
                    ts(ia, ia, 1.0, ALU.subtract, 1.0, ALU.add)
                    ts(ia, ia, float(NKEY), ALU.mult, 1.0, ALU.subtract)
                    ts(ic, ia, 0.5, ALU.mult)
                else:
                    ts(ia, ic, MAGIC, ALU.add, MAGIC, ALU.subtract)
                    tt(ib, ia, ic, ALU.is_gt)
                    tt(idd, ia, ib, ALU.subtract)
                    tt(w01[:, :, :, 1], ic, idd, ALU.subtract)
                    ts(w01[:, :, :, 0], w01[:, :, :, 1], -1.0, ALU.mult, 1.0, ALU.add)
                    ts(ia, idd, -2.0, ALU.max, float(NKEY + 1), ALU.min)
                    halves = ia.rearrange("p b (s j) -> p b s j", s=2)
                    ts(uu[:, :, :, 0:HHS], halves, float(NCTR), ALU.subtract)
                    dve.tensor_tensor(uu[:, :, :, HHS:2 * HHS], uu[:, :, :, 0:HHS], uu[:, :, :, 0:HHS], ALU.mult)\
                       .then_inc(uu_ready.sem, 1)

            def weight(g, h, p):
                k = 2 * h + p
                name = ("G", h, p)
                dve.wait_ge(wr(name), product_done(g, name))
                if k >= 4:
                    dve.wait_ge(kvs_ready.sem, kvs_ready.at(g, k - 3))
                src = ap(name).rearrange("q (t r) -> q t r", t=2)[:, :, 0:NS * 4 * E]\
                    .rearrange("q t (m e) -> q t m e", e=2 * E)
                w = w01[:, 2 * p:2 * p + 2, h * NS:(h + 1) * NS, :].rearrange("q t n s -> q t (n s)")
                dve.tensor_tensor(gwt[:, k % 4, :, :, :, :].rearrange("q t n s e -> q t (n s) e"), src,
                                  bc(w, 2 * E), ALU.mult).then_inc(em(name), 1)

            def quarter(q):
                return kvs[:, (q % 2) * HQ:(q % 2 + 1) * HQ, :, :, :].rearrange("p h b n e -> p (h b) n e")

            def score(g, q):
                dve.wait_ge(kvs_ready.sem, kvs_ready.at(g, (q + 1) * 2 * HQ))
                qs = q5[:, q * HQ:(q + 1) * HQ, :, :].rearrange("p h b e -> p (h b) e")
                link(g, dve.tensor_tensor(prod5, quarter(q)[:, :, :, 0:E],
                                          qs.unsqueeze(2).broadcast_to([P, HQ * B, NS, E]), ALU.mult))
                link(g, dve.tensor_reduce(sc5[:, 0, :, :], prod5, AX, ALU.add))
                link(g, dve.tensor_reduce(sm5[:, 0, :], sc5[:, 0, :, :], AX, ALU.max))
                dve.tensor_tensor(sc5[:, 1, :, :], sc5[:, 0, :, :], bc(sm5[:, 0, :], NS), ALU.subtract)\
                   .then_inc(s5_shifted.sem, 1)

            def mix(g, q):
                dve.wait_ge(s5_exp.sem, s5_exp.at(g, q + 1))
                link(g, dve.tensor_reduce(sm5[:, 1, :], sc5[:, 2, :, :], AX, ALU.add))
                link(g, dve.reciprocal(sm5[:, 2, :], sm5[:, 1, :]))
                link(g, dve.scalar_tensor_tensor(out=sc5[:, 0, :, :], in0=sc5[:, 2, :, :], scalar=0.5,
                                                 in1=bc(sm5[:, 2, :], NS), op0=ALU.mult, op1=ALU.mult))
                link(g, dve.tensor_tensor(prod5, quarter(q)[:, :, :, E:2 * E], bc(sc5[:, 0, :, :], E), ALU.mult))
                by_seq = prod5.rearrange("p (h b) n e -> p b h e n", b=B)
                for b in range(B):
                    m = dve.tensor_reduce(o5[:, b, q * HQ * E:(q + 1) * HQ * E]
                                          .rearrange("p (h e) -> p h e", e=E), by_seq[:, b], AX, ALU.add)
                m.then_inc(o5_ready.sem, 1)
                dve.wait_ge(o5_ready.sem, o5_ready.at(g, q + 1))

            def spikes(g, k):
                y, n, t, s = [lif[:, k, :] for k in range(4)]
                if k == 0:
                    dve.wait_ge(wr("y6"), product_done(g, "y6"))
                    dve.tensor_copy(y, ap("y6")).then_inc(em("y6"), 1)
                    dve.wait_ge(em("y6"), product_read(g, "y6"))
                    dve.tensor_scalar(n, y, -1.0, None, ALU.mult)
                    link(g, dve.tensor_scalar(s, y, 1.0, None, ALU.is_gt))
                else:
                    link(g, dve.scalar_tensor_tensor(out=t, in0=n, scalar=-0.9, in1=y, op0=ALU.mult, op1=ALU.add))
                    link(g, dve.scalar_tensor_tensor(out=n, in0=n, scalar=-1.0, in1=t, op0=ALU.is_lt,
                                                     op1=ALU.subtract))
                    link(g, dve.scalar_tensor_tensor(out=s, in0=n, scalar=-1.0, in1=s, op0=ALU.is_lt, op1=ALU.add))
                if k == 4:
                    link(g, dve.scalar_tensor_tensor(out=ys2[:, :, :], in0=s.rearrange("p (b d) -> p b d", b=B),
                                                     scalar=0.2, in1=xs2[:, :, :], op0=ALU.mult, op1=ALU.add))

            def second(g, step):
                half_now[0] = "y"
                if step == "xT3":
                    links["y"] = 0
                elif step == "elu":
                    linear_kv(g)
                elif step == "kvmask":
                    for p in range(2):
                        dve.wait_ge(wr(("kvsum", p)), product_done(g, ("kvsum", p)))
                        dve.tensor_tensor(kv4[:, 2 * p:2 * p + 2, :], ap(("kvsum", p)).rearrange("p (b d) -> p b d", b=2),
                                          per_batch(block4[:, :, :].rearrange("p a d -> p (a d)"), 2), ALU.mult)\
                           .then_inc(em(("kvsum", p)), 1)
                elif step[0] == "ratio":
                    p = step[1]
                    src = ap(("nd", p))
                    dve.wait_ge(wr(("nd", p)), product_done(g, ("nd", p)))
                    if p == 0:
                        dve.wait_ge(q4_ready.sem, q4_ready.at(g, 1))
                    link(g, dve.tensor_scalar(dn4[:, p, 0, :], src[:, 2 * P:4 * P], 1e-8, None, ALU.add))
                    link(g, dve.reciprocal(dn4[:, p, 1, :], dn4[:, p, 0, :]))
                    dve.tensor_tensor(t4[:, 0, 2 * p * P:(2 * p + 2) * P], src[:, 0:2 * P], dn4[:, p, 1, :],
                                      ALU.mult).then_inc(em(("nd", p)), 1)
                elif step == "norm4":
                    residual(g, "y4", 1)
                    layer_norm(g, ys2, xs2, ln2_ready)
                elif step == "scale5":
                    dve.wait_ge(wr("q5"), product_done(g, "q5"))
                    heads = lambda t: t.rearrange("p (h e) -> p h e", e=E)
                    for b in range(B):
                        m = dve.scalar_tensor_tensor(out=q5[:, :, b, :], in0=heads(ap("q5")[:, b * D:(b + 1) * D]),
                                                     scalar=0.5 * float(E) ** -0.5, in1=heads(b5_q[:, :]),
                                                     op0=ALU.mult, op1=ALU.add)
                    m.then_inc(em("q5"), 1)
                elif step[0] == "place":
                    sample_places(g, step[1])
                elif step[0] == "head":
                    h = step[1]
                    if 1 <= h <= H:
                        weight(g, h - 1, 0)
                    if h in VECTOR_ROW:
                        j = h * NS + VN
                        dve.wait_ge(wr(("hit", j)), product_done(g, ("hit", j)))
                        dve.tensor_scalar(hit[:, j % NHIT, :], ap(("hit", j))[0:NKP, :], hitbias[:, 0:1], 0.0,
                                          ALU.add, ALU.max).then_inc(em(("hit", j)), 1)
                    if 1 <= h <= H:
                        weight(g, h - 1, 1)
                elif step[0] == "score":
                    score(g, step[1])
                elif step[0] == "mix":
                    mix(g, step[1])
                elif step == "norm5":
                    residual(g, "y5", 2)
                    layer_norm(g, ys2, xs2, ln2_ready)
                elif step == "square":
                    for c in range(NF):
                        dve.wait_ge(em(("h6", c)), product_read(g, ("h6", c)))
                        dve.tensor_tensor(h6[:, c, :], h6[:, c, :], h6[:, c, :], ALU.mult).then_inc(h6_ready.sem, 1)
                elif step[0] == "spikes":
                    spikes(g, step[1])
                elif step == "out":
                    layer_norm(g, ys2, xs2, ln2_ready)
                    assert links["y"] == CHAIN[1], links

            run(dve, first, second)


def constants():
    q = np.arange(P, dtype=np.float32)
    start = 2.0 ** (-2.0 ** (-(np.log2(H) - 3)))
    slopes = np.asarray([start * start ** i for i in range(H)], np.float32)
    rel = q[None, :] - q[:, None]
    bias = np.where(rel[:, None, :] <= 0, slopes[None, :, None] * rel[:, None, :], np.float32(-1e30))
    key = np.arange(NKP) - 1 - NCTR
    pick = np.zeros((NKP, HHS, NKP), np.float16)
    for j in range(HHS):
        pick[j, j, :] = 2 * key
        pick[HHS + j, j, :] = -1
    head = np.arange(D) // E
    block = (head[:, None] == head[None, :]).astype(np.float32)
    return {
        "c_ident": np.eye(P, dtype=np.float32),
        "c_bias1": bias.astype(np.float32),
        "c_ramp": np.tile(np.arange(-NS // 2, NS - NS // 2 - 1, dtype=np.float32), (P, H)),
        "c_token": q[:, None].copy(),
        "c_pick": pick,
        "c_hitbias": (1.0 - key.astype(np.float32) ** 2)[:, None].copy(),
        "c_iskey": np.stack([(key >= -NCTR) & (key < NKEY - NCTR), np.arange(NKP) < NKEY], 1).astype(np.float32),
        "c_rank8": np.tile(np.arange(NE, 0, -1, dtype=np.float32), (P, 1)),
        "c_headmask": (head[:, None] == np.arange(H)[None, :]).astype(np.float32),
        "c_block4": np.stack([block, block], 1).copy(),
    }


AS_GIVEN = ["x", "ctx_1024", "mask_BxS2_if0", "L0_attn_W_attn", "L0_attn_b_attn", "L0_attn_W_proj", "L0_attn_b_proj",
            "L0_attn_temperature", "L0_xattn_Wq", "L0_xattn_Wk", "L0_xattn_Wv", "L0_xattn_Wo", "L0_xattn_bo",
            "L0_ffn_gate_w", "L0_ffn_fc_w", "L0_ffn_proj_w", "L1_attn_b_proj", "L1_xattn_bk", "L1_xattn_bv",
            "L1_xattn_bq", "L1_xattn_boff", "L1_xattn_bo"]
TRANSPOSED = {"w4T": "L1_attn_w_qkv", "w4_oT": "L1_attn_w_proj", "w5_kT": "L1_xattn_Wk", "w5_vT": "L1_xattn_Wv",
              "w5_qT": "L1_xattn_Wq", "w5_offT": "L1_xattn_Woff", "w5_oT": "L1_xattn_Wo", "w6_fcT": "L1_ffn_W_fc",
              "w6_projT": "L1_ffn_W_proj"}


def layout(inputs):
    arrays = {name: np.ascontiguousarray(inputs[name]) for name in AS_GIVEN}
    for name, source in TRANSPOSED.items():
        arrays[name] = np.ascontiguousarray(np.transpose(np.asarray(inputs[source])))
    arrays.update(constants())
    return arrays


def kernel(**inputs):
    import concourse.bacc as bacc
    from concourse.bass_utils import run_bass_kernel_spmd

    nc = bacc.Bacc("TRN2", target_bir_lowering=False, num_devices=1)
    arrays, a = {}, {}
    for name, value in layout(inputs).items():
        arrays[f"in_{name}_dram"] = value
        a[name] = nc.dram_tensor(f"in_{name}_dram", value.shape, mybir.dt.from_np(value.dtype),
                                 kind="ExternalInput").ap()
    shape = inputs["x"].shape
    out = nc.dram_tensor("out_dram", shape, F32, kind="ExternalOutput").ap()
    decoder(nc, a, out)
    r = run_bass_kernel_spmd(nc, [arrays], core_ids=[0])
    return r.results[0]["out_dram"]
```

```python
from contextlib import ExitStack

import numpy as np
import concourse.bass as bass
from concourse import mybir

F32 = mybir.dt.float32
F16 = mybir.dt.float16
BF16 = mybir.dt.bfloat16
I32 = mybir.dt.int32
ALU = mybir.AluOpType
ACT = mybir.ActivationFunctionType
AX = mybir.AxisListType.X

P = 128
D = 128
H = 16
E = D // H
NKEY = 77
NKP = 96
B = 4
T = B * P
HC = 4
NCH = H // HC
NE = 8
NF = 4
NS = 5
HS = H * NS
HH = H // 2
HHS = HH * NS
HQ = H // 4
NCTR = 38
EPS = 1e-5
SEED = 1597463007.0
NEWTON = 3
VN = 3
VECTOR_ROW = range(2, H - 1)
START = (0, 0)
CHAIN = (91, 113)


PACKS = {
    "early": [("ident", P), ("w1_qkv", 3 * D), ("w1_o", D), ("b1_qk", 2), ("headmask", H)],
    "rows": [("temp", 1), ("b1_v", D), ("b1_o", D), ("b2_o", D), ("b4_o", D), ("b5_q", D), ("b5_off", HS),
             ("b5_o", D), ("b5_tab", 2 * D)],
    "late": [("w2_q", D), ("w2_k", D), ("w2_v", D), ("w2_o", D), ("w4_q", D), ("w4_kv", 2 * D), ("w4_o", D),
             ("w5_kv", 2 * D), ("w5_q", D), ("w5_o", D), ("w6_fc", NF * P), ("w6_proj", NF * D), ("b5_qcol", 1),
             ("ramp", HS), ("token", 1), ("rank8", NE), ("block4", 2 * D)],
    "keys": [("hitbias", 1), ("iskey", 2)],
}


class Signal:

    def __init__(self, sem, per, start=0):
        self.sem, self.per, self.start = sem, per, start

    def at(self, g, n):
        return g[0] * self.per + (g[1] * self.per + n + self.start)


class Banks:

    def __init__(self, written, emptied):
        self.written, self.emptied = written, emptied
        self.turns = [0] * 8
        self.place = {}

    def product(self, name, bank):
        self.place[name] = (bank, self.turns[bank])
        self.turns[bank] += 1

    def bank(self, name):
        return self.place[name][0]


NCHUNK = B * NCH
NATT = NCHUNK + 6
LAST = NATT - 1


def output_of(i):
    return B - 1 if i == LAST else (i - 11) // NCH if i >= 11 and (i - 11) % NCH == 0 and i < LAST - 1 else None


def divided_in(i):
    return B - 1 if i == LAST - 1 else (i - 9) // NCH if i >= 9 and (i - 9) % NCH == 0 and i < LAST else None


def plan_products(banks):
    for name, bank in (("xT", 0), 0), ("k1T", 1), ("q1T", 2), ("v1", 3), ("cT", 0):
        banks.product(name, bank)
    for s in (1, 2):
        if s == 2:
            for name, bank in ("k2T", 1), ("v2", 3), (("xT", 1), 0), ("q2T", 1):
                banks.product(name, bank)
        for i in range(NATT):
            if output_of(i) is not None:
                banks.product(("y", s, output_of(i)), 2)
            if i < NCHUNK:
                banks.product(("S", s, i), i % 2)
            if 4 <= i < NCHUNK + 4:
                banks.product(("PT", s, i - 4), 2)
        for b in range(B):
            banks.product(("PV", s, b), 3)
    banks.product(("xT", 2), 0)
    banks.product("gate", 3)
    for i in range(NE * NF):
        banks.product(("h", i), 1 + i % 2)
    for b in range(B):
        banks.product(("tab", b), 0)
    for e in range(NE):
        banks.product(("expert", e), 3 if e < NE - 1 else 1)
    for name, bank in (("xT", 3), 4), (("kv4", 0), 6), (("kv4", 1), 7), ("q4T", 5), (("kvsum", 0), 4), \
            (("kvsum", 1), 5), (("nd", 0), 6), (("nd", 1), 7), ("y4", 4), (("xT", 4), 5), ("q5T", 6), ("q5", 7), \
            ("off", 4), (("uT", 0), 5), (("uT", 1), 6):
        banks.product(name, bank)
    for j in range(HS):
        banks.product(("hit", j), 4 + j % 2)
    for h in range(H):
        for p in range(2):
            banks.product(("G", h, p), 6 + p)
    for name, bank in ("c5T", 4), ("y5", 5), (("xT", 5), 6), (("h6", 0), 7), (("h6", 1), 4), (("h6", 2), 5), \
            (("h6", 3), 6), ("y6", 7):
        banks.product(name, bank)


def schedule():
    after = {
        ("a1", 1): ["xT3"], ("a1", 2): ["kv4"], ("a1", 3): ["elu"], ("a1", 4): ["kvsum"],
        ("a1", 5): ["kvmask", "nd", ("ratio", 0)], ("a1", 6): [("ratio", 1)], ("a1", 7): ["y4"], ("a1", 8): ["norm4"],
        ("a1", 10): ["norm4b"], ("a1", 11): ["xT4"], ("a1", 12): ["q5"], ("a1", 13): ["off"],
        ("a1", 14): ["scale5", ("place", 0)], ("a1", 15): [("place", 1)], ("a1", 16): [("place", 2)],
        ("a1", 18): [("place", 3)], ("a1", 20): ["uT"], "kv2": [("head", 0), ("head", 1)], ("a2", 1): [("head", 2)],
        ("a2", 2): [("head", 3)], ("a2", 3): [("head", 4)],
        ("a2", 4): [("head", 5), ("score", 0), ("head", 6), ("mix", 0)], ("a2", 5): [("head", 7)],
        ("a2", 8): [("head", 8)], ("a2", 11): [("head", 9)], ("a2", 12): [("score", 1)], ("a2", 13): [("head", 10)],
        ("a2", 14): [("mix", 1)], ("a2", 15): [("head", 11)], ("a2", 17): [("head", 12), ("head", 13)],
        ("a2", 18): [("score", 2)], ("a2", 19): [("mix", 2)], ("a2", 20): [("head", 14)], ("a2", LAST): [("head", 15)],
        "xT2": [("head", 16)], ("m", 0): [("score", 3)], ("m", 1): [("mix", 3)], ("m", 3): ["c5T"],
        ("m", 4): ["y5", "norm5"], ("m", 5): ["norm5b"], ("m", 6): ["xT5"], ("m", 7): ["h6"],
        ("m", 8): ["square", "y6", ("spikes", 0), ("spikes", 1)], ("m", 9): [("spikes", 2)],
        ("m", 10): [("spikes", 3)], ("m", 12): [("spikes", 4)], ("m", 13): ["out"],
    }
    beside = {
        "gates": ["gate_exp", "gate_shares"], ("m", 1): [("tab", 0)], ("m", 6): [("tab", 1)], ("m", 7): [("tab", 2)],
        ("m", 11): [("tab", 3)],
    }
    steps = ["load", "xT0", "prep1"] + [("a1", i) for i in range(NATT)]
    steps += ["kv2", "xT1", "prep2"] + [("a2", i) for i in range(NATT)]
    steps += ["xT2", "gates"] + [("m", i) for i in range(2 * NE + 2)] + ["end"]
    order = []
    for x in steps:
        order += [("x", x)] + [("x", b) for b in beside.get(x, [])] + [("y", y) for y in after.get(x, [])]
    return order


ORDER = schedule()


def decoder(nc, a, out):
    NB = a["x"].shape[0]
    G = NB // B
    with ExitStack() as ctx:
        def sb(name, shape, dt=F32):
            return ctx.enter_context(nc.sbuf_tensor(name, shape, dt))

        def sem(name):
            return ctx.enter_context(nc.semaphore(name))

        def signal(name, per, start=0):
            return Signal(sem(name), per, start)

        ps = ctx.enter_context(nc.psum_tensor("ps", [P, 8, 512], F32))
        banks = Banks([sem(f"bank{k}_written") for k in range(8)], [sem(f"bank{k}_emptied") for k in range(8)])
        plan_products(banks)

        def turn(g, name, n):
            k, before = banks.place[name]
            return g[0] * banks.turns[k] + (g[1] * banks.turns[k] + before + n)

        def bank_free(g, name):
            return turn(g, name, 1)

        def product_done(g, name):
            return turn(g, name, 1)

        def product_read(g, name):
            return turn(g, name, 2)

        def wr(name):
            return banks.written[banks.bank(name)]

        def em(name):
            return banks.emptied[banks.bank(name)]

        def ap(name):
            return ps[:, banks.bank(name), :]

        def run(eng, first, second):
            def both(gx, gy):
                for half, step in ORDER:
                    if half == "x" and gx is not None:
                        first(gx, step)
                    if half == "y" and gy is not None:
                        second(gy, step)

            both(START, None)
            if G > 1:
                with eng.Fori(0, G - 1, 1) as i:
                    both((i, 1), (i, 0))
            both(None, (0, G - 1))

        def packed(pack, rows=P):
            whole = sb(pack, [rows, sum(n for _, n in PACKS[pack])])
            at, arrays = 0, {}
            for name, n in PACKS[pack]:
                arrays[name] = whole[:, at:at + n]
                at += n
            return whole, arrays

        early, e_ = packed("early")
        ident, w1_qkv, w1_o = e_["ident"], e_["w1_qkv"], e_["w1_o"]
        b1_qk = e_["b1_qk"]
        headmask = e_["headmask"]
        rows, r_ = packed("rows")
        temp, b1_v, b1_o, b2_o, b4_o = r_["temp"], r_["b1_v"], r_["b1_o"], r_["b2_o"], r_["b4_o"]
        b5_q, b5_off, b5_o = r_["b5_q"], r_["b5_off"], r_["b5_o"]
        b5_tab = r_["b5_tab"][0:NKP]
        late, l_ = packed("late")
        w2_q, w2_k, w2_v, w2_o = l_["w2_q"], l_["w2_k"], l_["w2_v"], l_["w2_o"]
        w4_q, w4_kv, w4_o = l_["w4_q"], l_["w4_kv"], l_["w4_o"]
        w5_kv, w5_q, w5_o, b5_qcol = l_["w5_kv"], l_["w5_q"], l_["w5_o"], l_["b5_qcol"]
        w6_fc, w6_proj = l_["w6_fc"], l_["w6_proj"].rearrange("p (c d) -> p c d", c=NF)
        ramp = l_["ramp"]
        token = l_["token"]
        rank8 = l_["rank8"]
        block4 = l_["block4"]
        keys, k_ = packed("keys", NKP)
        hitbias = k_["hitbias"]
        iskey = k_["iskey"]
        w3_gate = sb("w3_gate", [D, P])
        w3_fc = sb("w3_fc", [D, NE, NF * P])
        w3_proj = sb("w3_proj", [P, NE, NF, D])
        w5_off = sb("w5_off", [D, P])
        bias1 = sb("bias1", [P, H, P])
        pick = sb("pick", [NKP, HHS, NKP], F16)
        qscale1 = sb("qscale1", [P, 1])
        qbias1 = sb("qbias1", [P, 1])
        zero64 = sb("zero64", [P, HH * E])
        glen = sb("glen", [P, 3, B])
        masked = sb("masked", [P, NB])
        length = sb("length", [P, NB])
        length2 = sb("length2", [P, NB])

        xin = sb("xin", [P, B, D])
        ctxin = sb("ctxin", [NKEY, B, D])
        xs = sb("xs", [P, B, D])
        xb = sb("xb", [P, B, D])
        ys = xb
        xT = sb("xT", [D, T])
        cT = sb("cT", [D, B, P])
        qT = sb("qT", [D, T])
        kT = sb("kT", [D, T])
        KM = sb("KM", [D, 4, HC, P])
        VM = sb("VM", [P, 2, 2, HH * P])
        Pq = sb("Pq", [P, 4, HC, P])
        mx = sb("mx", [P, 4, HC])
        PT = [sb("pt1", [P, 2, HC * P]), sb("pt2", [NKP, 2, HC * P])]
        rden = sb("rden", [P, P])
        pv = sb("pv", [P, 2, 2, P])
        oT = sb("oT", [D, 2, P])
        yo = sb("yo", [P, B - 1, D])
        gl = Pq[:, 0, :, :].rearrange("p h k -> p (h k)")[:, 0:10 * B * NE]\
            .rearrange("p (s b e) -> p s b e", s=10, b=B)
        gm = sb("gm", [P, 6, B])
        gw = sb("gw", [P, B, NE])
        hT = sb("hT", [P, 2, NF, T])
        v = hT[:, 1, NF - 1, :].rearrange("p (b d) -> p b d", b=B)
        mask_i = hT[:, :, :, :].rearrange("p a c t -> p (a c t)")[:, 0:NB * NKEY].bitcast(I32)\
            .rearrange("p (b k) -> p b k", b=NB)

        stats = sb("stats", [P, B, 6])
        mv = sb("mv", [P, B, 2])
        pause = sb("pause", [P, 1])
        vare = sb("vare", [P, B])
        hvar = sb("hvar", [P, B])
        rs = sb("rs", [P, 2, B])
        nt = sb("nt", [P, 2, B])

        xs2 = sb("xs2", [P, B, D])
        xb2 = sb("xb2", [P, B, D])
        ys2 = xb2
        xT2 = sb("xT2", [D, T])
        qT2 = sb("qT2", [D, T])
        v4 = sb("v4", [P, B, 2 * D])
        tab = sb("tab", [NKP, B, 3, H, 4 * E], BF16)
        q5 = sb("q5", [P, H, B, E])
        w01 = sb("w01", [P, B, HS, 2])
        uT = sb("uT", [NKP, 2, T], F16)
        NHIT = 2 * NS
        hit = sb("hit", [NKP, NHIT, T], BF16)
        o5 = sb("o5", [P, B, D])
        RING = HH * B * NS * 2 * E
        scratch = sb("scratch", [P, RING + 2208])

        def area(at, shape):
            n = int(np.prod(shape))
            names = "abcdef"[:len(shape)]
            t = scratch[:, at:at + n]
            if len(shape) == 1:
                return t
            return t.rearrange(f"p ({' '.join(names)}) -> p {' '.join(names)}", **dict(zip(names, shape)))

        e4, t4, k4 = area(0, [2, T]), area(2 * T, [2, T]), area(4 * T, [B, D])
        kv4, dn4 = area(5 * T, [B, 2 * D]), area(7 * T, [2, 2, 2 * P])
        ix = [area(n * B * HS, [B, HS]) for n in range(4)]
        tabf, tabr = [Pq[0:NKP, k, :, :] for k in (1, 2)]
        uu = area(4 * B * HS, [B, 2, 2 * HHS])
        kvs = area(0, [HH, B, NS, 2 * E])
        gwt = area(RING, [4, 2, NS, 2, 2 * E])
        prod5 = area(RING + 1280, [HQ * B, NS, E])
        sc5 = area(RING + 1920, [3, HQ * B, NS])
        sm5 = area(RING + 2160, [3, HQ * B])
        h6 = area(0, [NF, T])
        lif = area(NF * T, [4, T])
        c5T = qT2

        w_loaded = sem("early_weights_loaded")
        w2_loaded = sem("late_weights_loaded")
        bias_loaded = sem("attention_bias_loaded")
        zeroed = sem("constants_zeroed")
        prepared = sem("constants_prepared")
        x_loaded = signal("x_loaded", 16)
        c_loaded = signal("context_loaded", 16)
        km_ready = signal("masked_keys_ready", 2 * NCHUNK)
        vm_ready = signal("masked_values_ready", 2 * B)
        max_ready = signal("row_maxima_ready", NCHUNK)
        shifted = signal("scores_shifted", NCHUNK)
        probs = signal("probabilities_ready", 2 * NCHUNK)
        o_ready = signal("attention_output_ready", 2 * B)
        inputs_used = signal("inputs_used", 1, 1)
        xb_ready = signal("residual_ready", 1)
        xb2_ready = signal("residual2_ready", 2)
        ln_ready = signal("layer_norm_ready", 3, 1)
        ln2_ready = signal("layer_norm2_ready", 3)
        gate_shifted = signal("gates_shifted", 1)
        gate_exp = signal("gates_exponentiated", 1)
        tab_ready = signal("tables_ready", B)
        q4_ready = signal("linear_q_ready", 1)
        k4_ready = signal("linear_k_ready", 2)
        uu_ready = signal("samples_ready", 1)
        kvs_ready = signal("sampled_keys_values_ready", 2 * H)
        s5_shifted = signal("sample_scores_shifted", 4)
        s5_exp = signal("sample_scores_exponentiated", 4)
        o5_ready = signal("sampled_output_ready", 4)
        h6_ready = signal("spiking_hidden_ready", NF)
        stored = signal("output_stored", 32, 32)

        NLOAD = [0, 0]
        NZ = 10
        NPREP = 7
        chain = {"x": signal("vector_chain", CHAIN[0]), "y": signal("vector_chain2", CHAIN[1])}

        block = ctx.enter_context(nc.Block())

        @block.sync
        def _(sp):
            def load(dst, src, loaded, counted):
                sp.dma_start(dst, src).then_inc(loaded, 16)
                NLOAD[counted] += 1

            def load_late():
                load(late[:, :], a["late"], w2_loaded, 1)
                load(mask_i, a["mask_BxS2_if0"].rearrange("(a b) k -> a b k", a=1).broadcast_to([P, NB, NKEY]),
                     w2_loaded, 1)
                load(keys[:, :], a["keys"], w2_loaded, 1)
                load(pick[:, :, :], a["c_pick"], w2_loaded, 1)
                load(w3_fc[:, :, :], a["L0_ffn_fc_w"].rearrange("e d f -> d e f"), w2_loaded, 1)
                load(w3_proj[:, :, :, :], a["L0_ffn_proj_w"].rearrange("e (c p) d -> p e c d", p=P), w2_loaded, 1)
                sp.wait_ge(zeroed, NZ)
                load(w3_gate[:, 0:NE], a["L0_ffn_gate_w"], w2_loaded, 1)
                load(w5_off[:, 0:HS], a["w5_offT"], w2_loaded, 1)

            load(early[:, :], a["early"], w_loaded, 0)
            load(rows[:, :], a["rows"].broadcast_to([P, rows.shape[1]]), w_loaded, 0)

            def group(t, g, rows, b=0, n=B):
                at = g[0] * (B * rows * D) + (g[1] * B + b) * (rows * D)
                return bass.AP(t.tensor, at, [[D, rows], [rows * D, n], [1, D]])

            def first(g, step):
                if step == "load":
                    src_x, src_c = group(a["x"], g, P), group(a["ctx_1024"], g, NKEY)
                    sp.wait_ge(inputs_used.sem, inputs_used.at(g, 0))
                    sp.dma_start(xin[:, :, :], src_x).then_inc(x_loaded.sem, 16)
                    sp.dma_start(ctxin[:, :, :], src_c).then_inc(c_loaded.sem, 16)
                elif step == "prep1" and g is START:
                    sp.dma_start(bias1[:, :, :], a["c_bias1"]).then_inc(bias_loaded, 16)
                    load_late()

            def second(g, step):
                if step == "out":
                    sp.wait_ge(ln2_ready.sem, ln2_ready.at(g, 3))
                    for b in (B // 2, 0):
                        sp.dma_start(group(out, g, P, b, B // 2), xs2[:, b:b + B // 2, :]).then_inc(stored.sem, 16)

            run(sp, first, second)
            sp.wait_ge(stored.sem, stored.at((0, G - 1), 32))

        @block.tensor
        def _(pe):
            def mm(o, lhsT, rhs, start=True, stop=True):
                return pe.matmul(o, lhsT, rhs, start=start, stop=stop)

            def transpose_x(g, s, src):
                pe.wait_ge(em(("xT", s)), bank_free(g, ("xT", s)))
                for b in range(B):
                    m = pe.transpose(ap(("xT", s))[:, b * P:(b + 1) * P], src[:, b, :], ident[:, :])
                m.then_inc(wr(("xT", s)), 1)

            def project(g, name, w, x):
                pe.wait_ge(em(name), bank_free(g, name))
                mm(ap(name)[:, 0:x.shape[-1] if len(x.shape) == 2 else x.shape[1] * x.shape[2]], w, x)\
                    .then_inc(wr(name), 1)

            def project_rows(g, name, w, x, n, m=P):
                pe.wait_ge(em(name), bank_free(g, name))
                for b in range(B):
                    last = mm(ap(name)[0:m, b * P:b * P + n], x(b), w)
                last.then_inc(wr(name), 1)

            def cols(t):
                return lambda b: t[:, b * P:(b + 1) * P]

            def attention(g, s, i):
                nk = (P, NKEY)[s - 1]
                rows = (P, NKP)[s - 1]
                b = output_of(i)
                if b is not None:
                    pe.wait_ge(o_ready.sem, o_ready.at(g, (s - 1) * B + b + 1))
                    pe.wait_ge(em(("y", s, b)), bank_free(g, ("y", s, b)))
                    mm(ap(("y", s, b))[:, 0:D], oT[:, b % 2, :], (w1_o, w2_o)[s - 1][:, :])\
                        .then_inc(wr(("y", s, b)), 1)
                if i < NCHUNK:
                    b = i // NCH
                    pe.wait_ge(km_ready.sem, km_ready.at(g, (s - 1) * NCHUNK + i + 1))
                    pe.wait_ge(em(("S", s, i)), bank_free(g, ("S", s, i)))
                    mm(ap(("S", s, i))[:, 0:HC * nk], qT[:, b * P:(b + 1) * P], KM[:, i % 4, :, 0:nk])\
                        .then_inc(wr(("S", s, i)), 1)
                if 4 <= i < NCHUNK + 4:
                    k = i - 4
                    pe.wait_ge(probs.sem, probs.at(g, (s - 1) * NCHUNK + k + 1))
                    pe.wait_ge(em(("PT", s, k)), bank_free(g, ("PT", s, k)))
                    for n in range(HC):
                        m = pe.transpose(ap(("PT", s, k))[0:nk, n * P:(n + 1) * P], Pq[:, k % 4, n, 0:nk],
                                         ident[:, :])
                    m.then_inc(wr(("PT", s, k)), 1)
                if 5 <= i < NCHUNK + 5:
                    b, c = divmod(i - 5, NCH)
                    name = ("PV", s, b)
                    if c == 0:
                        pe.wait_ge(vm_ready.sem, vm_ready.at(g, (s - 1) * B + b + 1))
                        pe.wait_ge(em(name), bank_free(g, name))
                    pe.wait_ge(em(("PT", s, i - 5)), product_read(g, ("PT", s, i - 5)))
                    for n in range(HC):
                        half, r = divmod(c * HC + n, HH)
                        m = mm(ap(name)[:, half * P:(half + 1) * P], VM[0:rows, b % 2, half, r * P:(r + 1) * P],
                               PT[s - 1][0:rows, (i - 5) % 2, n * P:(n + 1) * P], start=(r == 0), stop=(r == HH - 1))
                    if c == NCH - 1:
                        m.then_inc(wr(name), 1)

            def first(g, step):
                if step == ("a1", 0) and g is START:
                    pe.wait_ge(zeroed, NZ)
                if step == "kv2" and g is START:
                    pe.wait_ge(w2_loaded, 16 * NLOAD[1])
                if step == "xT0":
                    pe.wait_ge(x_loaded.sem, x_loaded.at(g, 16))
                    transpose_x(g, 0, xin)
                elif step == "prep1":
                    pe.wait_ge(em(("xT", 0)), product_read(g, ("xT", 0)))
                    project(g, "k1T", w1_qkv[:, D:2 * D], xT[:, :])
                    project(g, "q1T", w1_qkv[:, 0:D], xT[:, :])
                    project_rows(g, "v1", w1_qkv[:, 2 * D:3 * D], cols(xT), D)
                    pe.wait_ge(c_loaded.sem, c_loaded.at(g, 16))
                    pe.wait_ge(em("cT"), bank_free(g, "cT"))
                    for b in range(B):
                        m = pe.transpose(ap("cT")[:, b * P:b * P + NKEY], ctxin[:, b, :], ident[0:NKEY, 0:NKEY])
                    m.then_inc(wr("cT"), 1)
                elif step == "kv2":
                    project(g, "k2T", w2_k[:, :], cT[:, :, 1:1 + NKEY])
                    project_rows(g, "v2", w2_v[:, :], lambda b: cT[:, b, 1:1 + NKP], D, NKP)
                elif step == "xT1":
                    pe.wait_ge(ln_ready.sem, ln_ready.at(g, 1))
                    transpose_x(g, 1, xs)
                elif step == "prep2":
                    pe.wait_ge(em(("xT", 1)), product_read(g, ("xT", 1)))
                    project(g, "q2T", w2_q[:, :], xT[:, :])
                    pe.wait_ge(em("q2T"), product_read(g, "q2T"))
                elif step == "xT2":
                    pe.wait_ge(ln_ready.sem, ln_ready.at(g, 2))
                    transpose_x(g, 2, xs)
                elif step == "gates":
                    pe.wait_ge(em(("xT", 2)), product_read(g, ("xT", 2)))
                    project_rows(g, "gate", w3_gate[:, :], cols(xT), P)
                elif step[0] in ("a1", "a2"):
                    if step == ("a1", 0):
                        pe.wait_ge(em("q1T"), product_read(g, "q1T"))
                    attention(g, 1 if step[0] == "a1" else 2, step[1])
                elif step[0] == "tab":
                    b = step[1]
                    pe.wait_ge(em(("tab", b)), bank_free(g, ("tab", b)))
                    for s in range(2):
                        m = mm(ap(("tab", b))[0:NKP, s * 2 * D:(s + 1) * 2 * D], cT[:, b, s:s + NKP], w5_kv[:, :])
                    m.then_inc(wr(("tab", b)), 1)
                elif step[0] == "m" and step[1] % 2 == 0 and step[1] < 2 * NE:
                    e = step[1] // 2
                    for c in range(NF):
                        name = ("h", e * NF + c)
                        pe.wait_ge(em(name), bank_free(g, name))
                        mm(ap(name), w3_fc[:, e, c * P:(c + 1) * P], xT[:, :]).then_inc(wr(name), 1)
                elif step[0] == "m" and step[1] % 2 == 1 and step[1] >= 3:
                    e = step[1] // 2 - 1
                    pe.wait_ge(em(("expert", e)), bank_free(g, ("expert", e)))
                    hidden = ("h", e * NF + NF - 1)
                    pe.wait_ge(em(hidden), product_read(g, hidden))
                    for b in range(B):
                        for c in range(NF):
                            m = mm(ap(("expert", e))[:, b * P:(b + 1) * P], hT[:, e % 2, c, b * P:(b + 1) * P],
                                   w3_proj[:, e, c, :], start=(c == 0), stop=(c == NF - 1))
                    m.then_inc(wr(("expert", e)), 1)

            def spread(g, j):
                pe.wait_ge(em(("hit", j)), bank_free(g, ("hit", j)))
                mm(ap(("hit", j))[0:NKP, :], pick[:, j % HHS, :], uT[:, j // HHS, :]).then_inc(wr(("hit", j)), 1)

            def gather(g, h, p, n):
                j = h * NS + n
                name = ("G", h, p)
                pe.wait_ge(em(("hit", j)), product_read(g, ("hit", j)))
                if n == 0:
                    pe.wait_ge(em(name), bank_free(g, name))
                for t in range(2):
                    b = 2 * p + t
                    o = t * 256 + n * 4 * E
                    for part in range(3):
                        m = mm(ap(name)[:, o:o + 4 * E], hit[:, j % NHIT, b * P:(b + 1) * P],
                               tab[:, b, part, h, :], start=(part == 0), stop=(part == 2))
                if n == NS - 1:
                    m.then_inc(wr(name), 1)

            def second(g, step):
                if step == "xT3":
                    pe.wait_ge(ln_ready.sem, ln_ready.at(g, 3))
                    transpose_x(g, 3, xs2)
                elif step == "kv4":
                    pe.wait_ge(em(("xT", 3)), product_read(g, ("xT", 3)))
                    for p in range(2):
                        pe.wait_ge(em(("kv4", p)), bank_free(g, ("kv4", p)))
                        for j in range(2):
                            m = mm(ap(("kv4", p))[:, j * 2 * D:(j + 1) * 2 * D], cols(xT2)(2 * p + j), w4_kv[:, :])
                        m.then_inc(wr(("kv4", p)), 1)
                    project(g, "q4T", w4_q[:, :], xT2[:, :])
                elif step == "kvsum":
                    for p in range(2):
                        pe.wait_ge(k4_ready.sem, k4_ready.at(g, p + 1))
                        pe.wait_ge(em(("kvsum", p)), bank_free(g, ("kvsum", p)))
                        for j in range(2):
                            b = 2 * p + j
                            m = mm(ap(("kvsum", p))[:, j * 2 * D:(j + 1) * 2 * D], k4[:, b, :], v4[:, b, :])
                        m.then_inc(wr(("kvsum", p)), 1)
                elif step == "nd":
                    pe.wait_ge(q4_ready.sem, q4_ready.at(g, 1))
                    for p in range(2):
                        pe.wait_ge(em(("kvsum", p)), product_read(g, ("kvsum", p)))
                        pe.wait_ge(em(("nd", p)), bank_free(g, ("nd", p)))
                        for j in range(2):
                            b = 2 * p + j
                            for t in range(2):
                                m = mm(ap(("nd", p))[:, (2 * t + j) * P:(2 * t + j + 1) * P],
                                       kv4[:, b, t * D:(t + 1) * D], cols(qT2)(b))
                        m.then_inc(wr(("nd", p)), 1)
                elif step == "y4":
                    pe.wait_ge(em(("nd", 0)), product_read(g, ("nd", 0)))
                    pe.wait_ge(em(("nd", 1)), product_read(g, ("nd", 1)))
                    project_rows(g, "y4", w4_o[:, :], cols(t4[:, 0, :]), D)
                elif step == "xT4":
                    pe.wait_ge(ln2_ready.sem, ln2_ready.at(g, 1))
                    transpose_x(g, 4, xs2)
                elif step == "q5":
                    pe.wait_ge(em(("xT", 4)), product_read(g, ("xT", 4)))
                    project(g, "q5T", w5_q[:, :], xT2[:, :])
                    project_rows(g, "q5", w5_q[:, :], cols(xT2), D)
                elif step == "off":
                    pe.wait_ge(em("q5T"), product_read(g, "q5T"))
                    project_rows(g, "off", w5_off[:, :], cols(qT2), P)
                elif step == "uT":
                    pe.wait_ge(uu_ready.sem, uu_ready.at(g, 1))
                    for half in range(2):
                        pe.wait_ge(em(("uT", half)), bank_free(g, ("uT", half)))
                        for b in range(B):
                            m = pe.transpose(ap(("uT", half))[0:2 * HHS, b * P:(b + 1) * P], uu[:, b, half, :],
                                             ident[:, :])
                        m.then_inc(wr(("uT", half)), 1)
                elif step[0] == "head":
                    h = step[1]
                    if h == 0:
                        pe.wait_ge(tab_ready.sem, tab_ready.at(g, B))
                        pe.wait_ge(em(("uT", 0)), product_read(g, ("uT", 0)))
                        pe.wait_ge(em(("uT", 1)), product_read(g, ("uT", 1)))
                    work = [(p, n) for p in range(2) for n in range(NS)]
                    for n in range(NS):
                        if h < H:
                            spread(g, h * NS + n)
                        if 1 <= h <= H:
                            gather(g, h - 1, *work[2 * n])
                            gather(g, h - 1, *work[2 * n + 1])
                elif step == "c5T":
                    pe.wait_ge(o5_ready.sem, o5_ready.at(g, 4))
                    pe.wait_ge(em("c5T"), bank_free(g, "c5T"))
                    for b in range(B):
                        m = pe.transpose(ap("c5T")[:, b * P:(b + 1) * P], o5[:, b, :], ident[:, :])
                    m.then_inc(wr("c5T"), 1)
                elif step == "y5":
                    pe.wait_ge(em("c5T"), product_read(g, "c5T"))
                    project_rows(g, "y5", w5_o[:, :], cols(c5T), D)
                elif step == "xT5":
                    pe.wait_ge(ln2_ready.sem, ln2_ready.at(g, 2))
                    transpose_x(g, 5, xs2)
                elif step == "h6":
                    pe.wait_ge(em(("xT", 5)), product_read(g, ("xT", 5)))
                    for c in range(NF):
                        project(g, ("h6", c), w6_fc[:, c * P:(c + 1) * P], xT2[:, :])
                elif step == "y6":
                    pe.wait_ge(h6_ready.sem, h6_ready.at(g, NF))
                    pe.wait_ge(em("y6"), bank_free(g, "y6"))
                    for b in range(B):
                        for c in range(NF):
                            m = mm(ap("y6")[:, b * P:(b + 1) * P], h6[:, c, b * P:(b + 1) * P], w6_proj[:, c, :],
                                   start=(c == 0), stop=(c == NF - 1))
                    m.then_inc(wr("y6"), 1)

            pe.wait_ge(w_loaded, 16 * NLOAD[0])
            run(pe, first, second)

        @block.scalar
        def _(act):
            def take(g, name, dst, src=None):
                act.wait_ge(wr(name), product_done(g, name))
                act.copy(dst, ap(name) if src is None else src).then_inc(em(name), 1)

            def attention(g, s, i):
                nk = (P, NKEY)[s - 1]
                if 2 <= i < NCHUNK + 2:
                    k = i - 2
                    if s == 1:
                        act.wait_ge(shifted.sem, shifted.at(g, k + 1))
                    else:
                        act.wait_ge(em(("S", s, k)), product_read(g, ("S", s, k)))
                    act.activation(Pq[:, k % 4, :, 0:nk], Pq[:, k % 4, :, 0:nk], ACT.Exp).then_inc(probs.sem, 1)
                b = output_of(i)
                if b is not None and b < B - 1:
                    take(g, ("y", s, b), yo[:, b, :], ap(("y", s, b))[:, 0:D])
                if 4 <= i < NCHUNK + 4:
                    k = i - 4
                    take(g, ("PT", s, k), PT[s - 1][0:nk, k % 2, :], ap(("PT", s, k))[0:nk, :])
                if i >= 8 and (i - 8) % NCH == 0:
                    b = (i - 8) // NCH
                    if b >= 2:
                        act.wait_ge(o_ready.sem, o_ready.at(g, (s - 1) * B + b - 1))
                    name = ("PV", s, b)
                    act.wait_ge(wr(name), product_done(g, name))
                    for half in range(2):
                        heads = slice(half * P // 2, (half + 1) * P // 2)
                        for t in range(2):
                            m = act.copy(pv[heads, b % 2, t, :],
                                         ap(name)[t * P // 2:(t + 1) * P // 2, half * P:(half + 1) * P])
                    m.then_inc(em(name), 1)

            def first(g, step):
                if step == "kv2" and g is START:
                    act.wait_ge(w2_loaded, 16 * NLOAD[1])
                if step in ("xT0", "xT1", "xT2"):
                    take(g, ("xT", int(step[2])), xT[:, :])
                elif step == "prep1":
                    act.wait_ge(wr("k1T"), product_done(g, "k1T"))
                    act.activation(kT[:, :], ap("k1T"), ACT.Identity, bias=b1_qk[:, 1:2]).then_inc(em("k1T"), 1)
                    act.wait_ge(wr("q1T"), product_done(g, "q1T"))
                    act.activation(qT[:, :], ap("q1T"), ACT.Identity, bias=qbias1[:, :], scale=qscale1[:, :])\
                        .then_inc(em("q1T"), 1)
                    take(g, "v1", v[:, :, :])
                    if g is START:
                        act.wait_ge(zeroed, NZ)
                    take(g, "cT", cT[:, :, 1:1 + NKEY], ap("cT").rearrange("p (b k) -> p b k", b=B)[:, :, 0:NKEY])
                elif step == "kv2":
                    take(g, "k2T", kT[:, 0:B * NKEY], ap("k2T")[:, 0:B * NKEY])
                    take(g, "v2", v[0:NKP, :, :], ap("v2")[0:NKP, :])
                elif step == "prep2":
                    act.wait_ge(wr("q2T"), product_done(g, "q2T"))
                    act.activation(qT[:, :], ap("q2T"), ACT.Copy, scale=float(E) ** -0.5).then_inc(em("q2T"), 1)
                elif step == "gate_exp":
                    act.wait_ge(gate_shifted.sem, gate_shifted.at(g, 1))
                    act.activation(gl[:, 8, :, :], gl[:, 7, :, :], ACT.Exp).then_inc(gate_exp.sem, 1)
                elif step[0] in ("a1", "a2"):
                    attention(g, 1 if step[0] == "a1" else 2, step[1])
                elif step[0] == "m" and step[1] % 2 == 0 and step[1] < 2 * NE:
                    e = step[1] // 2
                    for c in range(NF):
                        name = ("h", e * NF + c)
                        act.wait_ge(wr(name), product_done(g, name))
                        act.activation(hT[:, e % 2, c, :], ap(name), ACT.Gelu).then_inc(em(name), 1)

            def second(g, step):
                if step in ("xT3", "xT4", "xT5"):
                    take(g, ("xT", int(step[2])), xT2[:, :])
                elif step == "kv4":
                    for p in range(2):
                        at = slice(p * 2 * P, (p + 1) * 2 * P)
                        src = ap(("kv4", p)).rearrange("p (b k) -> p b k", b=2)
                        act.wait_ge(wr(("kv4", p)), product_done(g, ("kv4", p)))
                        for dst, fn in (e4[:, 0, at], ACT.Exp), (t4[:, 1, at], ACT.Relu):
                            act.activation(dst.rearrange("p (b k) -> p b k", b=2), src[:, :, 0:D], fn)
                        act.copy(v4[:, 2 * p:2 * p + 2, 0:D], src[:, :, D:2 * D]).then_inc(em(("kv4", p)), 1)
                    act.wait_ge(wr("q4T"), product_done(g, "q4T"))
                    act.activation(e4[:, 1, :], ap("q4T"), ACT.Exp)
                    act.activation(t4[:, 0, :], ap("q4T"), ACT.Relu).then_inc(em("q4T"), 1)
                elif step == "q5":
                    act.wait_ge(wr("q5T"), product_done(g, "q5T"))
                    act.activation(qT2[:, :], ap("q5T"), ACT.Identity, bias=b5_qcol[:, :]).then_inc(em("q5T"), 1)
                elif step == "uT":
                    for half in range(2):
                        take(g, ("uT", half), uT[0:2 * HHS, half, :], ap(("uT", half))[0:2 * HHS, :])
                elif step[0] == "head":
                    h = step[1]
                    for n in range(NS):
                        j = h * NS + n
                        if h < H and not (n == VN and h in VECTOR_ROW):
                            act.wait_ge(wr(("hit", j)), product_done(g, ("hit", j)))
                            act.activation(hit[:, j % NHIT, :], ap(("hit", j))[0:NKP, :], ACT.Relu,
                                           bias=hitbias[:, :]).then_inc(em(("hit", j)), 1)
                elif step[0] == "mix":
                    act.wait_ge(s5_shifted.sem, s5_shifted.at(g, step[1] + 1))
                    act.activation(sc5[:, 2, :, :], sc5[:, 1, :, :], ACT.Exp).then_inc(s5_exp.sem, 1)
                elif step == "c5T":
                    take(g, "c5T", c5T[:, :])
                elif step == "h6":
                    for c in range(NF):
                        act.wait_ge(wr(("h6", c)), product_done(g, ("h6", c)))
                        act.activation(h6[:, c, :], ap(("h6", c)), ACT.Relu).then_inc(em(("h6", c)), 1)

            act.wait_ge(w_loaded, 16 * NLOAD[0])
            act.wait_ge(prepared, 3)
            run(act, first, second)

        @block.gpsimd
        def _(pool):
            for k in range(8):
                pool.sem_inc(banks.emptied[k], 1)
            pool.sem_inc(inputs_used.sem, 1)
            pool.sem_inc(ln_ready.sem, 1)
            pool.sem_inc(stored.sem, 32)
            for zeros in VM[:, :, :, :], cT[:, :, :], w3_gate[:, :], w5_off[:, :], PT[1][:, :, :], uT[:, :, :], \
                    zero64[:, :]:
                pool.memset(zeros, 0.0).then_inc(zeroed, 1)
            pool.wait_ge(zeroed, 7)
            for slot in range(2):
                for half in range(2):
                    area1 = VM[:, slot, half, :]
                    ones = bass.AP(area1.tensor, area1.offset + HH * E, [list(area1.ap[0]), [P + E, HH], [1, E]])
                    last = pool.memset(ones, 1.0)
            last.then_inc(zeroed, 1)
            pool.memset(v4[:, :, D:2 * D], 1.0).then_inc(zeroed, 1)
            pool.memset(mx[:, :, :], 0.0).then_inc(zeroed, 1)
            pool.wait_ge(w_loaded, 16 * NLOAD[0])

            def spread_rows(t, n):
                return t.unsqueeze(1).broadcast_to([t.shape[0], n, t.shape[1]])

            def residual(dst, src, bias, ready):
                pool.tensor_tensor(dst[:, :, :], src[:, :, :], spread_rows(bias[:, :], B), ALU.add)\
                    .then_inc(ready.sem, 1)

            def values(g, s, b):
                rows = (P, NKP)[s - 1]
                for half in range(2):
                    o = VM[0:rows, b % 2, half, :]
                    o = bass.AP(o.tensor, o.offset, [list(o.ap[0]), [P + E, HH], [1, E]])
                    at = slice(half * HH * E, (half + 1) * HH * E)
                    bias = b1_v[:, at] if s == 1 else zero64[0:rows, :]
                    m = pool.tensor_tensor(o, v[0:rows, b, at].rearrange("p (h e) -> p h e", e=E),
                                           bias.rearrange("p (h e) -> p h e", e=E), ALU.add)
                m.then_inc(vm_ready.sem, 1)

            def mask_keys(g, s, i):
                nk = (P, NKEY)[s - 1]
                b, c = divmod(i, NCH)
                if i >= 4:
                    pool.wait_ge(wr(("S", s, i - 4)), product_done(g, ("S", s, i - 4)))
                pool.tensor_tensor(KM[:, i % 4, :, 0:nk], spread_rows(kT[:, b * nk:(b + 1) * nk], HC),
                                   headmask[:, c * HC:(c + 1) * HC].unsqueeze(2).broadcast_to([P, HC, nk]),
                                   ALU.mult).then_inc(km_ready.sem, 1)

            def first(g, step):
                if step in ("prep1", "prep2"):
                    s = 1 if step == "prep1" else 2
                    pool.wait_ge(em(f"k{s}T"), product_read(g, f"k{s}T"))
                    mask_keys(g, s, 0)
                    mask_keys(g, s, 1)
                    pool.wait_ge(em(f"v{s}"), product_read(g, f"v{s}"))
                    values(g, s, 0)
                    values(g, s, 1)
                    if s == 1:
                        pool.wait_ge(em("cT"), product_read(g, "cT"))
                        pool.wait_ge(ln_ready.sem, ln_ready.at(g, 0))
                        residual(xb, xin, b1_o, inputs_used)
                    else:
                        pool.wait_ge(ln_ready.sem, ln_ready.at(g, 1))
                        residual(xb, xs, b2_o, xb_ready)
                elif step[0] in ("a1", "a2"):
                    s, i = 1 if step[0] == "a1" else 2, step[1]
                    if i + 2 < NCHUNK:
                        mask_keys(g, s, i + 2)
                    if s == 1 and 1 <= i < NCHUNK + 1:
                        k = i - 1
                        pool.wait_ge(max_ready.sem, max_ready.at(g, k + 1))
                        pool.tensor_tensor(Pq[:, k % 4, :, :], Pq[:, k % 4, :, :],
                                           mx[:, k % 4, :].unsqueeze(2).broadcast_to([P, HC, P]), ALU.subtract)\
                            .then_inc(shifted.sem, 1)
                    if i in (9, 13):
                        b = (i - 1) // 4
                        pool.wait_ge(wr(("PV", s, b - 2)), product_done(g, ("PV", s, b - 2)))
                        values(g, s, b)

            def second(g, step):
                if step == "xT3":
                    pool.wait_ge(ln_ready.sem, ln_ready.at(g, 3))
                    residual(xb2, xs2, b4_o, xb2_ready)
                elif step == "xT4":
                    pool.wait_ge(ln2_ready.sem, ln2_ready.at(g, 1))
                    residual(xb2, xs2, b5_o, xb2_ready)
                elif step[0] == "head" and 1 <= step[1] <= H:
                    h = step[1] - 1
                    for p in range(2):
                        k = 2 * h + p
                        pool.wait_ge(em(("G", h, p)), product_read(g, ("G", h, p)))
                        pool.tensor_tensor(kvs[:, h % HH, 2 * p:2 * p + 2, :, :].rearrange("q b n e -> q (b n) e"),
                                           gwt[:, k % 4, :, :, 0, :].rearrange("q b n e -> q (b n) e"),
                                           gwt[:, k % 4, :, :, 1, :].rearrange("q b n e -> q (b n) e"),
                                           ALU.add).then_inc(kvs_ready.sem, 1)

            run(pool, first, second)

        @block.vector
        def _(dve):
            pre = [0]

            def prep(ins, last=False):
                ins.then_inc(prepared, 1)
                pre[0] += 1
                dve.wait_ge(prepared, pre[0])

            dve.wait_ge(w_loaded, 16 * NLOAD[0])
            prep(dve.reciprocal(qscale1[:, :], temp[:, :]))
            prep(dve.tensor_scalar(qscale1[:, :], qscale1[:, :], float(E) ** -0.5, None, ALU.mult))
            prep(dve.tensor_tensor(qbias1[:, :], b1_qk[:, 0:1], qscale1[:, :], ALU.mult))
            prep(dve.tensor_scalar(b5_q[:, :], b5_q[:, :], 0.5 * float(E) ** -0.5, None, ALU.mult))

            def lengths():
                prep(dve.tensor_reduce(masked[:, :], mask_i, AX, ALU.add))
                prep(dve.tensor_scalar(length[:, :], masked[:, :], -1.0, float(NKEY - 1), ALU.mult, ALU.add))
                prep(dve.tensor_tensor(length2[:, :], length[:, :], length[:, :], ALU.mult))
                assert pre[0] == NPREP, pre

            links = {}
            half_now = ["x"]

            def link(g, ins):
                half = half_now[0]
                ins.then_inc(chain[half].sem, 1)
                links[half] = links.get(half, 0) + 1
                dve.wait_ge(chain[half].sem, chain[half].at(g, links[half]))

            def bc(t, n):
                return t.unsqueeze(len(t.shape)).broadcast_to([*t.shape, n])

            def per_batch(t, n=B):
                return t.unsqueeze(1).broadcast_to([t.shape[0], n, *t.shape[1:]])

            def moments(g, src):
                for b in range(B):
                    m = dve.bn_stats(stats[:, b, :], src[:, b, :])
                link(g, m)
                dve.memset(pause[:, :], 0.0)
                for b in range(B):
                    m = dve.bn_aggr(mv[:, b, :], stats[:, b, :])
                link(g, m)

            def normalize(g, src, dst, ready):
                link(g, dve.tensor_scalar(vare[:, :], mv[:, :, 1], EPS, None, ALU.add))
                dve.tensor_scalar(hvar[:, :], vare[:, :], -0.5, None, ALU.mult)
                link(g, dve.tensor_scalar(rs[:, 0, :].bitcast(I32), vare[:, :].bitcast(I32), -0.5, SEED,
                                          ALU.mult, ALU.add))
                for n in range(NEWTON):
                    link(g, dve.tensor_tensor(nt[:, 0, :], rs[:, n % 2, :], rs[:, n % 2, :], ALU.mult))
                    link(g, dve.tensor_tensor(nt[:, 1, :], nt[:, 0, :], hvar[:, :], ALU.mult))
                    link(g, dve.scalar_tensor_tensor(out=rs[:, (n + 1) % 2, :], in0=nt[:, 1, :], scalar=1.5,
                                                     in1=rs[:, n % 2, :], op0=ALU.add, op1=ALU.mult))
                for b in range(B):
                    m = dve.tensor_scalar(dst[:, b, :], src[:, b, :], mv[:, b, 0:1], rs[:, NEWTON % 2, b:b + 1],
                                          ALU.subtract, ALU.mult)
                m.then_inc(ready.sem, 1)

            def attention(g, s, i):
                nk = (P, NKEY)[s - 1]
                if 1 <= i < NCHUNK + 1:
                    k = i - 1
                    c = k % NCH
                    name = ("S", s, k)
                    dve.wait_ge(wr(name), product_done(g, name))
                    if k >= 4:
                        dve.wait_ge(wr(("PT", s, k - 4)), product_done(g, ("PT", s, k - 4)))
                    src = ap(name)[:, 0:HC * nk].rearrange("p (h k) -> p h k", h=HC)
                    if s == 1:
                        dve.tensor_tensor(Pq[:, k % 4, :, :], src, bias1[:, c * HC:(c + 1) * HC, :], ALU.add)\
                           .then_inc(em(name), 1)
                        dve.wait_ge(em(name), product_read(g, name))
                        dve.tensor_reduce(mx[:, k % 4, :], Pq[:, k % 4, :, :], AX, ALU.max)\
                           .then_inc(max_ready.sem, 1)
                    else:
                        link(g, dve.tensor_reduce(mx[:, k % 4, :], src, AX, ALU.max))
                        dve.tensor_tensor(Pq[:, k % 4, :, 0:nk], src, bc(mx[:, k % 4, :], nk), ALU.subtract)\
                           .then_inc(em(name), 1)
                b = divided_in(i)
                if b is not None:
                    dve.wait_ge(em(("PV", s, b)), product_read(g, ("PV", s, b)))
                    if b >= 2:
                        dve.wait_ge(wr(("y", s, b - 2)), product_done(g, ("y", s, b - 2)))
                    link(g, dve.reciprocal(rden[:, :], pv[:, b % 2, 1, :]))
                    dve.tensor_tensor(oT[:, b % 2, :], pv[:, b % 2, 0, :], rden[:, :], ALU.mult)\
                       .then_inc(o_ready.sem, 1)
                b = output_of(i - 1)
                if b == 0:
                    if s == 1:
                        dve.wait_ge(inputs_used.sem, inputs_used.at(g, 1))
                    else:
                        dve.wait_ge(xb_ready.sem, xb_ready.at(g, 1))
                if b is not None:
                    dve.wait_ge(em(("y", s, b)), product_read(g, ("y", s, b)))
                    dve.tensor_tensor(ys[:, b, :], yo[:, b, :], xb[:, b, :], ALU.add)
                if i == LAST:
                    name = ("y", s, B - 1)
                    dve.wait_ge(wr(name), product_done(g, name))
                    dve.tensor_tensor(ys[:, B - 1, :], ap(name)[:, 0:D], xb[:, B - 1, :], ALU.add)\
                       .then_inc(em(name), 1)
                    dve.wait_ge(em(("y", s, B - 1)), product_read(g, ("y", s, B - 1)))
                    moments(g, ys)
                    normalize(g, ys, xs, ln_ready)

            def gates(g):
                dve.wait_ge(wr("gate"), product_done(g, "gate"))
                dve.tensor_copy(gl[:, 0, :, :], ap("gate").rearrange("p (b k) -> p b k", b=B)[:, :, 0:NE])\
                   .then_inc(em("gate"), 1)
                dve.wait_ge(em("gate"), product_read(g, "gate"))
                rank = per_batch(rank8[:, :])

                def best(src, m, km, dst):
                    link(g, dve.tensor_reduce(gm[:, m, :], gl[:, src, :, :], AX, ALU.max))
                    link(g, dve.tensor_tensor(gl[:, 1, :, :], gl[:, src, :, :], bc(gm[:, m, :], NE), ALU.is_equal))
                    link(g, dve.tensor_tensor(gl[:, 2, :, :], gl[:, 1, :, :], rank, ALU.mult))
                    link(g, dve.tensor_reduce(gm[:, km, :], gl[:, 2, :, :], AX, ALU.max))
                    link(g, dve.tensor_tensor(gl[:, dst, :, :], gl[:, 2, :, :], bc(gm[:, km, :], NE), ALU.is_equal))

                best(0, 0, 1, 3)
                dve.tensor_tensor(gl[:, 7, :, :], gl[:, 0, :, :], bc(gm[:, 0, :], NE), ALU.subtract)\
                   .then_inc(gate_shifted.sem, 1)
                link(g, dve.scalar_tensor_tensor(out=gl[:, 4, :, :], in0=gl[:, 3, :, :], scalar=-1e30,
                                                 in1=gl[:, 0, :, :], op0=ALU.mult, op1=ALU.add))
                best(4, 2, 3, 5)
                link(g, dve.tensor_tensor(gl[:, 6, :, :], gl[:, 3, :, :], gl[:, 5, :, :], ALU.add))

            def gate_shares(g):
                dve.wait_ge(gate_exp.sem, gate_exp.at(g, 1))
                link(g, dve.tensor_tensor(gl[:, 9, :, :], gl[:, 8, :, :], gl[:, 6, :, :], ALU.mult))
                link(g, dve.tensor_reduce(gm[:, 4, :], gl[:, 9, :, :], AX, ALU.add))
                link(g, dve.reciprocal(gm[:, 5, :], gm[:, 4, :]))
                link(g, dve.tensor_tensor(gw[:, :, :], gl[:, 9, :, :], bc(gm[:, 5, :], NE), ALU.mult))

            def table(g, b):
                by_head = lambda t: t.rearrange("p s (h e) -> p s h e", e=E)
                part = lambda n: tab[:, b, n, :, :].rearrange("p h (s e) -> p s h e", e=E)
                dve.wait_ge(wr(("tab", b)), product_done(g, ("tab", b)))
                for t in range(2):
                    m = dve.scalar_tensor_tensor(out=tabf[:, 2 * t:2 * t + 2, :].rearrange("p s d -> p (s d)"),
                                                 in0=b5_tab[:, :], scalar=iskey[:, t:t + 1],
                                                 in1=ap(("tab", b))[0:NKP, t * 2 * D:(t + 1) * 2 * D],
                                                 op0=ALU.mult, op1=ALU.add)
                m.then_inc(em(("tab", b)), 1)
                dve.wait_ge(em(("tab", b)), product_read(g, ("tab", b)))
                link(g, dve.tensor_copy(part(0), by_head(tabf)))
                link(g, dve.tensor_tensor(by_head(tabr), by_head(tabf), part(0), ALU.subtract))
                link(g, dve.tensor_copy(part(1), by_head(tabr)))
                dve.tensor_tensor(part(2), by_head(tabr), part(1), ALU.subtract).then_inc(tab_ready.sem, 1)
                dve.wait_ge(tab_ready.sem, tab_ready.at(g, b + 1))

            def first(g, step):
                half_now[0] = "x"
                if step == "prep1" and g is START:
                    dve.wait_ge(bias_loaded, 16)
                if step == "prep2" and g is START:
                    dve.wait_ge(w2_loaded, 16 * NLOAD[1])
                    lengths()
                if step == "load":
                    links["x"] = 0
                elif step[0] in ("a1", "a2"):
                    attention(g, 1 if step[0] == "a1" else 2, step[1])
                elif step == "gates":
                    gates(g)
                elif step == "gate_shares":
                    gate_shares(g)
                elif step[0] == "tab":
                    table(g, step[1])
                elif step[0] == "m" and step[1] % 2 == 1 and step[1] >= 3:
                    e = step[1] // 2 - 1
                    name = ("expert", e)
                    dve.wait_ge(wr(name), product_done(g, name))
                    if e:
                        dve.wait_ge(em(("expert", e - 1)), product_read(g, ("expert", e - 1)))
                    for b in range(B):
                        m = dve.scalar_tensor_tensor(out=ys[:, b, :], in0=ap(name)[:, b * P:(b + 1) * P],
                                                     scalar=gw[:, b, e:e + 1], in1=(ys if e else xs)[:, b, :],
                                                     op0=ALU.mult, op1=ALU.add)
                    m.then_inc(em(name), 1)
                elif step == "end":
                    dve.wait_ge(em(("expert", NE - 1)), product_read(g, ("expert", NE - 1)))
                    dve.wait_ge(stored.sem, stored.at(g, 0))
                    moments(g, ys)
                    normalize(g, ys, xs2, ln_ready)
                    assert links["x"] == CHAIN[0], links

            def residual(g, name, n):
                dve.wait_ge(wr(name), product_done(g, name))
                dve.wait_ge(xb2_ready.sem, xb2_ready.at(g, n))
                dve.tensor_tensor(ys2[:, :, :], ap(name).rearrange("p (b d) -> p b d", b=B), xb2[:, :, :],
                                  ALU.add).then_inc(em(name), 1)
                dve.wait_ge(em(name), product_read(g, name))

            def linear_kv(g):
                two = lambda t: t.rearrange("p (b k) -> p b k", b=2)
                for p in range(2):
                    at = slice(2 * p * P, (2 * p + 2) * P)
                    dve.wait_ge(em(("kv4", p)), product_read(g, ("kv4", p)))
                    dve.scalar_tensor_tensor(out=k4[:, 2 * p:2 * p + 2, :], in0=two(e4[:, 0, at]), scalar=1.0,
                                             in1=two(t4[:, 1, at]), op0=ALU.min, op1=ALU.add)\
                       .then_inc(k4_ready.sem, 1)
                dve.wait_ge(em("q4T"), product_read(g, "q4T"))
                dve.scalar_tensor_tensor(out=qT2[:, :], in0=e4[:, 1, :], scalar=1.0, in1=t4[:, 0, :],
                                         op0=ALU.min, op1=ALU.add).then_inc(q4_ready.sem, 1)

            def sample_places(g, part):
                ia, ib, ic, idd = ix
                L, L2, LR = [bc(glen[:, k, :], HS) for k in range(3)]

                def tt(o, x, y, op):
                    link(g, dve.tensor_tensor(o, x, y, op))

                def ts(o, x, s1, op1, s2=None, op2=ALU.bypass):
                    link(g, dve.tensor_scalar(o, x, s1, s2, op1, op2))

                MAGIC = 1.5 * 2.0 ** 23
                if part == 0:
                    at = bass.ds((g[0] * B + g[1] * B), B)
                    dve.tensor_copy(glen[:, 0, :], length[:, at])
                    link(g, dve.tensor_copy(glen[:, 1, :], length2[:, at]))
                    link(g, dve.reciprocal(glen[:, 2, :], glen[:, 0, :]))
                    dve.wait_ge(wr("off"), product_done(g, "off"))
                    dve.tensor_tensor(ia, ap("off").rearrange("p (b k) -> p b k", b=B)[:, :, 0:HS],
                                      per_batch(b5_off[:, :]), ALU.add).then_inc(em("off"), 1)
                    dve.wait_ge(em("off"), product_read(g, "off"))
                    tt(ib, ia, per_batch(ramp[:, :]), ALU.add)
                    ts(ic, ib, token[:, 0:1], ALU.add)
                    tt(ia, ic, LR, ALU.mult)
                    ts(ib, ia, MAGIC, ALU.add, MAGIC, ALU.subtract)
                elif part == 1:
                    tt(idd, ib, ia, ALU.is_gt)
                    tt(ib, ib, idd, ALU.subtract)
                    tt(idd, ib, L, ALU.mult)
                    tt(ia, ic, idd, ALU.subtract)
                    tt(ib, ia, L, ALU.mult)
                    link(g, dve.scalar_tensor_tensor(out=ib, in0=ib, scalar=0.0, in1=L, op0=ALU.is_lt, op1=ALU.mult))
                    tt(ia, ia, ib, ALU.add)
                elif part == 2:
                    tt(ib, ia, L, ALU.mult)
                    tt(ib, ib, L2, ALU.is_ge)
                    tt(ib, ib, L, ALU.mult)
                    tt(ia, ia, ib, ALU.subtract)
                    ts(ia, ia, 1.0 / (NKEY - 1), ALU.mult, 2.0, ALU.mult)
                    ts(ia, ia, 1.0, ALU.subtract, 1.0, ALU.add)
                    ts(ia, ia, float(NKEY), ALU.mult, 1.0, ALU.subtract)
                    ts(ic, ia, 0.5, ALU.mult)
                else:
                    ts(ia, ic, MAGIC, ALU.add, MAGIC, ALU.subtract)
                    tt(ib, ia, ic, ALU.is_gt)
                    tt(idd, ia, ib, ALU.subtract)
                    tt(w01[:, :, :, 1], ic, idd, ALU.subtract)
                    ts(w01[:, :, :, 0], w01[:, :, :, 1], -1.0, ALU.mult, 1.0, ALU.add)
                    ts(ia, idd, -2.0, ALU.max, float(NKEY + 1), ALU.min)
                    halves = ia.rearrange("p b (s j) -> p b s j", s=2)
                    ts(uu[:, :, :, 0:HHS], halves, float(NCTR), ALU.subtract)
                    dve.tensor_tensor(uu[:, :, :, HHS:2 * HHS], uu[:, :, :, 0:HHS], uu[:, :, :, 0:HHS], ALU.mult)\
                       .then_inc(uu_ready.sem, 1)

            def weight(g, h, p):
                k = 2 * h + p
                name = ("G", h, p)
                dve.wait_ge(wr(name), product_done(g, name))
                if k >= 4:
                    dve.wait_ge(kvs_ready.sem, kvs_ready.at(g, k - 3))
                src = ap(name).rearrange("q (t r) -> q t r", t=2)[:, :, 0:NS * 4 * E]\
                    .rearrange("q t (m e) -> q t m e", e=2 * E)
                w = w01[:, 2 * p:2 * p + 2, h * NS:(h + 1) * NS, :].rearrange("q t n s -> q t (n s)")
                dve.tensor_tensor(gwt[:, k % 4, :, :, :, :].rearrange("q t n s e -> q t (n s) e"), src,
                                  bc(w, 2 * E), ALU.mult).then_inc(em(name), 1)

            def quarter(q):
                return kvs[:, (q % 2) * HQ:(q % 2 + 1) * HQ, :, :, :].rearrange("p h b n e -> p (h b) n e")

            def score(g, q):
                dve.wait_ge(kvs_ready.sem, kvs_ready.at(g, (q + 1) * 2 * HQ))
                qs = q5[:, q * HQ:(q + 1) * HQ, :, :].rearrange("p h b e -> p (h b) e")
                link(g, dve.tensor_tensor(prod5, quarter(q)[:, :, :, 0:E],
                                          qs.unsqueeze(2).broadcast_to([P, HQ * B, NS, E]), ALU.mult))
                link(g, dve.tensor_reduce(sc5[:, 0, :, :], prod5, AX, ALU.add))
                link(g, dve.tensor_reduce(sm5[:, 0, :], sc5[:, 0, :, :], AX, ALU.max))
                dve.tensor_tensor(sc5[:, 1, :, :], sc5[:, 0, :, :], bc(sm5[:, 0, :], NS), ALU.subtract)\
                   .then_inc(s5_shifted.sem, 1)

            def mix(g, q):
                dve.wait_ge(s5_exp.sem, s5_exp.at(g, q + 1))
                link(g, dve.tensor_reduce(sm5[:, 1, :], sc5[:, 2, :, :], AX, ALU.add))
                link(g, dve.reciprocal(sm5[:, 2, :], sm5[:, 1, :]))
                link(g, dve.scalar_tensor_tensor(out=sc5[:, 0, :, :], in0=sc5[:, 2, :, :], scalar=0.5,
                                                 in1=bc(sm5[:, 2, :], NS), op0=ALU.mult, op1=ALU.mult))
                link(g, dve.tensor_tensor(prod5, quarter(q)[:, :, :, E:2 * E], bc(sc5[:, 0, :, :], E), ALU.mult))
                by_seq = prod5.rearrange("p (h b) n e -> p b h e n", b=B)
                for b in range(B):
                    m = dve.tensor_reduce(o5[:, b, q * HQ * E:(q + 1) * HQ * E]
                                          .rearrange("p (h e) -> p h e", e=E), by_seq[:, b], AX, ALU.add)
                m.then_inc(o5_ready.sem, 1)
                dve.wait_ge(o5_ready.sem, o5_ready.at(g, q + 1))

            def spikes(g, k):
                y, n, t, s = [lif[:, k, :] for k in range(4)]
                if k == 0:
                    dve.wait_ge(wr("y6"), product_done(g, "y6"))
                    dve.tensor_copy(y, ap("y6")).then_inc(em("y6"), 1)
                    dve.wait_ge(em("y6"), product_read(g, "y6"))
                    dve.tensor_scalar(n, y, -1.0, None, ALU.mult)
                    link(g, dve.tensor_scalar(s, y, 1.0, None, ALU.is_gt))
                else:
                    link(g, dve.scalar_tensor_tensor(out=t, in0=n, scalar=-0.9, in1=y, op0=ALU.mult, op1=ALU.add))
                    link(g, dve.scalar_tensor_tensor(out=n, in0=n, scalar=-1.0, in1=t, op0=ALU.is_lt,
                                                     op1=ALU.subtract))
                    link(g, dve.scalar_tensor_tensor(out=s, in0=n, scalar=-1.0, in1=s, op0=ALU.is_lt, op1=ALU.add))
                if k == 4:
                    link(g, dve.scalar_tensor_tensor(out=ys2[:, :, :], in0=s.rearrange("p (b d) -> p b d", b=B),
                                                     scalar=0.2, in1=xs2[:, :, :], op0=ALU.mult, op1=ALU.add))

            def second(g, step):
                half_now[0] = "y"
                if step == "xT3":
                    links["y"] = 0
                elif step == "elu":
                    linear_kv(g)
                elif step == "kvmask":
                    for p in range(2):
                        dve.wait_ge(wr(("kvsum", p)), product_done(g, ("kvsum", p)))
                        dve.tensor_tensor(kv4[:, 2 * p:2 * p + 2, :],
                                          ap(("kvsum", p)).rearrange("p (b d) -> p b d", b=2),
                                          per_batch(block4, 2), ALU.mult)\
                           .then_inc(em(("kvsum", p)), 1)
                elif step[0] == "ratio":
                    p = step[1]
                    src = ap(("nd", p))
                    dve.wait_ge(wr(("nd", p)), product_done(g, ("nd", p)))
                    if p == 0:
                        dve.wait_ge(q4_ready.sem, q4_ready.at(g, 1))
                    link(g, dve.tensor_scalar(dn4[:, p, 0, :], src[:, 2 * P:4 * P], 1e-8, None, ALU.add))
                    link(g, dve.reciprocal(dn4[:, p, 1, :], dn4[:, p, 0, :]))
                    dve.tensor_tensor(t4[:, 0, 2 * p * P:(2 * p + 2) * P], src[:, 0:2 * P], dn4[:, p, 1, :],
                                      ALU.mult).then_inc(em(("nd", p)), 1)
                elif step == "norm4":
                    residual(g, "y4", 1)
                    moments(g, ys2)
                elif step in ("norm4b", "norm5b"):
                    normalize(g, ys2, xs2, ln2_ready)
                elif step == "scale5":
                    dve.wait_ge(wr("q5"), product_done(g, "q5"))
                    heads = lambda t: t.rearrange("p (h e) -> p h e", e=E)
                    for b in range(B):
                        m = dve.scalar_tensor_tensor(out=q5[:, :, b, :], in0=heads(ap("q5")[:, b * D:(b + 1) * D]),
                                                     scalar=0.5 * float(E) ** -0.5, in1=heads(b5_q[:, :]),
                                                     op0=ALU.mult, op1=ALU.add)
                    m.then_inc(em("q5"), 1)
                elif step[0] == "place":
                    sample_places(g, step[1])
                elif step[0] == "head":
                    h = step[1]
                    if 1 <= h <= H:
                        weight(g, h - 1, 0)
                    if h in VECTOR_ROW:
                        j = h * NS + VN
                        dve.wait_ge(wr(("hit", j)), product_done(g, ("hit", j)))
                        dve.tensor_scalar(hit[:, j % NHIT, :], ap(("hit", j))[0:NKP, :], hitbias[:, 0:1], 0.0,
                                          ALU.add, ALU.max).then_inc(em(("hit", j)), 1)
                    if 1 <= h <= H:
                        weight(g, h - 1, 1)
                elif step[0] == "score":
                    score(g, step[1])
                elif step[0] == "mix":
                    mix(g, step[1])
                elif step == "norm5":
                    residual(g, "y5", 2)
                    moments(g, ys2)
                elif step == "square":
                    for c in range(NF):
                        dve.wait_ge(em(("h6", c)), product_read(g, ("h6", c)))
                        dve.tensor_tensor(h6[:, c, :], h6[:, c, :], h6[:, c, :], ALU.mult).then_inc(h6_ready.sem, 1)
                elif step[0] == "spikes":
                    spikes(g, step[1])
                elif step == "out":
                    moments(g, ys2)
                    normalize(g, ys2, xs2, ln2_ready)
                    assert links["y"] == CHAIN[1], links

            run(dve, first, second)


def constants():
    q = np.arange(P, dtype=np.float32)
    start = 2.0 ** (-2.0 ** (-(np.log2(H) - 3)))
    slopes = np.asarray([start * start ** i for i in range(H)], np.float32)
    rel = q[None, :] - q[:, None]
    bias = np.where(rel[:, None, :] <= 0, slopes[None, :, None] * rel[:, None, :], np.float32(-1e30))
    key = np.arange(NKP) - 1 - NCTR
    pick = np.zeros((NKP, HHS, NKP), np.float16)
    for j in range(HHS):
        pick[j, j, :] = 2 * key
        pick[HHS + j, j, :] = -1
    head = np.arange(D) // E
    block = (head[:, None] == head[None, :]).astype(np.float32)
    return {
        "ident": np.eye(P, dtype=np.float32),
        "bias1": bias.astype(np.float32),
        "ramp": np.tile(np.arange(-NS // 2, NS - NS // 2 - 1, dtype=np.float32), (P, H)),
        "token": q[:, None].copy(),
        "pick": pick,
        "hitbias": (1.0 - key.astype(np.float32) ** 2)[:, None].copy(),
        "iskey": np.stack([(key >= -NCTR) & (key < NKEY - NCTR), np.arange(NKP) < NKEY], 1).astype(np.float32),
        "rank8": np.tile(np.arange(NE, 0, -1, dtype=np.float32), (P, 1)),
        "headmask": (head[:, None] == np.arange(H)[None, :]).astype(np.float32),
        "block4": np.concatenate([block, block], 1),
    }


AS_GIVEN = ["x", "ctx_1024", "mask_BxS2_if0", "L0_ffn_gate_w", "L0_ffn_fc_w", "L0_ffn_proj_w"]


def layout(inputs):
    given = {name: np.asarray(value) for name, value in inputs.items()}
    arrays = {name: np.ascontiguousarray(given[name]) for name in AS_GIVEN}
    const = constants()
    row = lambda name: given[name].reshape(1, -1)
    parts = {
        "ident": const["ident"], "w1_qkv": given["L0_attn_W_attn"], "w1_o": given["L0_attn_W_proj"],
        "b1_qk": given["L0_attn_b_attn"][0:2 * D].reshape(2, D).T, "headmask": const["headmask"],
        "temp": row("L0_attn_temperature"), "b1_v": row("L0_attn_b_attn")[:, 2 * D:3 * D],
        "b1_o": row("L0_attn_b_proj"), "b2_o": row("L0_xattn_bo"), "b4_o": row("L1_attn_b_proj"),
        "b5_q": row("L1_xattn_bq"), "b5_off": row("L1_xattn_boff"), "b5_o": row("L1_xattn_bo"),
        "b5_tab": np.concatenate([row("L1_xattn_bk"), row("L1_xattn_bv")], 1),
        "w2_q": given["L0_xattn_Wq"], "w2_k": given["L0_xattn_Wk"], "w2_v": given["L0_xattn_Wv"],
        "w2_o": given["L0_xattn_Wo"], "w4_q": given["L1_attn_w_qkv"].T[:, 0:D],
        "w4_kv": given["L1_attn_w_qkv"].T[:, D:3 * D], "w4_o": given["L1_attn_w_proj"].T,
        "w5_kv": np.concatenate([given["L1_xattn_Wk"].T, given["L1_xattn_Wv"].T], 1),
        "w5_q": given["L1_xattn_Wq"].T, "w5_o": given["L1_xattn_Wo"].T, "w6_fc": given["L1_ffn_W_fc"].T,
        "w6_proj": given["L1_ffn_W_proj"].T.reshape(NF, P, D).transpose(1, 0, 2).reshape(P, NF * D),
        "b5_qcol": given["L1_xattn_bq"].reshape(D, 1), "ramp": const["ramp"], "token": const["token"],
        "rank8": const["rank8"], "block4": const["block4"], "hitbias": const["hitbias"], "iskey": const["iskey"],
    }
    for pack, names in PACKS.items():
        assert all(parts[name].shape[1] == n for name, n in names)
        arrays[pack] = np.ascontiguousarray(np.concatenate([parts[name] for name, _ in names], 1))
    arrays["w5_offT"] = np.ascontiguousarray(given["L1_xattn_Woff"].T)
    arrays["c_bias1"], arrays["c_pick"] = const["bias1"], const["pick"]
    return arrays


def kernel(**inputs):
    import concourse.bacc as bacc
    from concourse.bass_utils import run_bass_kernel_spmd

    nc = bacc.Bacc("TRN2", target_bir_lowering=False, num_devices=1)
    arrays, a = {}, {}
    for name, value in layout(inputs).items():
        arrays[f"in_{name}_dram"] = value
        a[name] = nc.dram_tensor(f"in_{name}_dram", value.shape, mybir.dt.from_np(value.dtype),
                                 kind="ExternalInput").ap()
    shape = inputs["x"].shape
    out = nc.dram_tensor("out_dram", shape, F32, kind="ExternalOutput").ap()
    decoder(nc, a, out)
    r = run_bass_kernel_spmd(nc, [arrays], core_ids=[0])
    return r.results[0]["out_dram"]
```
